# Optimizing a Trainium2 kernel written in Bass

```python
import numpy as np
import jax
import jax.numpy as jnp

def _softmax(x, axis=-1):
    return jax.nn.softmax(x, axis=axis)

def _gelu(x):
    return jax.nn.gelu(x, approximate=True)

def _silu(x):
    return jax.nn.silu(x)

def _sigmoid(x):
    return jax.nn.sigmoid(x)

def _layernorm(x, axis=-1, eps=1e-05):
    m = jnp.mean(x, axis=axis, keepdims=True)
    v = jnp.var(x, axis=axis, keepdims=True)
    return (x - m) / jnp.sqrt(v + eps)

def _scatter_add(tgt, idx, src, axis=0):
    return tgt.at[idx].add(src)

def _segment_sum(src, seg, n):
    return jax.ops.segment_sum(src, seg, n)
kernel_name = 'mk_prb_d2_jaxref_r8_4d9aff'

def setup_inputs(seed: int=0):
    np.random.seed(seed)
    _w = jnp.asarray

    def _L0_attn_setup():
        import jax, jax.numpy as jnp
        import numpy as np
        B, S, DIM = (2, 256, 256)
        H = 16
        NOPE, ROPE, VD = (128, 64, 128)
        QKD = NOPE + ROPE
        Q_LORA, KV_LORA = (96, 64)
        EPS = 1e-06
        THETA = 10000.0

        def rmsnorm(x, g):
            var = jnp.mean(x * x, axis=-1, keepdims=True)
            return x * jax.lax.rsqrt(var + EPS) * g

        def rope_cos_sin(seq_len, d, dtype=jnp.float32):
            inv_freq = 1.0 / THETA ** (jnp.arange(0, d, 2, dtype=jnp.float32) / d)
            t = jnp.arange(seq_len, dtype=jnp.float32)
            freqs = jnp.outer(t, inv_freq)
            return (jnp.cos(freqs).astype(dtype), jnp.sin(freqs).astype(dtype))

        def apply_rope(x, cos, sin):
            d2 = x.shape[-1] // 2
            x1, x2 = (x[..., :d2], x[..., d2:])
            c = cos[None, :, None, :]
            s = sin[None, :, None, :]
            return jnp.concatenate([x1 * c - x2 * s, x1 * s + x2 * c], axis=-1)
        key = jax.random.key(seed)
        ks = jax.random.split(key, 10)

        def w(k, fan_in, fan_out):
            return jax.random.normal(k, (fan_in, fan_out), jnp.float32) / np.sqrt(fan_in)
        return {'x': jax.random.normal(ks[0], (B, S, DIM), jnp.float32), 'w_dq': w(ks[1], DIM, Q_LORA), 'g_q': jnp.ones((Q_LORA,), jnp.float32), 'w_uq': w(ks[2], Q_LORA, H * QKD), 'w_dkv': w(ks[3], DIM, KV_LORA), 'w_kr': w(ks[4], DIM, ROPE), 'g_kv': jnp.ones((KV_LORA,), jnp.float32), 'w_uk': w(ks[5], KV_LORA, H * NOPE), 'w_uv': w(ks[6], KV_LORA, H * VD), 'w_o': w(ks[7], H * VD, DIM)}
    _L0_attn_in = _L0_attn_setup()

    def _L0_ffn_setup():
        import jax, jax.numpy as jnp
        import numpy as np
        key = jax.random.key(seed)
        k1, k2, k3, k4, k5 = jax.random.split(key, 5)
        B, L, H, N = (2, 256, 256, 1024)
        x = jax.random.normal(k1, (B, L, H), dtype=jnp.float32)
        W0 = jax.random.normal(k2, (N, H), dtype=jnp.float32) * (1.0 / np.sqrt(H))
        bias0 = jax.random.normal(k3, (N,), dtype=jnp.float32) * 0.02
        W1 = jax.random.normal(k4, (H, N), dtype=jnp.float32) * (1.0 / np.sqrt(N))
        bias1 = jax.random.normal(k5, (H,), dtype=jnp.float32) * 0.02
        return {'x': x, 'W0': W0, 'bias0': bias0, 'W1': W1, 'bias1': bias1}
    _L0_ffn_in = _L0_ffn_setup()

    def _L1_attn_setup():
        import jax, jax.numpy as jnp
        import numpy as np
        NUM_HEADS = 16

        def _l2_normalize_complex(z):
            n = jnp.sqrt(jnp.sum(jnp.abs(z) ** 2, axis=-1, keepdims=True))
            return z / n
        key = jax.random.key(seed)
        k1, k2, k3, k4 = jax.random.split(key, 4)
        B, S, D = (4, 512, 256)
        scale = 1.0 / np.sqrt(D)
        return {'x': jax.random.normal(k1, (B, S, D), dtype=jnp.float32), 'W_q': jax.random.normal(k2, (D, D), dtype=jnp.float32) * scale, 'W_kv': jax.random.normal(k3, (D, D), dtype=jnp.float32) * scale, 'W_o': jax.random.normal(k4, (D, D), dtype=jnp.float32) * scale}
    _L1_attn_in = _L1_attn_setup()

    def _L1_ffn_setup():
        import jax, jax.numpy as jnp
        import numpy as np
        B, S, H, I = (1, 64, 256, 768)

        def _quantized_matmul(x, w, scale):
            wq = w.astype(jnp.float8_e4m3fn).astype(x.dtype)
            y = jnp.einsum('bsi,io->bso', x, wq)
            return y * scale
        key = jax.random.key(seed)
        ks = jax.random.split(key, 7)
        return {'x': jax.random.normal(ks[0], (B, S, H), dtype=jnp.float32), 'gate_w': jax.random.normal(ks[1], (H, I), dtype=jnp.float32) * 0.02, 'up_w': jax.random.normal(ks[2], (H, I), dtype=jnp.float32) * 0.02, 'down_w': jax.random.normal(ks[3], (I, H), dtype=jnp.float32) * 0.02, 'gate_scale': jax.random.uniform(ks[4], (I,), dtype=jnp.float32, minval=0.5, maxval=1.5), 'up_scale': jax.random.uniform(ks[5], (I,), dtype=jnp.float32, minval=0.5, maxval=1.5), 'down_scale': jax.random.uniform(ks[6], (H,), dtype=jnp.float32, minval=0.5, maxval=1.5)}
    _L1_ffn_in = _L1_ffn_setup()
    _d = {'L0_attn_x': _L0_attn_in['x'], 'L0_attn_w_dq': _L0_attn_in['w_dq'], 'L0_attn_g_q': _L0_attn_in['g_q'], 'L0_attn_w_uq': _L0_attn_in['w_uq'], 'L0_attn_w_dkv': _L0_attn_in['w_dkv'], 'L0_attn_w_kr': _L0_attn_in['w_kr'], 'L0_attn_g_kv': _L0_attn_in['g_kv'], 'L0_attn_w_uk': _L0_attn_in['w_uk'], 'L0_attn_w_uv': _L0_attn_in['w_uv'], 'L0_attn_w_o': _L0_attn_in['w_o'], 'L0_ffn_W0': _L0_ffn_in['W0'], 'L0_ffn_bias0': _L0_ffn_in['bias0'], 'L0_ffn_W1': _L0_ffn_in['W1'], 'L0_ffn_bias1': _L0_ffn_in['bias1'], 'L1_attn_W_q': _L1_attn_in['W_q'], 'L1_attn_W_kv': _L1_attn_in['W_kv'], 'L1_attn_W_o': _L1_attn_in['W_o'], 'L1_ffn_gate_w': _L1_ffn_in['gate_w'], 'L1_ffn_up_w': _L1_ffn_in['up_w'], 'L1_ffn_down_w': _L1_ffn_in['down_w'], 'L1_ffn_gate_scale': _L1_ffn_in['gate_scale'], 'L1_ffn_up_scale': _L1_ffn_in['up_scale'], 'L1_ffn_down_scale': _L1_ffn_in['down_scale']}
    _x0 = _d['L0_attn_x']
    _d['L0_attn_x'] = jax.random.normal(jax.random.fold_in(jax.random.key(seed), 1), (4, 1024, 256), dtype=_x0.dtype)
    del _x0
    return _d

def reference(L0_attn_x, L0_attn_w_dq, L0_attn_g_q, L0_attn_w_uq, L0_attn_w_dkv, L0_attn_w_kr, L0_attn_g_kv, L0_attn_w_uk, L0_attn_w_uv, L0_attn_w_o, L0_ffn_W0, L0_ffn_bias0, L0_ffn_W1, L0_ffn_bias1, L1_attn_W_q, L1_attn_W_kv, L1_attn_W_o, L1_ffn_gate_w, L1_ffn_up_w, L1_ffn_down_w, L1_ffn_gate_scale, L1_ffn_up_scale, L1_ffn_down_scale):

    def _L0_attn_ref(x, w_dq, g_q, w_uq, w_dkv, w_kr, g_kv, w_uk, w_uv, w_o):
        import jax, jax.numpy as jnp
        import numpy as np
        B, S, DIM = (2, 256, 256)
        H = 16
        NOPE, ROPE, VD = (128, 64, 128)
        QKD = NOPE + ROPE
        Q_LORA, KV_LORA = (96, 64)
        EPS = 1e-06
        THETA = 10000.0

        def rmsnorm(x, g):
            var = jnp.mean(x * x, axis=-1, keepdims=True)
            return x * jax.lax.rsqrt(var + EPS) * g

        def rope_cos_sin(seq_len, d, dtype=jnp.float32):
            inv_freq = 1.0 / THETA ** (jnp.arange(0, d, 2, dtype=jnp.float32) / d)
            t = jnp.arange(seq_len, dtype=jnp.float32)
            freqs = jnp.outer(t, inv_freq)
            return (jnp.cos(freqs).astype(dtype), jnp.sin(freqs).astype(dtype))

        def apply_rope(x, cos, sin):
            d2 = x.shape[-1] // 2
            x1, x2 = (x[..., :d2], x[..., d2:])
            c = cos[None, :, None, :]
            s = sin[None, :, None, :]
            return jnp.concatenate([x1 * c - x2 * s, x1 * s + x2 * c], axis=-1)
        b, s, _ = x.shape
        scale = QKD ** (-0.5)
        q = rmsnorm(x @ w_dq, g_q) @ w_uq
        q = q.reshape(b, s, H, QKD)
        q_nope, q_pe = (q[..., :NOPE], q[..., NOPE:])
        kv = rmsnorm(x @ w_dkv, g_kv)
        k_nope = (kv @ w_uk).reshape(b, s, H, NOPE)
        v = (kv @ w_uv).reshape(b, s, H, VD)
        k_pe = (x @ w_kr)[:, :, None, :]
        cos, sin = rope_cos_sin(s, ROPE, x.dtype)
        q_pe = apply_rope(q_pe, cos, sin)
        k_pe = apply_rope(k_pe, cos, sin)
        scores = (jnp.einsum('bqhd,bkhd->bhqk', q_nope, k_nope) + jnp.einsum('bqhd,bkd->bhqk', q_pe, k_pe[:, :, 0, :])) * scale
        causal = jnp.tril(jnp.ones((s, s), bool))
        scores = jnp.where(causal[None, None], scores, jnp.finfo(scores.dtype).min)
        attn = jax.nn.softmax(scores, axis=-1)
        out = jnp.einsum('bhqk,bkhd->bqhd', attn, v).reshape(b, s, H * VD)
        return out @ w_o

    def _L0_ffn_ref(x, W0, bias0, W1, bias1):
        import jax, jax.numpy as jnp
        import numpy as np
        B, L, H = x.shape
        X = x.reshape(-1, H).astype(jnp.float16)
        D = jnp.dot(X.astype(jnp.float32), W0.T) + bias0
        D = jax.nn.gelu(D, approximate=False).astype(jnp.float16)
        E = jnp.dot(D.astype(jnp.float32), W1.T) + bias1
        return E.astype(jnp.float16).reshape(B, L, H)

    def _L1_attn_ref(x, W_q, W_kv, W_o):
        import jax, jax.numpy as jnp
        import numpy as np
        NUM_HEADS = 16

        def _l2_normalize_complex(z):
            n = jnp.sqrt(jnp.sum(jnp.abs(z) ** 2, axis=-1, keepdims=True))
            return z / n
        B, S, D = x.shape
        H = NUM_HEADS
        hd = D // H
        q = (x @ W_q.T).reshape(B, S, H, hd)
        kv = (x @ W_kv.T).reshape(B, S, H, hd)
        qf = jnp.fft.fft(q, axis=-1)
        kvf = jnp.fft.fft(kv, axis=-1)
        qf = _l2_normalize_complex(qf)
        kvf = _l2_normalize_complex(kvf)
        kvf = jnp.cumsum(kvf, axis=1)
        qv = qf * kvf
        values_hat = jnp.fft.ifft(qv, axis=-1).real.astype(x.dtype)
        values_hat = values_hat.reshape(B, S, D)
        return values_hat @ W_o.T

    def _L1_ffn_ref(x, gate_w, up_w, down_w, gate_scale, up_scale, down_scale):
        import jax, jax.numpy as jnp
        import numpy as np
        B, S, H, I = (1, 64, 256, 768)

        def _quantized_matmul(x, w, scale):
            wq = w.astype(jnp.float8_e4m3fn).astype(x.dtype)
            y = jnp.einsum('bsi,io->bso', x, wq)
            return y * scale
        gate = jax.nn.silu(_quantized_matmul(x, gate_w, gate_scale))
        up = _quantized_matmul(x, up_w, up_scale)
        fuse = gate * up
        return _quantized_matmul(fuse, down_w, down_scale)
    x = L0_attn_x
    xn = _layernorm(x, axis=-1)
    x = x + _L0_attn_ref(xn, L0_attn_w_dq, L0_attn_g_q, L0_attn_w_uq, L0_attn_w_dkv, L0_attn_w_kr, L0_attn_g_kv, L0_attn_w_uk, L0_attn_w_uv, L0_attn_w_o) + _L0_ffn_ref(xn, L0_ffn_W0, L0_ffn_bias0, L0_ffn_W1, L0_ffn_bias1)
    xn = _layernorm(x, axis=-1)
    x = x + _L1_attn_ref(xn, L1_attn_W_q, L1_attn_W_kv, L1_attn_W_o) + _L1_ffn_ref(xn, L1_ffn_gate_w, L1_ffn_up_w, L1_ffn_down_w, L1_ffn_gate_scale, L1_ffn_up_scale, L1_ffn_down_scale)
    return x

_drawn_inputs = setup_inputs


def setup_inputs(seed=0):
    import zlib

    import numpy as np

    out = dict(_drawn_inputs(seed))
    spreads = {'L0_attn_g_q': (1.0, 0.6), 'L0_attn_g_kv': (1.0, 0.2)}
    factors = {'L1_ffn_gate_w': 4.235,
     'L1_ffn_up_w': 4.183,
     'L1_ffn_down_w': 4.225,
     'L1_ffn_gate_scale': 8.0,
     'L1_ffn_up_scale': 8.0,
     'L1_ffn_down_scale': 8.0,
     'L0_ffn_bias0': 3.675,
     'L1_attn_W_q': 44.777,
     'L1_attn_W_kv': 45.156,
     'L1_attn_W_o': 45.022}
    for name, (base, spread) in spreads.items():
        noise = np.random.default_rng([zlib.crc32(name.encode()), seed]).standard_normal(out[name].shape)
        drawn = base * np.exp(spread * noise) if base else spread * noise
        out[name] = jnp.asarray(drawn.astype(out[name].dtype))
    for name, factor in factors.items():
        out[name] = (out[name] * factor).astype(out[name].dtype)
    return out
```

```python
from contextlib import ExitStack

import concourse.bass as bass
from concourse import mybir

F32 = mybir.dt.float32
F16 = mybir.dt.float16
BF16 = mybir.dt.bfloat16
U32 = mybir.dt.uint32
ALU = mybir.AluOpType
ACT = mybir.ActivationFunctionType
AX_X = mybir.AxisListType.X

P = 128
HALF = 512
WUP = 64.0
WO1UP = 16.0
FDOWN = 1.0 / 64
LN_EPS = 1e-5
RMS_EPS = 1e-6


def two_layer_kernel(nc, a, out):
    B, S, D = a["x"].shape
    T = S // P
    QL, KL, ROPE = 96, 64, 64
    LAT = QL + KL + ROPE
    NP = a["w_pe"].shape[1]
    H = 2 * NP
    F0 = a["W0T"].shape[1]
    NF0 = F0 // P
    F1 = a["gate_w"].shape[1]
    NF1 = F1 // P
    DC = D // P
    STEPS = 2 * T
    TASKS = 3 * T
    LAST = NP // 2 - 1

    with ExitStack() as ctx:
        def sb(name, shape, dt):
            return ctx.enter_context(nc.sbuf_tensor(name, shape, dt))

        def sem(name):
            return ctx.enter_context(nc.semaphore(name))

        ps = ctx.enter_context(nc.psum_tensor("ps", [P, 8, HALF], F32))

        ident = sb("ident", [P, P], F32)
        identb = sb("identb", [P, P], BF16)
        maskb = sb("maskb", [P, P], BF16)
        tri = sb("tri", [P, P], F32)
        ones = sb("ones", [P, P], F32)
        ct_e = sb("ct_e", [P, S], F32)
        ct_o = sb("ct_o", [P, S], F32)
        st = sb("st", [P, S], F32)
        cos_t = sb("cos_t", [P, T, 32], F32)
        sin_t = sb("sin_t", [P, T, 32], F32)
        gq = sb("gq", [QL, 1], F32)
        ge = sb("ge", [P, 1], F32)
        go = sb("go", [P, 1], F32)
        gkv = sb("gkv", [P, 1], F32)
        bias0 = sb("bias0", [P, NF0], F32)
        bias1 = sb("bias1", [P, D], F32)
        gate_s = sb("gate_s", [P, NF1], F32)
        up_s = sb("up_s", [P, NF1], F32)
        down_s = sb("down_s", [P, D], F32)
        eps = sb("eps", [P, 3], F32)
        wlat_h, wlat_l = (sb(f"wlat_{x}", [P, DC, LAT], F16) for x in "hl")
        wq_h, wq_l = (sb(f"wq_{x}", [QL, NP, 3, P], F16) for x in "hl")
        wb_h, wb_l = (sb(f"wb_{x}", [P, NP, D], F16) for x in "hl")
        w0_h, w0_l = (sb(f"w0_{x}", [P, DC, F0], F16) for x in "hl")
        w1_h, w1_l = (sb(f"w1_{x}", [P, NF0, D], F16) for x in "hl")
        wsp_h, wsp_l = (sb(f"wsp_{x}", [P, DC, 2 * D], F16) for x in "hl")
        wo1_h, wo1_l = (sb(f"wo1_{x}", [P, DC, D], F16) for x in "hl")
        gate_w = sb("gate_w", [P, DC, F1], F16)
        up_w = sb("up_w", [P, DC, F1], F16)
        down_w = sb("down_w", [P, NF1, D], F16)

        xb = sb("xb", [P, T, D], F32)
        xT_h, xT_l = (sb(f"xT_{x}", [P, DC, S], F16) for x in "hl")
        qT_h, qT_l = (sb(f"qT_{x}", [QL, S], F16) for x in "hl")
        kTe_h, kTe_l, kTo_h, kTo_l = (sb(f"kT{x}", [P, S], F16) for x in ("eh", "el", "oh", "ol"))
        kT_h, kT_l = [kTe_h, kTo_h], [kTe_l, kTo_l]
        v_h, v_l = (sb(f"v_{x}", [P, T, KL], F16) for x in "hl")
        negmax = sb("negmax", [P, STEPS], F32)
        rowsum = sb("rowsum", [P, STEPS], F32)
        rinv = sb("rinv", [P, 2, 4], F32)
        bnst = sb("bnst", [P, T, 6], F32)
        mv = sb("mv", [P, T, 2], F32)
        sd = sb("sd", [P, T], F32)
        rstd = sb("rstd", [P, T], F32)
        tick = sb("tick", [P, 1], F32)
        ss = sb("ss", [P, 2, T], F32)
        rs = sb("rs", [P, 2, T], F32)
        rr = sb("rr", [P, 2, T], F32)
        ss2 = sb("ss2", [P, T, 32], F32)
        rs2 = sb("rs2", [P, T, 32], F32)
        rr2 = sb("rr2", [P, T, 32], F32)
        e16 = sb("e16", [P, 2, D], F16)
        outb = sb("outb", [P, 2, D], F32)

        reg_o = sb("reg_o", [P, 8192], F32)
        reg_p = sb("reg_p", [P, 4096], F32)
        reg_q = sb("reg_q", [P, 4096], F32)
        reg_a = sb("reg_a", [P, 4096], F32)
        reg_x = sb("reg_x", [P, 2048], F32)
        reg_t = sb("reg_t", [P, 2048], F32)
        s_wo = reg_o[:, 0:4096].rearrange("p (h n) -> p h n", h=H)
        s_w0 = reg_o[:, 4096:6144].rearrange("p (k n) -> p k n", k=DC)
        s_w1 = reg_o[:, 6144:8192].rearrange("p (k n) -> p k n", k=NF0)
        s_uqT = reg_p[:, 0:1536].rearrange("p (h n) -> p h n", h=H)
        s_ukT = reg_p[:, 1536:2560].rearrange("p (h n) -> p h n", h=H)
        s_uvT = reg_p[:, 2560:3584].rearrange("p (h n) -> p h n", h=H)
        s_lat = reg_p[:, 3584:3584 + 448].rearrange("p (k n) -> p k n", k=DC)
        s_wq = reg_q[0:QL, 0:3072].rearrange("p (r j n) -> p r j n", r=NP, j=3)
        s_q1 = reg_q[:, 3072:3584].rearrange("p (k n) -> p k n", k=DC)
        s_kv1 = reg_q[:, 3584:4096].rearrange("p (k n) -> p k n", k=DC)
        s_gate = reg_a[:, 0:1536]
        s_up = reg_a[:, 1536:3072]
        s_ft = reg_a[:, 3072:3584].rearrange("p (k n) -> p k n", k=DC)
        s_gt = reg_a[:, 3584:4096].rearrange("p (k n) -> p k n", k=DC)
        s_down = reg_x[:, 0:1536]
        s_o1 = reg_x[:, 1536:2048].rearrange("p (k n) -> p k n", k=DC)
        s_m = reg_t[:, 0:1536]
        xn = reg_x[:, :].rearrange("p (t n) -> p t n", t=T)
        run = xn
        lat = reg_a[:, 0:T * LAT].rearrange("p (t n) -> p t n", t=T)
        kcat = reg_a[:, 1792:1792 + T * 192].rearrange("p (t n) -> p t n", t=T)
        qn = reg_a[:, 3328:3328 + T * QL].rearrange("p (t n) -> p t n", t=T)
        ropet = reg_t[:, 0:4 * T * 32].rearrange("p (j t n) -> p j t n", j=4, t=T)
        qt = [reg_a[:, 1024 * j:1024 * j + 1024].rearrange("p (h n) -> p h n", h=2) for j in range(3)]
        QT = reg_q[:, :].bitcast(F16).rearrange("p (r e j n) -> p r e j n", r=2, e=2, j=2)
        dT = reg_q[:, :].bitcast(F16).rearrange("p (f n) -> p f n", f=NF0)
        prob = reg_p[:, :].rearrange("p (j n) -> p j n", j=4)
        pT_h = reg_t[:, 0:1024].bitcast(F16).rearrange("p (j n) -> p j n", j=2)
        pT_l = reg_t[:, 1024:2048].bitcast(F16).rearrange("p (j n) -> p j n", j=2)
        o_sb = reg_o[:, :].rearrange("p (t n) -> p t n", t=T)
        spec = reg_p[:, :].rearrange("p (t n) -> p t n", t=T)
        sq = reg_a[:, 0:1024].rearrange("p (j n) -> p j n", j=2)
        sil = reg_a[:, 1024:2048].rearrange("p (j n) -> p j n", j=2)
        fz = reg_a[:, 2048:3072].rearrange("p (j n) -> p j n", j=2)
        prod = reg_a[:, 3072:3584].rearrange("p (j n) -> p j n", j=2)
        cross = reg_t[:, 0:448].rearrange("p (j i n) -> p j i n", j=2, i=2)
        fin = reg_t[:, 1024:2048].rearrange("p (j i n) -> p j i n", j=2, i=2)
        sT_h = reg_a[:, 3584:3840].bitcast(F16).rearrange("p (j k n) -> p j k n", j=2, k=2)
        sT_l = reg_a[:, 3840:4096].bitcast(F16).rearrange("p (j k n) -> p j k n", j=2, k=2)
        fT_h = reg_o[:, 0:3072].bitcast(F16).rearrange("p (f n) -> p f n", f=NF1)
        fT_l = reg_o[:, 3072:6144].bitcast(F16).rearrange("p (f n) -> p f n", f=NF1)

        N = {}

        def per_row(name, n):
            s = sem(name)
            N[id(s)] = n
            return s

        loaded = sem("loaded")
        w_const = sem("w_const")
        w_mm = sem("w_mm")
        w_cast = sem("w_cast")
        w_cp = sem("w_cp")
        w_hi = sem("w_hi")
        w_lo = sem("w_lo")
        w_qz = sem("w_qz")
        x_in = sem("x_in")
        row_free = sem("row_free")
        stored = [sem("stored0"), sem("stored1")]
        ln = [{k: per_row(f"ln{i}_{k}", n) for k, n in
               (("stat", T), ("mv", T), ("sd", 1), ("rstd", 1), ("xn", T), ("tr", 4), ("hi", 4), ("lo", 4))}
              for i in range(2)]
        lat_mm = per_row("lat_mm", T)
        lat_ev = per_row("lat_ev", T)
        lat_sd = per_row("lat_sd", 1)
        lat_rr = per_row("lat_rr", 1)
        rope_m = per_row("rope_m", 1)
        kq_n = per_row("kq_n", 1)
        v_hi = per_row("v_hi", 1)
        v_lo = per_row("v_lo", 1)
        kq_tr = per_row("kq_tr", 6)
        kq_hi = per_row("kq_hi", 6)
        kq_lo = per_row("kq_lo", 6)
        q_mm = per_row("q_mm", 6 * NP)
        q_ev = per_row("q_ev", 6 * NP)
        q_add = per_row("q_add", 4 * NP)
        q_hi = per_row("q_hi", 4 * NP)
        q_lo = per_row("q_lo", 4 * NP)
        qk_done = per_row("qk_done", STEPS * NP)
        max_done = per_row("max_done", STEPS * NP)
        exp_done = per_row("exp_done", STEPS * NP)
        pt_ready = per_row("pt_ready", TASKS * NP)
        pt_hi = per_row("pt_hi", TASKS * NP)
        pt_lo = per_row("pt_lo", TASKS * NP)
        pv_done = per_row("pv_done", STEPS * NP)
        rinv_done = per_row("rinv_done", STEPS // 4 * NP)
        o_done = per_row("o_done", STEPS // 4 * NP)
        ot_tr = per_row("ot_tr", 2 * T)
        ot_hi = per_row("ot_hi", 2 * T)
        ot_lo = per_row("ot_lo", 2 * T)
        op_mm = per_row("op_mm", T)
        op_add = per_row("op_add", T)
        ff_mm = per_row("ff_mm", 2 * NF0)
        ff_act = per_row("ff_act", 2 * NF0)
        fe_mm = per_row("fe_mm", T)
        fe_ev = per_row("fe_ev", T)
        fe_add = per_row("fe_add", T)
        sp_mm = per_row("sp_mm", T)
        sp_cp = per_row("sp_cp", T)
        sp_sq = per_row("sp_sq", T)
        sp_ss = per_row("sp_ss", T)
        sp_sd = per_row("sp_sd", 1)
        sp_rr = per_row("sp_rr", 1)
        sp_n = per_row("sp_n", T)
        sp_run = per_row("sp_run", T - 2)
        g_mm = per_row("g_mm", 2 * NF1)
        u_mm = per_row("u_mm", 2 * NF1)
        g_act = per_row("g_act", 2 * NF1)
        fz_done = per_row("fz_done", 2 * NF1)
        f_hi = per_row("f_hi", 2 * NF1)
        f_lo = per_row("f_lo", 2 * NF1)
        cs_mm = per_row("cs_mm", T)
        cs_m = per_row("cs_m", T)
        cs_y = per_row("cs_y", 2 * T)
        yt_tr = per_row("yt_tr", T)
        yt_hi = per_row("yt_hi", T)
        yt_lo = per_row("yt_lo", T)
        l1_mm = per_row("l1_mm", T)
        l1_ev = per_row("l1_ev", T)

        def wait(eng, s, b, n):
            eng.wait_ge(s, b * N[id(s)] + n)

        def bank(i, n=HALF):
            return ps[:, i, 0:n]

        ORDER = [T - 1 - k // 2 if k % 2 == 0 else k // 2 for k in range(T)]

        def step_of(s):
            i = ORDER[s % T]
            return s % STEPS // T, i, 1 + (i >= T // 2)

        def o_slot(i):
            return {0: 0, 1: 1, T - 2: 2, T - 1: 3}.get(i, i - 2)

        def tasks_before(s):
            return 3 * (s // 2) + 2 * (s % 2)

        def first(dp):
            return isinstance(dp, int) and dp == 0

        def last(dp):
            return isinstance(dp, int) and dp == LAST

        Q_AT = {0: 0, 1: 1, 4: 2, 5: 3, 8: 4, 9: 5}
        QH_AT = {4: 0, 7: 1, 11: 2, 13: 3}
        LOADS = 30

        block = ctx.enter_context(nc.Block())

        @block.sync
        def _(sp):
            n = 0
            for dst, src in (
                (s_uqT, a["w_uqT"]), (s_ukT, a["w_ukT"]),
                (s_wq[:, :, 0, 64:128], a["w_pe"][:, :, 0, :]), (s_wq[:, :, 1, 0:64], a["w_pe"][:, :, 1, :]),
                (s_wq[:, :, 2, 0:128], a["w_pe"][:, :, 2:4, :].rearrange("p r j n -> p r (j n)")),
                (s_uvT, a["w_uvT"]), (s_wo, a["w_o"]), (s_lat, a["w_lat"]),
                (s_w0, a["W0T"].rearrange("(k p) n -> p k n", p=P)),
                (s_w1, a["W1T"].rearrange("(k p) n -> p k n", p=P)),
                (s_q1, a["W_q"].rearrange("(k p) n -> p k n", p=P)),
                (s_kv1, a["W_kv"].rearrange("(k p) n -> p k n", p=P)),
                (s_o1, a["W_o1T"].rearrange("(k p) n -> p k n", p=P)),
                (s_ft, a["dftT"]), (s_gt, a["idftT"]),
                (s_gate.rearrange("p (k n) -> p k n", k=DC), a["gate_w"].rearrange("(k p) n -> p k n", p=P)),
                (s_up.rearrange("p (k n) -> p k n", k=DC), a["up_w"].rearrange("(k p) n -> p k n", p=P)),
                (s_down.rearrange("p (k n) -> p k n", k=NF1), a["down_w"].rearrange("(k p) n -> p k n", p=P)),
                (ident[:, :], a["consts"][0]), (tri[:, :], a["consts"][1]), (ones[:, :], a["consts"][2]),
                (reg_t[:, 1920:2048], a["consts"][3]),
                (ct_e[:, :], a["rot"][0]), (ct_o[:, :], a["rot"][1]), (st[:, :], a["rot"][2]),
                (cos_t[:, :, :], a["cs"][0]), (sin_t[:, :, :], a["cs"][1]),
                (bias0[:, :], a["bias0"]), (bias1[:, :], a["bias1"]), (gate_s[:, :], a["gate_s"]),
            ):
                sp.dma_start(dst, src).then_inc(loaded, 16)
                n += 1
            assert n == LOADS
            sp.dma_start(up_s[:, :], a["up_s"]).then_inc(loaded, 16)
            sp.dma_start(down_s[:, :], a["down_s"]).then_inc(loaded, 16)
            sp.dma_start(gq[:, :], a["g_q"]).then_inc(loaded, 16)
            sp.dma_start(gkv[0:KL, :], a["g_kv"]).then_inc(loaded, 16)
            sp.dma_start(gkv[KL:P, :], a["g_kv"]).then_inc(loaded, 16)
            sp.wait_ge(w_const, 1)
            sp.dma_start(ge[0:KL, :], a["g_kv"]).then_inc(loaded, 16)
            sp.dma_start(go[KL:P, :], a["g_kv"]).then_inc(loaded, 16)

            def load(b):
                sp.dma_start(xb[:, :, :], a["x"][b].rearrange("(t p) n -> p t n", p=P)).then_inc(x_in, 16)

            def store(b):
                for t in range(T):
                    sp.wait_ge(row_free, b * T + t + 2)
                    sp.dma_start(out[b, t * P:(t + 1) * P, :], outb[:, t % 2, :]).then_inc(stored[t % 2], 16)
                for s in stored:
                    sp.wait_ge(s, b * (16 * T // 2) + 16 * T // 2)

            load(0)
            with sp.Fori(0, B - 1) as b:
                store(b)
                load(b + 1)
            store(B - 1)

        ALL_LOADED = 16 * (LOADS + 7)

        @block.tensor
        def _(pe):
            def product3(o, l_h, l_l, r_h, r_l, start=True, stop=True):
                nc.tensor.matmul(o, l_h, r_h, start=start, stop=False)
                nc.tensor.matmul(o, l_h, r_l, start=False, stop=False)
                return nc.tensor.matmul(o, l_l, r_h, start=False, stop=stop)

            pe.wait_ge(loaded, ALL_LOADED)
            for h in range(H):
                mm = nc.tensor.matmul(ps[0:QL, h // 8, h % 8 * 64:h % 8 * 64 + 64], s_uqT[:, h, :], s_ukT[:, h, :],
                                      start=True, stop=True)
            mm.then_inc(w_mm, 1)
            for k in range(DC):
                for j, w in enumerate((s_q1, s_kv1)):
                    for c in range(DC):
                        mm = nc.tensor.matmul(ps[:, 2 + k, j * D:(j + 1) * D], w[:, c, k * P:(k + 1) * P], s_ft[:, c, :],
                                              start=(c == 0), stop=(c == DC - 1))
            mm.then_inc(w_mm, 1)
            for k in range(DC):
                for c in range(DC):
                    mm = nc.tensor.matmul(ps[:, 4, k * D:(k + 1) * D], s_gt[:, c, k * P:(k + 1) * P], s_o1[:, c, :],
                                          start=(c == 0), stop=(c == DC - 1))
            mm.then_inc(w_mm, 1)
            for g in range(NP // 2):
                if g == 3:
                    pe.wait_ge(w_cp, 2)
                for r in range(2):
                    for e in range(2):
                        h = 4 * g + 2 * r + e
                        mm = nc.tensor.matmul(ps[64 * e:64 * e + 64, (5 + g) % 8, r * D:(r + 1) * D], s_uvT[:, h, :],
                                              s_wo[:, h, :], start=True, stop=True)
                mm.then_inc(w_mm, 1)

            def turn(b, L):
                for g in range(4):
                    wait(pe, L["xn"], b, 2 * g + 2)
                    for k in range(DC):
                        for j in range(2):
                            tr = nc.tensor.transpose(ps[:, g, 256 * k + P * j:256 * k + P * j + P],
                                                     xn[:, 2 * g + j, k * P:(k + 1) * P], ident[:, :])
                    tr.then_inc(L["tr"], 1)

            def latents(b):
                for t in range(T):
                    wait(pe, ln[0]["lo"], b, t // 2 + 1)
                    if t >= 2:
                        wait(pe, lat_ev, b, t - 1)
                    for k in range(DC):
                        tt = slice(t * P, (t + 1) * P)
                        mm = product3(bank(4 + t % 2, LAT), xT_h[:, k, tt], xT_l[:, k, tt], wlat_h[:, k, :],
                                      wlat_l[:, k, :], start=(k == 0), stop=(k == DC - 1))
                    mm.then_inc(lat_mm, 1)

            def turn_latents(b):
                wait(pe, kq_n, b, 1)
                for half in range(2):
                    for j, (src, lo, w) in enumerate(((qn, 0, QL), (kcat, 0, P), (kcat, 64, P))):
                        for i in range(4):
                            tr = nc.tensor.transpose(ps[0:w, 3 * half + j, P * i:P * i + P],
                                                     src[:, 4 * half + i, lo:lo + w], ident[:, :])
                        tr.then_inc(kq_tr, 1)

            def query(b, pair, j, where):
                half, r = j // 3, (2, 0, 1)[j % 3]
                hs = slice(HALF * half, HALF * half + HALF)
                product3(bank(where), wq_h[:, pair, r, :], wq_l[:, pair, r, :], qT_h[:, hs], qT_l[:, hs]).then_inc(q_mm, 1)

            def scores(b, dp, s):
                head, i, banks = step_of(s)
                r = s // STEPS
                if s % STEPS == 0:
                    wait(pe, q_lo, b, 8 * dp + 4 * r + 4)
                if not (first(dp) and s < 2):
                    wait(pe, exp_done, b, dp * 2 * STEPS + s - 1)
                l_h, l_l = (QT[:, r, head, x, i * P:(i + 1) * P] for x in range(2))
                for c in range(banks):
                    w = min((i + 1) * P - c * HALF, HALF)
                    o = ps[:, 2 * (s % 2) + c, 0:w]
                    k_h, k_l = kT_h[head][:, c * HALF:c * HALF + w], kT_l[head][:, c * HALF:c * HALF + w]
                    mm = product3(o, l_h, l_l, k_h, k_l, stop=(c < banks - 1))
                    if c == banks - 1:
                        mm = nc.tensor.matmul(o[:, w - P:w], identb[:, :], maskb[:, :], start=False, stop=True)
                mm.then_inc(qk_done, 1)

            def turn_probs(b, dp, s):
                head, i, banks = step_of(s)
                wait(pe, exp_done, b, dp * 2 * STEPS + s + 1)
                for c in range(banks):
                    n = tasks_before(s) + c
                    if not (first(dp) and n < 3):
                        wait(pe, pt_lo, b, dp * 2 * TASKS + n - 2)
                    for j in range(4 * c, min(4 * c + 4, i + 1)):
                        tr = nc.tensor.transpose(ps[:, 3 + n % 3, (j - 4 * c) * P:(j - 4 * c + 1) * P],
                                                 prob[:, s % 4, j * P:(j + 1) * P], ident[:, :])
                    tr.then_inc(pt_ready, 1)

            def values(b, dp, s):
                head, i, banks = step_of(s)
                wait(pe, pt_lo, b, dp * 2 * TASKS + tasks_before(s + 1))
                if s % 4 == 0 and not (first(dp) and s == 0):
                    wait(pe, o_done, b, dp * 2 * (STEPS // 4) + s // 4)
                slot = o_slot(i)
                o = ps[:, 6, slot * KL:(slot + 1) * KL]
                for j in range(i + 1):
                    mm = product3(o, pT_h[:, s % 2, j * P:(j + 1) * P], pT_l[:, s % 2, j * P:(j + 1) * P],
                                  v_h[:, j, :], v_l[:, j, :], start=(j == 0), stop=(j == i))
                mm.then_inc(pv_done, 1)

            def double_pair(b, dp):
                for s in range(2 * STEPS):
                    scores(b, dp, s)
                    if not (first(dp) and s < 3):
                        turn_probs(b, dp, s - 3)
                    j = Q_AT.get(s % STEPS)
                    r = s // STEPS
                    if j is not None and not (last(dp) and r == 1):
                        wait(pe, q_ev, b, dp * 12 + 6 * r + 6 + j)
                        query(b, 2 * dp + r + 1, j, 7)
                    if not (first(dp) and s < 4):
                        values(b, dp, s - 4)

            def turn_out(b, t):
                for c in range(2):
                    if t >= 2:
                        wait(pe, ot_lo, b, 2 * (t - 2) + c + 1)
                    for j in range(4):
                        tr = nc.tensor.transpose(ps[:, 2 * (t % 2) + c, j * P:(j + 1) * P],
                                                 o_sb[:, t, (4 * c + j) * P:(4 * c + j + 1) * P], ident[:, :])
                    tr.then_inc(ot_tr, 1)

            def project(b, t):
                wait(pe, ot_lo, b, 2 * t + 2)
                if t >= 2:
                    wait(pe, op_add, b, t - 1)
                for r in range(NP):
                    rs_ = slice(r * P, (r + 1) * P)
                    mm = product3(bank(6 + t % 2, D), pT_h[:, t % 2, rs_], pT_l[:, t % 2, rs_], wb_h[:, r, :],
                                  wb_l[:, r, :], start=(r == 0), stop=(r == NP - 1))
                mm.then_inc(op_mm, 1)

            def hidden(b, n):
                half, f = n // NF0, n % NF0
                if n >= 2:
                    wait(pe, ff_act, b, n - 1)
                for k in range(DC):
                    for w in (w0_h, w0_l):
                        mm = nc.tensor.matmul(bank(4 + n % 2), w[:, k, f * P:(f + 1) * P],
                                              xT_h[:, k, half * HALF:(half + 1) * HALF],
                                              start=(k == 0 and w is w0_h), stop=(k == DC - 1 and w is w0_l))
                mm.then_inc(ff_mm, 1)

            def feed_out(b, t):
                wait(pe, ff_act, b, NF0 * (t // 4 + 1))
                if t < 2:
                    wait(pe, ot_lo, b, 2 * T)
                else:
                    wait(pe, fe_ev, b, t - 1)
                for f in range(NF0):
                    for w in (w1_h, w1_l):
                        mm = nc.tensor.matmul(bank(t % 2, D), dT[:, f, t * P:(t + 1) * P], w[:, f, :],
                                              start=(f == 0 and w is w1_h), stop=(f == NF0 - 1 and w is w1_l))
                mm.then_inc(fe_mm, 1)

            def spectra(b, t):
                wait(pe, ln[1]["lo"], b, t // 2 + 1)
                if t >= 2:
                    wait(pe, sp_sq, b, t - 1)
                for k in range(DC):
                    tt = slice(t * P, (t + 1) * P)
                    mm = product3(bank(4 + t % 2), xT_h[:, k, tt], xT_l[:, k, tt], wsp_h[:, k, :], wsp_l[:, k, :],
                                  start=(k == 0), stop=(k == DC - 1))
                mm.then_inc(sp_mm, 1)

            def gate_up(b, n):
                half, f = n // NF1, n % NF1
                if n >= 2:
                    wait(pe, g_act, b, n - 1)
                    wait(pe, fz_done, b, n - 1)
                for w, at, done in ((gate_w, 0, g_mm), (up_w, 2, u_mm)):
                    for k in range(DC):
                        for x in (xT_h, xT_l):
                            mm = nc.tensor.matmul(bank(at + n % 2), w[:, k, f * P:(f + 1) * P],
                                                  x[:, k, half * HALF:(half + 1) * HALF],
                                                  start=(k == 0 and x is xT_h), stop=(k == DC - 1 and x is xT_l))
                    mm.then_inc(done, 1)

            def cumulate(b, t):
                wait(pe, sp_n, b, t + 1)
                if t >= 2:
                    wait(pe, sp_run, b, t - 1)
                    wait(pe, cs_m, b, t - 1)
                mm = nc.tensor.matmul(bank(4 + t % 2, D), tri[:, :], spec[:, t, D:2 * D], start=True, stop=(t == 0))
                if t:
                    before = spec[:, 0, D:2 * D] if t == 1 else run[:, t, :]
                    mm = nc.tensor.matmul(bank(4 + t % 2, D), ones[:, :], before, start=False, stop=True)
                mm.then_inc(cs_mm, 1)

            def turn_prod(b, t):
                wait(pe, cs_y, b, 2 * t + 2)
                if t >= 2:
                    wait(pe, yt_lo, b, t - 1)
                for k in range(DC):
                    tr = nc.tensor.transpose(ps[:, 6 + t % 2, k * P:(k + 1) * P], prod[:, t % 2, k * P:(k + 1) * P],
                                             ident[:, :])
                tr.then_inc(yt_tr, 1)

            def outputs(b, t):
                wait(pe, yt_lo, b, t + 1)
                wait(pe, f_lo, b, 2 * NF1)
                if t >= 2:
                    wait(pe, l1_ev, b, t - 1)
                for k in range(DC):
                    product3(bank(t % 2, D), sT_h[:, t % 2, k, :], sT_l[:, t % 2, k, :], wo1_h[:, k, :], wo1_l[:, k, :],
                             start=(k == 0), stop=(k == DC - 1))
                for f in range(NF1):
                    for x in (fT_h, fT_l):
                        mm = nc.tensor.matmul(ps[:, t % 2, D:2 * D], x[:, f, t * P:(t + 1) * P], down_w[:, f, :],
                                              start=(f == 0 and x is fT_h), stop=(f == NF1 - 1 and x is fT_l))
                mm.then_inc(l1_mm, 1)

            pe.wait_ge(w_lo, 9)
            pe.wait_ge(w_qz, 24)
            with pe.Fori(0, B) as b:
                turn(b, ln[0])
                latents(b)
                turn_latents(b)
                for j in range(6):
                    wait(pe, kq_lo, b, 4 if j >= 3 else 1)
                    if j >= 2:
                        wait(pe, q_ev, b, j - 1)
                    query(b, 0, j, 6 + j % 2)
                wait(pe, kq_lo, b, 6)
                wait(pe, v_lo, b, 1)
                wait(pe, q_ev, b, 6)
                double_pair(b, 0)
                with pe.Fori(1, LAST) as dp:
                    double_pair(b, dp)
                double_pair(b, LAST)
                for s in range(2 * STEPS, 2 * STEPS + 4):
                    if s < 2 * STEPS + 3:
                        turn_probs(b, LAST, s - 3)
                    values(b, LAST, s - 4)
                wait(pe, o_done, b, NP * STEPS // 4)
                turn_out(b, 0)
                for t in range(T):
                    hidden(b, 2 * t)
                    hidden(b, 2 * t + 1)
                    if t + 1 < T:
                        turn_out(b, t + 1)
                    project(b, t)
                for t in range(T):
                    feed_out(b, t)
                turn(b, ln[1])
                for t in range(T):
                    spectra(b, t)
                for n in range(2 * NF1):
                    gate_up(b, n)
                for t in range(T + 2):
                    if t < T:
                        cumulate(b, t)
                    if 1 <= t <= T:
                        turn_prod(b, t - 1)
                    if t >= 2:
                        outputs(b, t - 2)

        @block.scalar
        def _(act):
            def copy(o, i, **kw):
                return nc.scalar.activation(o, i, ACT.Copy, **kw)

            act.wait_ge(loaded, ALL_LOADED)
            act.wait_ge(w_mm, 1)
            for e in range(2):
                src = ps[0:QL, 0:2, :].rearrange("p c (r e n) -> p (c r) e n", e=2, n=64)[:, :, e, :]
                copy(s_wq[:, :, e, 64 * e:64 * e + 64], src).then_inc(w_cp, 1)
            act.wait_ge(w_cp, 2)
            act.wait_ge(w_const, 3)
            copy(wq_h[:, :, :, :], s_wq, scale=gq[:, 0:1]).then_inc(w_hi, 1)
            copy(wlat_h[:, :, :], s_lat, scale=WUP).then_inc(w_hi, 1)
            copy(w0_h[:, :, :], s_w0, scale=WUP).then_inc(w_hi, 1)
            copy(w1_h[:, :, :], s_w1, scale=WUP).then_inc(w_hi, 1)
            act.wait_ge(w_mm, 2)
            copy(wsp_h[:, :, :], ps[:, 2:4, :]).then_inc(w_hi, 1)
            act.wait_ge(w_mm, 3)
            copy(wo1_h[:, :, :], ps[:, 4, :].rearrange("p (k n) -> p k n", k=DC), scale=WO1UP).then_inc(w_hi, 1)
            act.wait_ge(w_mm, 7)
            copy(wb_h[:, 0:6, :], ps[:, 5:8, :].rearrange("p g (r n) -> p (g r) n", r=2), scale=gkv[:, 0:1]).then_inc(w_hi, 1)
            copy(wb_h[:, 6:8, :], ps[:, 0, :].rearrange("p (r n) -> p r n", r=2), scale=gkv[:, 0:1]).then_inc(w_hi, 1)

            def roots(b, L):
                wait(act, L["mv"], b, T)
                nc.scalar.activation(sd[:, :], mv[:, :, 1], ACT.Sqrt, bias=eps[:, 0:1]).then_inc(L["sd"], 1)

            def turned(b, L):
                for g in range(4):
                    wait(act, L["tr"], b, g + 1)
                    copy(xT_h[:, :, 256 * g:256 * g + 256], ps[:, g, :].rearrange("p (k n) -> p k n", k=DC)).then_inc(L["hi"], 1)

            def latents(b):
                for t in range(T):
                    wait(act, lat_mm, b, t + 1)
                    nc.scalar.activation(qn[:, t, :], bank(4 + t % 2)[:, 0:QL], ACT.Square, accum_out=ss[:, 0, t:t + 1])
                    nc.scalar.activation(kcat[:, t, 0:KL], bank(4 + t % 2)[:, QL:QL + KL], ACT.Square,
                                         accum_out=ss[:, 1, t:t + 1])
                    copy(lat[:, t, :], bank(4 + t % 2, LAT)).then_inc(lat_ev, 1)
                wait(act, lat_ev, b, T)
                nc.scalar.activation(rs[:, 0, :], ss[:, 0, :], ACT.Sqrt, bias=eps[:, 1:2], scale=1.0 / QL)
                nc.scalar.activation(rs[:, 1, :], ss[:, 1, :], ACT.Sqrt, bias=eps[:, 1:2], scale=1.0 / KL).then_inc(lat_sd, 1)
                wait(act, kq_n, b, 1)
                copy(v_h[:, :, :], kcat[:, :, 0:KL]).then_inc(v_hi, 1)
                for j in range(6):
                    wait(act, kq_tr, b, j + 1)
                    hs = slice(HALF * (j // 3), HALF * (j // 3) + HALF)
                    if j % 3 == 0:
                        copy(qT_h[:, hs], ps[0:QL, j, :]).then_inc(kq_hi, 1)
                    elif j % 3 == 1:
                        copy(kTe_h[:, hs], bank(j), scale=ge[:, 0:1]).then_inc(kq_hi, 1)
                    else:
                        copy(kTo_h[:, hs], bank(j), scale=go[:, 0:1]).then_inc(kq_hi, 1)

            def query_hi(b, before, r, i):
                half, e = i // 2, i % 2
                wait(act, q_add, b, before + i + 1)
                copy(QT[:, r, e, 0, half * HALF:(half + 1) * HALF], qt[1 + e][:, half, :]).then_inc(q_hi, 1)

            def exponent(b, dp, s):
                head, i, banks = step_of(s)
                wait(act, max_done, b, dp * 2 * STEPS + s + 1)
                if not (first(dp) and s < 4):
                    wait(act, pt_ready, b, dp * 2 * TASKS + tasks_before(s - 3))
                if s % 4 == 0 and not (first(dp) and s < STEPS):
                    wait(act, o_done, b, dp * 2 * (STEPS // 4) + s // 4 - STEPS // 4 + 1)
                w = (i + 1) * P
                sum_slot = s % STEPS // 4 * 4 + o_slot(i)
                nc.scalar.activation(prob[:, s % 4, 0:w], ps[:, 2 * (s % 2):2 * (s % 2) + banks, :].rearrange("p c n -> p (c n)")[:, 0:w],
                                     ACT.Exp, bias=negmax[:, s % STEPS:s % STEPS + 1],
                                     accum_out=rowsum[:, sum_slot:sum_slot + 1]).then_inc(exp_done, 1)

            def probs_hi(b, dp, s):
                head, i, banks = step_of(s)
                if not (first(dp) and s < 2):
                    wait(act, pv_done, b, dp * 2 * STEPS + s - 1)
                for c in range(banks):
                    n = tasks_before(s) + c
                    w = min((i + 1) * P - c * HALF, HALF)
                    wait(act, pt_ready, b, dp * 2 * TASKS + n + 1)
                    copy(pT_h[:, s % 2, c * HALF:c * HALF + w], bank(3 + n % 3, w)).then_inc(pt_hi, 1)

            def double_pair(b, dp):
                for s in range(2 * STEPS):
                    if not (first(dp) and s < 1):
                        exponent(b, dp, s - 1)
                    if not (first(dp) and s < 3):
                        probs_hi(b, dp, s - 3)
                    i, r = QH_AT.get(s % STEPS), s // STEPS
                    if i is not None and not (last(dp) and r == 1):
                        query_hi(b, dp * 8 + 4 * r + 4, 1 - r, i)
            def out_hi(b, t):
                for c in range(2):
                    if t >= 2 and c == 0:
                        wait(act, op_mm, b, t - 1)
                    wait(act, ot_tr, b, 2 * t + c + 1)
                    copy(pT_h[:, t % 2, c * HALF:(c + 1) * HALF], bank(2 * (t % 2) + c)).then_inc(ot_hi, 1)

            def gelu(b, n):
                half, f = n // NF0, n % NF0
                wait(act, ff_mm, b, n + 1)
                nc.scalar.activation(dT[:, f, half * HALF:(half + 1) * HALF], bank(4 + n % 2), ACT.Gelu,
                                     bias=bias0[:, f:f + 1], scale=1 / WUP).then_inc(ff_act, 1)

            with act.Fori(0, B) as b:
                act.wait_ge(row_free, b * T + 1)
                roots(b, ln[0])
                turned(b, ln[0])
                latents(b)
                for i in range(4):
                    query_hi(b, 0, 0, i)
                double_pair(b, 0)
                with act.Fori(1, LAST) as dp:
                    double_pair(b, dp)
                double_pair(b, LAST)
                exponent(b, LAST, 2 * STEPS - 1)
                probs_hi(b, LAST, 2 * STEPS - 3)
                probs_hi(b, LAST, 2 * STEPS - 2)
                probs_hi(b, LAST, 2 * STEPS - 1)
                wait(act, pv_done, b, NP * STEPS)
                out_hi(b, 0)
                for t in range(T):
                    gelu(b, 2 * t)
                    gelu(b, 2 * t + 1)
                    if t + 1 < T:
                        out_hi(b, t + 1)
                roots(b, ln[1])
                turned(b, ln[1])
                for t in range(T):
                    wait(act, sp_mm, b, t + 1)
                    copy(spec[:, t, :], bank(4 + t % 2)).then_inc(sp_cp, 1)
                    if t >= 2:
                        wait(act, sp_ss, b, t - 1)
                    nc.scalar.activation(sq[:, t % 2, :], bank(4 + t % 2), ACT.Square).then_inc(sp_sq, 1)
                wait(act, sp_ss, b, T)
                nc.scalar.activation(rs2[:, :, :], ss2[:, :, :], ACT.Sqrt).then_inc(sp_sd, 1)
                for n in range(2 * NF1):
                    half, f = n // NF1, n % NF1
                    wait(act, g_mm, b, n + 1)
                    if n >= 2:
                        wait(act, fz_done, b, n - 1)
                    nc.scalar.activation(sil[:, n % 2, :], bank(n % 2), ACT.Silu, scale=gate_s[:, f:f + 1]).then_inc(g_act, 1)
                    wait(act, fz_done, b, n + 1)
                    copy(fT_h[:, f, half * HALF:(half + 1) * HALF], fz[:, n % 2, :]).then_inc(f_hi, 1)
                for t in range(T):
                    wait(act, yt_tr, b, t + 1)
                    if t >= 2:
                        wait(act, l1_mm, b, t - 1)
                    copy(sT_h[:, t % 2, :, :], ps[:, 6 + t % 2, 0:D].rearrange("p (k n) -> p k n", k=DC)).then_inc(yt_hi, 1)

        @block.vector
        def _(dve):
            tt, ts, stt = nc.vector.tensor_tensor, nc.vector.tensor_scalar, nc.vector.scalar_tensor_tensor

            nc.vector.memset(ge[:, :], 1.0)
            nc.vector.memset(eps[:, 0:1], LN_EPS)
            nc.vector.memset(eps[:, 1:2], RMS_EPS * WUP * WUP)
            nc.vector.memset(go[:, :], 1.0).then_inc(w_const, 1)
            dve.wait_ge(loaded, ALL_LOADED)
            ts(gq[:, :], gq[:, :], WUP, None, ALU.mult).then_inc(w_const, 1)
            ts(gkv[:, :], gkv[:, :], WUP, None, ALU.mult).then_inc(w_const, 1)
            nc.vector.tensor_copy(identb[:, :], ident[:, :]).then_inc(w_cast, 1)
            nc.vector.tensor_copy(maskb[:, :], reg_t[:, 1920:2048]).then_inc(w_cast, 1)
            ts(up_s[:, :], up_s[:, :], FDOWN, None, ALU.mult).then_inc(w_cast, 1)
            ts(down_s[:, :], down_s[:, :], 1 / FDOWN, None, ALU.mult).then_inc(w_cast, 1)
            q = 0

            def done(ins):
                nonlocal q
                q += 1
                ins.then_inc(w_qz, 1)
                dve.wait_ge(w_qz, q)

            for w, o in ((s_gate, gate_w), (s_up, up_w), (s_down, down_w)):
                done(ts(s_m.bitcast(U32), w.bitcast(U32), 0x7F800000, None, ALU.bitwise_and))
                done(ts(s_m, s_m, 2.0 ** -6, 1.5 * 2.0 ** 20, ALU.max, ALU.mult))
                done(tt(w, w, s_m, ALU.add))
                done(tt(w, w, s_m, ALU.subtract))
                done(tt(s_m, w, w, ALU.mult))
                done(ts(s_m, s_m, 448.0 ** 2, 3e38, ALU.is_gt, ALU.mult))
                done(ts(s_m, s_m, 3e38, 0.0, ALU.mult, ALU.mult))
                done(tt(o[:, :, :].rearrange("p k n -> p (k n)"), w, s_m, ALU.add))
            for n, (o, src, scale, h) in enumerate((
                (wq_l[:, :, :, :].rearrange("p r j n -> p (r j n)"), s_wq.rearrange("p r j n -> p (r j n)"), gq[:, 0:1],
                 wq_h[:, :, :, :].rearrange("p r j n -> p (r j n)")),
                (wlat_l[:, :, :], s_lat, WUP, wlat_h[:, :, :]),
                (w0_l[:, :, :], s_w0, WUP, w0_h[:, :, :]),
                (w1_l[:, :, :], s_w1, WUP, w1_h[:, :, :]),
                (wsp_l[:, :, :], ps[:, 2:4, :], 1.0, wsp_h[:, :, :]),
                (wo1_l[:, :, :], ps[:, 4, :].rearrange("p (k n) -> p k n", k=DC), WO1UP, wo1_h[:, :, :]),
                (wb_l[:, 0:6, :], ps[:, 5:8, :].rearrange("p g (r n) -> p (g r) n", r=2), gkv[:, 0:1], wb_h[:, 0:6, :]),
                (wb_l[:, 6:8, :], ps[:, 0, :].rearrange("p (r n) -> p r n", r=2), gkv[:, 0:1], wb_h[:, 6:8, :]),
            )):
                dve.wait_ge(w_hi, n + 1)
                stt(out=o, in0=src, scalar=scale, in1=h, op0=ALU.mult, op1=ALU.subtract).then_inc(w_lo, 1)
            dve.wait_ge(w_lo, 8)
            nc.vector.memset(eps[:, 2:3], 0.0).then_inc(w_lo, 1)
            dve.wait_ge(w_lo, 9)
            nc.vector.memset(tick[:, :], 0.0).then_inc(row_free, 1)

            def stats(b, L):
                for t in range(T):
                    if L is ln[1]:
                        wait(dve, fe_add, b, t + 1)
                    nc.vector.bn_stats(bnst[:, t, :], xb[:, t, :]).then_inc(L["stat"], 1)
                wait(dve, L["stat"], b, T)
                nc.vector.memset(tick[:, :], 0.0)
                for t in range(T):
                    nc.vector.bn_aggr(mv[:, t, :], bnst[:, t, :]).then_inc(L["mv"], 1)
                wait(dve, L["sd"], b, 1)
                nc.vector.reciprocal(rstd[:, :], sd[:, :]).then_inc(L["rstd"], 1)
                wait(dve, L["rstd"], b, 1)
                for t in range(T):
                    ts(xn[:, t, :], xb[:, t, :], mv[:, t, 0:1], rstd[:, t:t + 1], ALU.subtract, ALU.mult).then_inc(L["xn"], 1)
                for g in range(4):
                    wait(dve, L["hi"], b, g + 1)
                    gs_ = slice(256 * g, 256 * g + 256)
                    tt(xT_l[:, :, gs_], ps[:, g, :].rearrange("p (k n) -> p k n", k=DC), xT_h[:, :, gs_],
                       ALU.subtract).then_inc(L["lo"], 1)

            def latents(b):
                wait(dve, lat_sd, b, 1)
                nc.vector.reciprocal(rr[:, :, :], rs[:, :, :]).then_inc(lat_rr, 1)
                x1, x2 = lat[:, :, QL + KL:QL + KL + 32], lat[:, :, QL + KL + 32:LAT]
                tt(ropet[:, 0, :, :], x1, cos_t[:, :, :], ALU.mult)
                tt(ropet[:, 1, :, :], x2, sin_t[:, :, :], ALU.mult)
                tt(ropet[:, 2, :, :], x1, sin_t[:, :, :], ALU.mult)
                tt(ropet[:, 3, :, :], x2, cos_t[:, :, :], ALU.mult).then_inc(rope_m, 1)
                wait(dve, lat_rr, b, 1)
                tt(qn, lat[:, :, 0:QL], rr[:, 0, :].unsqueeze(2).broadcast_to([P, T, QL]), ALU.mult)
                kv_r = rr[:, 1, :].unsqueeze(2).broadcast_to([P, T, KL])
                tt(kcat[:, :, 0:KL], lat[:, :, QL:QL + KL], kv_r, ALU.mult)
                tt(kcat[:, :, P:P + KL], lat[:, :, QL:QL + KL], kv_r, ALU.mult)
                wait(dve, rope_m, b, 1)
                tt(kcat[:, :, KL:KL + 32], ropet[:, 0, :, :], ropet[:, 1, :, :], ALU.subtract)
                tt(kcat[:, :, KL + 32:P], ropet[:, 2, :, :], ropet[:, 3, :, :], ALU.add).then_inc(kq_n, 1)
                wait(dve, v_hi, b, 1)
                tt(v_l[:, :, :], kcat[:, :, 0:KL], v_h[:, :, :], ALU.subtract).then_inc(v_lo, 1)
                for j in range(6):
                    wait(dve, kq_hi, b, j + 1)
                    hs = slice(HALF * (j // 3), HALF * (j // 3) + HALF)
                    if j % 3 == 0:
                        tt(qT_l[:, hs], ps[0:QL, j, :], qT_h[:, hs], ALU.subtract).then_inc(kq_lo, 1)
                    else:
                        g, h_, l_ = ((ge, kTe_h, kTe_l), (go, kTo_h, kTo_l))[j % 3 - 1]
                        stt(out=l_[:, hs], in0=bank(j), scalar=g[:, 0:1], in1=h_[:, hs], op0=ALU.mult,
                            op1=ALU.subtract).then_inc(kq_lo, 1)

            def query_ev(b, before, j, where, lo_before=None):
                half = j // 3
                wait(dve, q_mm, b, before + j + 1)
                if j % 3 == 0 and lo_before is not None:
                    wait(dve, q_lo, b, lo_before + 2 * half + 2)
                table = (st, ct_e, ct_o)[j % 3]
                tt(qt[j % 3][:, half, :], bank(where), table[:, half * HALF:(half + 1) * HALF], ALU.mult).then_inc(q_ev, 1)

            def maxima(b, dp, s):
                head, i, banks = step_of(s)
                wait(dve, qk_done, b, dp * 2 * STEPS + s + 1)
                w = (i + 1) * P
                nc.vector.tensor_reduce(negmax[:, s % STEPS:s % STEPS + 1],
                                        ps[:, 2 * (s % 2):2 * (s % 2) + banks, :].rearrange("p c n -> p (c n)")[:, 0:w],
                                        AX_X, ALU.max, negate=True).then_inc(max_done, 1)

            def probs_lo(b, dp, s):
                head, i, banks = step_of(s)
                for c in range(banks):
                    n = tasks_before(s) + c
                    w = min((i + 1) * P - c * HALF, HALF)
                    wait(dve, pt_hi, b, dp * 2 * TASKS + n + 1)
                    cs = slice(c * HALF, c * HALF + w)
                    tt(pT_l[:, s % 2, cs], bank(3 + n % 3, w), pT_h[:, s % 2, cs], ALU.subtract).then_inc(pt_lo, 1)

            def sums(b, dp, s):
                wait(dve, exp_done, b, dp * 2 * STEPS + s + 1)
                nc.vector.reciprocal(rinv[:, s // 4 % 2, :], rowsum[:, s % STEPS - 3:s % STEPS + 1]).then_inc(rinv_done, 1)

            def out_ev(b, dp, s):
                head, i, banks = step_of(s)
                r = s // STEPS
                wait(dve, rinv_done, b, dp * 2 * (STEPS // 4) + s // 4 + 1)
                wait(dve, pv_done, b, dp * 2 * STEPS + s + 1)
                col = (2 * dp + r) * P + KL * head
                near = slice(1, 3) if 2 <= i < T - 2 else slice(0, 4, 3)
                tt(o_sb.rearrange("p (g v) n -> p g v n", v=2)[:, near, :, bass.ds(col, KL)],
                   bank(6, 4 * KL).rearrange("p (g v n) -> p g v n", g=2, v=2),
                   rinv[:, s // 4 % 2, :].rearrange("p (g v) -> p g v", v=2).unsqueeze(3).broadcast_to([P, 2, 2, KL]),
                   ALU.mult).then_inc(o_done, 1)

            def double_pair(b, dp):
                for s in range(2 * STEPS):
                    maxima(b, dp, s)
                    if s % 4 == 3 and not (first(dp) and s < 4):
                        out_ev(b, dp, s - 4)
                    if not (first(dp) and s < 3):
                        probs_lo(b, dp, s - 3)
                    if s % 4 == 2 and not (first(dp) and s < 6):
                        sums(b, dp, s - 3)
                    j, r = Q_AT.get(s % STEPS), s // STEPS
                    if j is not None and not (last(dp) and r == 1):
                        query_ev(b, dp * 12 + 6 * r + 6, j, 7, dp * 8 + 4 * r)
            def out_lo(b, t):
                for c in range(2):
                    wait(dve, ot_hi, b, 2 * t + c + 1)
                    cs = slice(c * HALF, (c + 1) * HALF)
                    tt(pT_l[:, t % 2, cs], bank(2 * (t % 2) + c), pT_h[:, t % 2, cs], ALU.subtract).then_inc(ot_lo, 1)

            with dve.Fori(0, B) as b:
                dve.wait_ge(row_free, b * T + 1)
                dve.wait_ge(x_in, b * 16 + 16)
                stats(b, ln[0])
                latents(b)
                for j in range(6):
                    query_ev(b, 0, j, 6 + j % 2)
                double_pair(b, 0)
                with dve.Fori(1, LAST) as dp:
                    double_pair(b, dp)
                double_pair(b, LAST)
                probs_lo(b, LAST, 2 * STEPS - 3)
                probs_lo(b, LAST, 2 * STEPS - 2)
                probs_lo(b, LAST, 2 * STEPS - 1)
                sums(b, LAST, 2 * STEPS - 1)
                out_ev(b, LAST, 2 * STEPS - 1)
                out_lo(b, 0)
                for t in range(T):
                    if t + 1 < T:
                        out_lo(b, t + 1)
                    wait(dve, op_mm, b, t + 1)
                    stt(out=xb[:, t, :], in0=bank(6 + t % 2, D), scalar=1 / WUP, in1=xb[:, t, :], op0=ALU.mult,
                        op1=ALU.add).then_inc(op_add, 1)
                for t in range(T):
                    wait(dve, fe_mm, b, t + 1)
                    if t >= 2:
                        wait(dve, fe_add, b, t - 1)
                    stt(out=e16[:, t % 2, :], in0=bank(t % 2, D), scalar=1 / WUP, in1=bias1[:, :], op0=ALU.mult,
                        op1=ALU.add).then_inc(fe_ev, 1)
                    wait(dve, fe_ev, b, t + 1)
                    tt(xb[:, t, :], xb[:, t, :], e16[:, t % 2, :], ALU.add).then_inc(fe_add, 1)
                stats(b, ln[1])
                for t in range(T):
                    wait(dve, sp_sq, b, t + 1)
                    nc.vector.tensor_reduce(ss2[:, t, :].rearrange("p (j h) -> p j h", j=2),
                                            sq[:, t % 2, :].rearrange("p (j c h) -> p j h c", j=2, h=16),
                                            AX_X, ALU.add).then_inc(sp_ss, 1)
                wait(dve, sp_sd, b, 1)
                nc.vector.reciprocal(rr2[:, :, :], rs2[:, :, :]).then_inc(sp_rr, 1)
                for n in range(2 * NF1):
                    half, f = n // NF1, n % NF1
                    wait(dve, g_act, b, n + 1)
                    wait(dve, u_mm, b, n + 1)
                    if n >= 2:
                        wait(dve, f_lo, b, n - 1)
                    stt(out=fz[:, n % 2, :], in0=bank(2 + n % 2), scalar=up_s[:, f:f + 1], in1=sil[:, n % 2, :],
                        op0=ALU.mult, op1=ALU.mult).then_inc(fz_done, 1)
                    wait(dve, f_hi, b, n + 1)
                    hs = slice(half * HALF, (half + 1) * HALF)
                    tt(fT_l[:, f, hs], fz[:, n % 2, :], fT_h[:, f, hs], ALU.subtract).then_inc(f_lo, 1)
                for t in range(T + 2):
                    if t < T:
                        wait(dve, cs_mm, b, t + 1)
                        if t >= 2:
                            wait(dve, yt_tr, b, t - 1)
                            wait(dve, cs_y, b, 2 * t - 2)
                        c_ps = bank(4 + t % 2, D)
                        tt(prod[:, t % 2, :], spec[:, t, 0:D], c_ps, ALU.mult)
                        tt(cross[:, t % 2, 0, :], spec[:, t, 32:144], c_ps[:, 144:256], ALU.mult)
                        tt(cross[:, t % 2, 1, :], spec[:, t, 144:256], c_ps[:, 32:144], ALU.mult).then_inc(cs_m, 1)
                    if 1 <= t <= T:
                        wait(dve, yt_hi, b, t)
                        tt(sT_l[:, (t - 1) % 2, :, :], ps[:, 6 + (t - 1) % 2, 0:D].rearrange("p (k n) -> p k n", k=DC),
                           sT_h[:, (t - 1) % 2, :, :], ALU.subtract).then_inc(yt_lo, 1)
                    if t >= 2:
                        u = t - 2
                        wait(dve, l1_mm, b, u + 1)
                        if u >= 2:
                            dve.wait_ge(row_free, b * T + u)
                        tt(fin[:, u % 2, 0, :], ps[:, u % 2, D:2 * D], down_s[:, :], ALU.mult)
                        stt(out=fin[:, u % 2, 1, :], in0=bank(u % 2, D), scalar=1 / WO1UP, in1=xb[:, u, :], op0=ALU.mult,
                            op1=ALU.add).then_inc(l1_ev, 1)

        @block.gpsimd
        def _(pool):
            tt = nc.gpsimd.tensor_tensor

            def pair_queries(b, pair, r):
                for half in range(2):
                    if not (first(pair) and half == 0):
                        wait(pool, q_lo, b, pair * 4 + 2 * half)
                    for e in range(2):
                        wait(pool, q_ev, b, pair * 6 + 3 * half + 2 + e)
                        if e:
                            wait(pool, q_add, b, pair * 4 + 2 * half + 1)
                        rows = slice(64, 128) if e == 0 else slice(0, 64)
                        tt(qt[1 + e][rows, half, :], qt[1 + e][rows, half, :], qt[0][rows, half, :],
                           ALU.add).then_inc(q_add, 1)
                    wait(pool, q_add, b, pair * 4 + 2 * half + 2)
                    for e in range(2):
                        wait(pool, q_hi, b, pair * 4 + 2 * half + e + 1)
                        hs = slice(half * HALF, (half + 1) * HALF)
                        tt(QT[:, r, e, 1, hs], qt[1 + e][:, half, :], QT[:, r, e, 0, hs], ALU.subtract).then_inc(q_lo, 1)

            with pool.Fori(0, B) as b:
                pool.wait_ge(row_free, b * T + 1)
                pair_queries(b, 0, 0)
                with pool.Fori(0, LAST) as dp:
                    pair_queries(b, 2 * dp + 1, 1)
                    pair_queries(b, 2 * dp + 2, 0)
                pair_queries(b, NP - 1, 1)
                wait(pool, sp_rr, b, 1)
                for t in range(T):
                    v = spec[:, t, :].rearrange("p (j c h) -> p j c h", j=2, h=16)
                    for j in range(2):
                        ins = tt(v[:, j], v[:, j], rr2[:, t, 16 * j:16 * j + 16].unsqueeze(1).broadcast_to([P, 16, 16]), ALU.mult)
                    ins.then_inc(sp_n, 1)
                    wait(pool, sp_n, b, t + 1)
                    if 1 <= t < T - 1:
                        before = spec[:, 0, D:2 * D] if t == 1 else run[:, t, :]
                        if t >= 2:
                            wait(pool, sp_run, b, t - 1)
                        tt(run[:, t + 1, :], before, spec[:, t, D:2 * D], ALU.add).then_inc(sp_run, 1)
                for t in range(T + 2):
                    if t < T:
                        wait(pool, cs_m, b, t + 1)
                        p_ = prod[:, t % 2, :]
                        tt(p_[:, 32:144], p_[:, 32:144], p_[:, 144:256], ALU.subtract).then_inc(cs_y, 1)
                        wait(pool, cs_y, b, 2 * t + 1)
                        tt(p_[:, 144:256], cross[:, t % 2, 0, :], cross[:, t % 2, 1, :], ALU.add).then_inc(cs_y, 1)
                    if t >= 2:
                        u = t - 2
                        wait(pool, l1_ev, b, u + 1)
                        if u >= 2:
                            pool.wait_ge(stored[u % 2], b * (16 * T // 2) + 16 * (u // 2))
                        tt(outb[:, u % 2, :], fin[:, u % 2, 0, :], fin[:, u % 2, 1, :], ALU.add).then_inc(row_free, 1)


_OUT = ((4, 1024, 256), "float32")


def _layout(i):
    import numpy as np

    H, NOPE, ROPE, VD, S, HD = 16, 128, 64, 128, 1024, 16
    c = np.ascontiguousarray
    w_uq = np.asarray(i["L0_attn_w_uq"]).reshape(96, H, NOPE + ROPE)
    pe = w_uq[:, :, NOPE:]
    swapped = np.concatenate([pe[:, :, 32:], pe[:, :, :32]], axis=2)
    w_pe = np.stack([pe[:, 0::2], pe[:, 1::2], swapped[:, 1::2], swapped[:, 0::2]], axis=2)
    lat = np.concatenate([i["L0_attn_w_dq"], i["L0_attn_w_dkv"], i["L0_attn_w_kr"]], axis=1)
    d = {
        "x": i["L0_attn_x"],
        "w_uqT": w_uq[:, :, :NOPE].transpose(2, 1, 0),
        "w_ukT": np.asarray(i["L0_attn_w_uk"]).reshape(64, H, NOPE).transpose(2, 1, 0),
        "w_uvT": np.asarray(i["L0_attn_w_uv"]).reshape(64, H, VD).transpose(2, 1, 0),
        "w_pe": w_pe,
        "w_o": np.asarray(i["L0_attn_w_o"]).reshape(H, VD, 256).transpose(1, 0, 2),
        "w_lat": lat.reshape(2, 128, 224).transpose(1, 0, 2),
        "g_q": np.asarray(i["L0_attn_g_q"]).reshape(96, 1), "g_kv": np.asarray(i["L0_attn_g_kv"]).reshape(64, 1),
        "W0T": np.asarray(i["L0_ffn_W0"]).T, "W1T": np.asarray(i["L0_ffn_W1"]).T,
        "bias0": np.asarray(i["L0_ffn_bias0"]).reshape(8, 128).T,
        "bias1": np.tile(np.asarray(i["L0_ffn_bias1"]).reshape(1, 256), (128, 1)),
        "W_q": i["L1_attn_W_q"], "W_kv": i["L1_attn_W_kv"], "W_o1T": np.asarray(i["L1_attn_W_o"]).T,
        "gate_w": i["L1_ffn_gate_w"], "up_w": i["L1_ffn_up_w"], "down_w": i["L1_ffn_down_w"],
        "gate_s": np.asarray(i["L1_ffn_gate_scale"]).reshape(6, 128).T,
        "up_s": np.asarray(i["L1_ffn_up_scale"]).reshape(6, 128).T,
        "down_s": np.tile(np.asarray(i["L1_ffn_down_scale"]).reshape(1, 256), (128, 1)),
    }
    inv_freq = (np.float32(1.0) / np.float32(10000.0) ** (np.arange(0, ROPE, 2, dtype=np.float32) / np.float32(ROPE))).astype(np.float32)
    freqs = np.outer(np.arange(S, dtype=np.float32), inv_freq).astype(np.float32).astype(np.float64)
    cos, sin = np.cos(freqs), np.sin(freqs)
    sc = (NOPE + ROPE) ** -0.5 / WUP
    pe_c = np.concatenate([cos, cos], axis=1).T * sc
    pe_s = np.concatenate([-sin, sin], axis=1).T * sc
    flat = np.full_like(pe_c, sc)
    d["rot"] = np.stack([np.concatenate([flat, pe_c]), np.concatenate([pe_c, flat]), np.concatenate([pe_s, pe_s])]).astype(np.float32)
    d["cs"] = np.stack([x.reshape(8, 128, 32).transpose(1, 0, 2) / WUP for x in (cos, sin)]).astype(np.float32)
    j = np.arange(HD)
    rows, back = [], []
    for k in (0, 8):
        rows.append(np.cos(2 * np.pi * j * k / HD) / 4)
        back.append(np.cos(2 * np.pi * j * k / HD) / HD)
    for k in range(1, 8):
        rows.append(np.cos(2 * np.pi * j * k / HD) * 2 ** 0.5 / 4)
        back.append(np.cos(2 * np.pi * j * k / HD) / HD)
    for k in range(1, 8):
        rows.append(-np.sin(2 * np.pi * j * k / HD) * 2 ** 0.5 / 4)
        back.append(-np.sin(2 * np.pi * j * k / HD) / HD)
    dftT = np.zeros((256, 256))
    idftT = np.zeros((256, 256))
    for h in range(H):
        for n in range(16):
            dftT[h * 16:(h + 1) * 16, n * 16 + h] = rows[n]
            idftT[h * 16:(h + 1) * 16, n * 16 + h] = back[n]
    for name, m in (("dftT", dftT), ("idftT", idftT)):
        d[name] = m.reshape(2, 128, 256).transpose(1, 0, 2).astype(np.float32)
    one = np.ones((128, 128), np.float32)
    d["consts"] = np.stack([np.eye(128, dtype=np.float32), np.triu(one), one, np.triu(one, 1) * np.float32(-1e30)])
    return {k: c(v) for k, v in d.items()}


def kernel(**inputs):
    import concourse.bacc as _bacc
    from concourse import mybir as _mybir
    from concourse.bass_utils import run_bass_kernel_spmd as _run

    nc = _bacc.Bacc("TRN2", target_bir_lowering=False, num_devices=1)
    arrays = _layout(inputs)
    aps = {n: nc.dram_tensor(f"in_{n}", v.shape, _mybir.dt.from_np(v.dtype), kind="ExternalInput").ap()
           for n, v in arrays.items()}
    out = nc.dram_tensor("out_x", _OUT[0], _mybir.dt.float32, kind="ExternalOutput").ap()
    two_layer_kernel(nc, aps, out)
    r = _run(nc, [{f"in_{n}": v for n, v in arrays.items()}], core_ids=[0])
    return r.results[0]["out_x"]
```

```python
from contextlib import ExitStack

import concourse.bass as bass
from concourse import mybir

F32 = mybir.dt.float32
F16 = mybir.dt.float16
BF16 = mybir.dt.bfloat16
U32 = mybir.dt.uint32
ALU = mybir.AluOpType
ACT = mybir.ActivationFunctionType
AX_X = mybir.AxisListType.X

P = 128
HALF = 512
WUP = 64.0
WO1UP = 16.0
FDOWN = 1.0 / 64
LN_EPS = 1e-5
RMS_EPS = 1e-6


def two_layer_kernel(nc, a, out):
    B, S, D = a["x"].shape
    T = S // P
    QL, KL, ROPE = 96, 64, 64
    LAT = QL + KL + ROPE
    NP = a["w_pe"].shape[1]
    H = 2 * NP
    F0 = a["W0T"].shape[1]
    NF0 = F0 // P
    F1 = a["gate_w"].shape[1]
    NF1 = F1 // P
    DC = D // P
    STEPS = 2 * T
    TASKS = 3 * T
    LAST = NP // 2 - 1

    with ExitStack() as ctx:
        def sb(name, shape, dt):
            return ctx.enter_context(nc.sbuf_tensor(name, shape, dt))

        def sem(name):
            return ctx.enter_context(nc.semaphore(name))

        ps = ctx.enter_context(nc.psum_tensor("ps", [P, 8, HALF], F32))

        ident = sb("ident", [P, P], F32)
        identb = sb("identb", [P, P], BF16)
        maskb = sb("maskb", [P, P], BF16)
        tri = sb("tri", [P, P], F32)
        ones = sb("ones", [P, P], F32)
        ct_e = sb("ct_e", [P, S], F32)
        ct_o = sb("ct_o", [P, S], F32)
        st = sb("st", [P, S], F32)
        cos_t = sb("cos_t", [P, T, 32], F32)
        sin_t = sb("sin_t", [P, T, 32], F32)
        gq = sb("gq", [QL, 1], F32)
        ge = sb("ge", [P, 1], F32)
        go = sb("go", [P, 1], F32)
        gkv = sb("gkv", [P, 1], F32)
        bias0 = sb("bias0", [P, NF0], F32)
        bias1 = sb("bias1", [P, D], F32)
        gate_s = sb("gate_s", [P, NF1], F32)
        up_s = sb("up_s", [P, NF1], F32)
        down_s = sb("down_s", [P, D], F32)
        eps = sb("eps", [P, 3], F32)
        wlat_h, wlat_l = (sb(f"wlat_{x}", [P, DC, LAT], F16) for x in "hl")
        wq_h, wq_l = (sb(f"wq_{x}", [QL, NP, 3, P], F16) for x in "hl")
        wb_h, wb_l = (sb(f"wb_{x}", [P, NP, D], F16) for x in "hl")
        w0_h, w0_l = (sb(f"w0_{x}", [P, DC, F0], F16) for x in "hl")
        w1_h, w1_l = (sb(f"w1_{x}", [P, NF0, D], F16) for x in "hl")
        wsp_h, wsp_l = (sb(f"wsp_{x}", [P, DC, 2 * D], F16) for x in "hl")
        wo1_h, wo1_l = (sb(f"wo1_{x}", [P, DC, D], F16) for x in "hl")
        gate_w = sb("gate_w", [P, DC, F1], F16)
        up_w = sb("up_w", [P, DC, F1], F16)
        down_w = sb("down_w", [P, NF1, D], F16)

        xb = sb("xb", [P, T, D], F32)
        xT_h, xT_l = (sb(f"xT_{x}", [P, DC, S], F16) for x in "hl")
        qT_h, qT_l = (sb(f"qT_{x}", [QL, S], F16) for x in "hl")
        kTe_h, kTe_l, kTo_h, kTo_l = (sb(f"kT{x}", [P, S], F16) for x in ("eh", "el", "oh", "ol"))
        kT_h, kT_l = [kTe_h, kTo_h], [kTe_l, kTo_l]
        v_h, v_l = (sb(f"v_{x}", [P, T, KL], F16) for x in "hl")
        negmax = sb("negmax", [P, STEPS], F32)
        rowsum = sb("rowsum", [P, STEPS], F32)
        rinv = sb("rinv", [P, 2, 4], F32)
        bnst = sb("bnst", [P, T, 6], F32)
        mv = sb("mv", [P, T, 2], F32)
        sd = sb("sd", [P, T], F32)
        rstd = sb("rstd", [P, T], F32)
        tick = sb("tick", [P, T], F32)
        ss = sb("ss", [P, 2, T], F32)
        rs = sb("rs", [P, 2, T], F32)
        rr = sb("rr", [P, 2, T], F32)
        ss2 = sb("ss2", [P, T, 32], F32)
        rs2 = sb("rs2", [P, T, 32], F32)
        rr2 = sb("rr2", [P, T, 32], F32)
        e16 = sb("e16", [P, 2, D], F16)
        outb = sb("outb", [P, 2, D], F32)

        reg_o = sb("reg_o", [P, 8192], F32)
        reg_p = sb("reg_p", [P, 4096], F32)
        reg_q = sb("reg_q", [P, 4096], F32)
        reg_a = sb("reg_a", [P, 4096], F32)
        reg_x = sb("reg_x", [P, 2048], F32)
        reg_t = sb("reg_t", [P, 2048], F32)
        s_wo = reg_o[:, 0:4096].rearrange("p (h n) -> p h n", h=H)
        s_w0 = reg_o[:, 4096:6144].rearrange("p (k n) -> p k n", k=DC)
        s_w1 = reg_o[:, 6144:8192].rearrange("p (k n) -> p k n", k=NF0)
        s_uqT = reg_p[:, 0:1536].rearrange("p (h n) -> p h n", h=H)
        s_ukT = reg_p[:, 1536:2560].rearrange("p (h n) -> p h n", h=H)
        s_uvT = reg_p[:, 2560:3584].rearrange("p (h n) -> p h n", h=H)
        s_lat = reg_p[:, 3584:3584 + 448].rearrange("p (k n) -> p k n", k=DC)
        s_wq = reg_q[0:QL, 0:3072].rearrange("p (r j n) -> p r j n", r=NP, j=3)
        s_q1 = reg_q[:, 3072:3584].rearrange("p (k n) -> p k n", k=DC)
        s_kv1 = reg_q[:, 3584:4096].rearrange("p (k n) -> p k n", k=DC)
        s_gate = reg_a[:, 0:1536]
        s_up = reg_p[:, 0:1536]
        xb_flat = xb[:, :, :].rearrange("p t n -> p (t n)")
        s_down = xb_flat[:, 0:1536]
        s_o1 = xb_flat[:, 1536:2048].rearrange("p (k n) -> p k n", k=DC)
        s_ft = reg_t[:, 1024:1536].rearrange("p (k n) -> p k n", k=DC)
        s_gt = reg_t[:, 1536:2048].rearrange("p (k n) -> p k n", k=DC)
        s_mask = outb[:, 0, 0:P]
        xn = reg_x[:, :].rearrange("p (t n) -> p t n", t=T)
        run = reg_q[:, 2048:4096].rearrange("p (t n) -> p t n", t=T)
        lat = reg_a[:, 0:T * LAT].rearrange("p (t n) -> p t n", t=T)
        kcat = reg_a[:, 1792:1792 + T * 192].rearrange("p (t n) -> p t n", t=T)
        qn = reg_a[:, 3328:3328 + T * QL].rearrange("p (t n) -> p t n", t=T)
        ropet = reg_t[:, 0:4 * T * 32].rearrange("p (j t n) -> p j t n", j=4, t=T)
        qt = [reg_a[:, 1024 * j:1024 * j + 1024].rearrange("p (h n) -> p h n", h=2) for j in range(3)]
        QT = reg_q[:, :].bitcast(F16).rearrange("p (r e j n) -> p r e j n", r=2, e=2, j=2)
        dT = reg_q[:, :].bitcast(F16).rearrange("p (f n) -> p f n", f=NF0)
        prob = reg_p[:, :].rearrange("p (j n) -> p j n", j=4)
        pT_h = reg_t[:, 0:1024].bitcast(F16).rearrange("p (j n) -> p j n", j=2)
        pT_l = reg_t[:, 1024:2048].bitcast(F16).rearrange("p (j n) -> p j n", j=2)
        o_sb = reg_o[:, :].rearrange("p (t n) -> p t n", t=T)
        spec = reg_p[:, :].rearrange("p (t n) -> p t n", t=T)
        sq = reg_a[:, 0:1024].rearrange("p (j n) -> p j n", j=2)
        sil = reg_a[:, 1024:2048].rearrange("p (j n) -> p j n", j=2)
        fz = reg_a[:, 2048:3072].rearrange("p (j n) -> p j n", j=2)
        prod = reg_o[:, 6144:6656].rearrange("p (j n) -> p j n", j=2)
        cross = reg_o[:, 7168:7616].rearrange("p (j i n) -> p j i n", j=2, i=2)
        fin = reg_t[:, 1024:2048].rearrange("p (j i n) -> p j i n", j=2, i=2)
        sT_h = reg_o[:, 6656:6912].bitcast(F16).rearrange("p (j k n) -> p j k n", j=2, k=2)
        sT_l = reg_o[:, 6912:7168].bitcast(F16).rearrange("p (j k n) -> p j k n", j=2, k=2)
        fT_h = reg_o[:, 0:3072].bitcast(F16).rearrange("p (f n) -> p f n", f=NF1)
        fT_l = reg_o[:, 3072:6144].bitcast(F16).rearrange("p (f n) -> p f n", f=NF1)

        N = {}

        def per_row(name, n):
            s = sem(name)
            N[id(s)] = n
            return s

        in_small = sem("in_small")
        in_gate = sem("in_gate")
        in_query = sem("in_query")
        in_rot = sem("in_rot")
        in_sum = sem("in_sum")
        in_up = sem("in_up")
        in_down = sem("in_down")
        in_spec = sem("in_spec")
        in_w0 = sem("in_w0")
        in_out = sem("in_out")
        w_const = sem("w_const")
        w_mm = sem("w_mm")
        w_cast = sem("w_cast")
        w_cp = sem("w_cp")
        w_hi = sem("w_hi")
        w_lo = sem("w_lo")
        w_qz = sem("w_qz")
        x_in = sem("x_in")
        xb_in = sem("xb_in")
        row_free = sem("row_free")
        stored = [sem("stored0"), sem("stored1")]
        ln = [{k: per_row(f"ln{i}_{k}", n) for k, n in
               (("stat", T), ("mv", T), ("sd", 2), ("rstd", 2), ("xn", T), ("tr", 4), ("hi", 4), ("lo", 4))}
              for i in range(2)]
        lat_mm = per_row("lat_mm", T)
        lat_ev = per_row("lat_ev", T)
        lat_sd = per_row("lat_sd", 1)
        lat_rr = per_row("lat_rr", 1)
        rope_m = per_row("rope_m", 1)
        kq_n = per_row("kq_n", 1)
        v_hi = per_row("v_hi", 1)
        v_lo = per_row("v_lo", 1)
        kq_tr = per_row("kq_tr", 6)
        kq_hi = per_row("kq_hi", 6)
        kq_lo = per_row("kq_lo", 6)
        q_mm = per_row("q_mm", 6 * NP)
        q_ev = per_row("q_ev", 6 * NP)
        q_add = per_row("q_add", 4 * NP)
        q_hi = per_row("q_hi", 4 * NP)
        q_lo = per_row("q_lo", 4 * NP)
        qk_done = per_row("qk_done", STEPS * NP)
        max_done = per_row("max_done", STEPS * NP)
        exp_done = per_row("exp_done", STEPS * NP)
        pt_ready = per_row("pt_ready", TASKS * NP)
        pt_hi = per_row("pt_hi", TASKS * NP)
        pt_lo = per_row("pt_lo", TASKS * NP)
        pv_done = per_row("pv_done", STEPS * NP)
        rinv_done = per_row("rinv_done", STEPS // 4 * NP)
        o_done = per_row("o_done", STEPS // 4 * NP)
        ot_tr = per_row("ot_tr", 2 * T)
        ot_hi = per_row("ot_hi", 2 * T)
        ot_lo = per_row("ot_lo", 2 * T)
        op_mm = per_row("op_mm", T)
        op_add = per_row("op_add", T)
        ff_mm = per_row("ff_mm", 2 * NF0)
        ff_act = per_row("ff_act", 2 * NF0)
        fe_mm = per_row("fe_mm", T)
        fe_ev = per_row("fe_ev", T)
        fe_add = per_row("fe_add", T)
        sp_mm = per_row("sp_mm", T)
        sp_cp = per_row("sp_cp", T)
        sp_sq = per_row("sp_sq", T)
        sp_ss = per_row("sp_ss", T)
        sp_sd = per_row("sp_sd", 1)
        sp_rr = per_row("sp_rr", 1)
        sp_n = per_row("sp_n", T)
        sp_run = per_row("sp_run", T - 2)
        g_mm = per_row("g_mm", 2 * NF1)
        u_mm = per_row("u_mm", 2 * NF1)
        g_act = per_row("g_act", 2 * NF1)
        fz_done = per_row("fz_done", 2 * NF1)
        f_hi = per_row("f_hi", 2 * NF1)
        f_lo = per_row("f_lo", 2 * NF1)
        cs_mm = per_row("cs_mm", T)
        cs_m = per_row("cs_m", T)
        cs_y = per_row("cs_y", 2 * T)
        yt_tr = per_row("yt_tr", T)
        yt_hi = per_row("yt_hi", T)
        yt_lo = per_row("yt_lo", T)
        l1_mm = per_row("l1_mm", T)
        l1_ev = per_row("l1_ev", T)

        def wait(eng, s, b, n):
            eng.wait_ge(s, b * N[id(s)] + n)

        def bank(i, n=HALF):
            return ps[:, i, 0:n]

        ORDER = [T - 1 - k // 2 if k % 2 == 0 else k // 2 for k in range(T)]

        def step_of(s):
            i = ORDER[s % T]
            return s % STEPS // T, i, 1 + (i >= T // 2)

        def o_slot(i):
            return {0: 0, 1: 1, T - 2: 2, T - 1: 3}.get(i, i - 2)

        def tasks_before(s):
            return 3 * (s // 2) + 2 * (s % 2)

        def first(dp):
            return isinstance(dp, int) and dp == 0

        def last(dp):
            return isinstance(dp, int) and dp == LAST

        Q_AT = {0: 0, 1: 1, 4: 2, 5: 3, 8: 4, 9: 5}
        QH_AT = {4: 0, 7: 1, 11: 2, 13: 3}
        AHEAD = {2: ([("turn", 0), ("turn", 1)], []), 3: ([("turn", 2), ("turn", 3)], []),
                 4: ([("latent", 0), ("latent", 1)], [("latent", 2), ("latent", 3)]),
                 5: ([("latent", 4), ("latent", 5)], [("latent", 6), ("latent", 7)]),
                 6: ([], [("turn_latent", 0), ("turn_latent", 1)]),
                 7: ([("turn_latent", 2), ("turn_latent", 3)], [("turn_latent", 4), ("turn_latent", 5)]),
                 8: ([("query", 0), ("query", 1)], [("query", 2), ("query", 3)]),
                 9: ([("query", 4), ("query", 5)], [])}
        CHUNK = 768
        ROUND = 8

        block = ctx.enter_context(nc.Block())

        @block.sync
        def _(sp):
            def load(done, *pairs):
                for dst, src in pairs:
                    sp.dma_start(dst, src).then_inc(done, 16)

            def flat_k(w, k):
                return w.rearrange("p (k n) -> p k n", k=k)

            def by_rows(w):
                return w.rearrange("(k p) n -> p k n", p=P)

            load(in_gate, (flat_k(s_gate, DC), by_rows(a["gate_w"])))
            load(in_small, (ident[:, :], a["consts"][0]), (s_mask, a["consts"][3]), (s_lat, a["w_lat"]),
                 (gq[:, :], a["g_q"]), (gkv[0:KL, :], a["g_kv"]), (gkv[KL:P, :], a["g_kv"]))
            sp.wait_ge(w_const, 1)
            load(in_small, (ge[0:KL, :], a["g_kv"]), (go[KL:P, :], a["g_kv"]))
            load(x_in, (xn, a["x"][0].rearrange("(t p) n -> p t n", p=P)))
            load(in_query, (s_uqT, a["w_uqT"]), (s_ukT, a["w_ukT"]),
                 (s_wq[:, :, 0, 64:128], a["w_pe"][:, :, 0, :]), (s_wq[:, :, 1, 0:64], a["w_pe"][:, :, 1, :]),
                 (s_wq[:, :, 2, 0:128], a["w_pe"][:, :, 2:4, :].rearrange("p r j n -> p r (j n)")))
            load(in_rot, (cos_t[:, :, :], a["cs"][0]), (sin_t[:, :, :], a["cs"][1]),
                 (st[:, :], a["rot"][2]), (ct_e[:, :], a["rot"][0]), (ct_o[:, :], a["rot"][1]))
            load(in_sum, (up_s[:, :], a["up_s"]), (down_s[:, :], a["down_s"]), (gate_s[:, :], a["gate_s"]),
                 (bias0[:, :], a["bias0"]), (bias1[:, :], a["bias1"]), (tri[:, :], a["consts"][1]), (ones[:, :], a["consts"][2]))
            sp.wait_ge(w_mm, 1)
            load(in_up, (flat_k(s_up, DC), by_rows(a["up_w"])))
            load(in_down, (flat_k(s_down, NF1), by_rows(a["down_w"])))
            load(in_spec, (s_q1, by_rows(a["W_q"])), (s_kv1, by_rows(a["W_kv"])), (s_ft, a["dftT"]),
                 (s_gt, a["idftT"]), (s_o1, by_rows(a["W_o1T"])))
            load(in_w0, (s_w0, by_rows(a["W0T"])), (s_w1, by_rows(a["W1T"])))
            load(in_out, (s_uvT, a["w_uvT"]), (s_wo, a["w_o"]))
            sp.wait_ge(w_mm, 3)
            sp.wait_ge(w_qz, 6 * ROUND)
            load(xb_in, (xb[:, :, :], a["x"][0].rearrange("(t p) n -> p t n", p=P)))

            def store(b):
                for t in range(T):
                    sp.wait_ge(row_free, b * T + t + 2)
                    sp.dma_start(out[b, t * P:(t + 1) * P, :], outb[:, t % 2, :]).then_inc(stored[t % 2], 16)
                for s in stored:
                    sp.wait_ge(s, b * (16 * T // 2) + 16 * T // 2)

            with sp.Fori(0, B - 1) as b:
                wait(sp, ln[1]["tr"], b, 4)
                load(x_in, (xn, a["x"][b + 1].rearrange("(t p) n -> p t n", p=P)))
                store(b)
                load(xb_in, (xb[:, :, :], a["x"][b + 1].rearrange("(t p) n -> p t n", p=P)))
            store(B - 1)

        @block.tensor
        def _(pe):
            def product3(o, l_h, l_l, r_h, r_l, start=True, stop=True):
                nc.tensor.matmul(o, l_h, r_h, start=start, stop=False)
                nc.tensor.matmul(o, l_h, r_l, start=False, stop=False)
                return nc.tensor.matmul(o, l_l, r_h, start=False, stop=stop)

            def fold_queries():
                pe.wait_ge(in_query, 16 * 5)
                for h in range(H):
                    mm = nc.tensor.matmul(ps[0:QL, h // 8, h % 8 * 64:h % 8 * 64 + 64], s_uqT[:, h, :], s_ukT[:, h, :],
                                          start=True, stop=True)
                mm.then_inc(w_mm, 1)

            def fold_spectra():
                pe.wait_ge(in_spec, 16 * 5)
                for k in range(DC):
                    for j, w in enumerate((s_q1, s_kv1)):
                        for c in range(DC):
                            mm = nc.tensor.matmul(ps[:, 4 + k, j * D:(j + 1) * D], w[:, c, k * P:(k + 1) * P], s_ft[:, c, :],
                                                  start=(c == 0), stop=(c == DC - 1))
                mm.then_inc(w_mm, 1)
                for k in range(DC):
                    for c in range(DC):
                        mm = nc.tensor.matmul(ps[:, 6, k * D:(k + 1) * D], s_gt[:, c, k * P:(k + 1) * P], s_o1[:, c, :],
                                              start=(c == 0), stop=(c == DC - 1))
                mm.then_inc(w_mm, 1)

            def fold_outputs():
                pe.wait_ge(in_out, 16 * 2)
                pe.wait_ge(w_cp, 2)
                wait(pe, q_ev, 0, 5)
                for g in range(NP // 2):
                    for r in range(2):
                        for e in range(2):
                            h = 4 * g + 2 * r + e
                            mm = nc.tensor.matmul(ps[64 * e:64 * e + 64, (7 + g) % 8, r * D:(r + 1) * D], s_uvT[:, h, :],
                                                  s_wo[:, h, :], start=True, stop=True)
                    mm.then_inc(w_mm, 1)

            def turn(b, L, g):
                wait(pe, L["xn"], b, 2 * g + 2)
                if g >= 2:
                    wait(pe, L["lo"], b, g - 1)
                for k in range(DC):
                    for j in range(2):
                        tr = nc.tensor.transpose(ps[:, 2 + g % 2, 256 * k + P * j:256 * k + P * j + P],
                                                 xn[:, 2 * g + j, k * P:(k + 1) * P], ident[:, :])
                tr.then_inc(L["tr"], 1)

            def latent(b, t):
                wait(pe, ln[0]["lo"], b, 4 if t < 2 else t // 2 + 1)
                if t >= 2:
                    wait(pe, lat_ev, b, t - 1)
                for k in range(DC):
                    tt = slice(t * P, (t + 1) * P)
                    mm = product3(bank(2 + t % 2, LAT), xT_h[:, k, tt], xT_l[:, k, tt], wlat_h[:, k, :],
                                  wlat_l[:, k, :], start=(k == 0), stop=(k == DC - 1))
                mm.then_inc(lat_mm, 1)

            def turn_latent(b, n):
                wait(pe, kq_n, b, 1)
                if n >= 2:
                    wait(pe, kq_lo, b, n - 1)
                half = n // 3
                src, lo, w = ((qn, 0, QL), (kcat, 0, P), (kcat, 64, P))[n % 3]
                for i in range(4):
                    tr = nc.tensor.transpose(ps[0:w, 2 + n % 2, P * i:P * i + P],
                                             src[:, 4 * half + i, lo:lo + w], ident[:, :])
                tr.then_inc(kq_tr, 1)

            def query(b, pair, j, where):
                half, r = j // 3, (2, 0, 1)[j % 3]
                hs = slice(HALF * half, HALF * half + HALF)
                product3(bank(where), wq_h[:, pair, r, :], wq_l[:, pair, r, :], qT_h[:, hs], qT_l[:, hs]).then_inc(q_mm, 1)

            def scores(b, dp, s):
                head, i, banks = step_of(s)
                r = s // STEPS
                if s % STEPS == 0:
                    wait(pe, q_lo, b, 8 * dp + 4 * r + 4)
                if not (first(dp) and s < 2):
                    wait(pe, exp_done, b, dp * 2 * STEPS + s - 1)
                l_h, l_l = (QT[:, r, head, x, i * P:(i + 1) * P] for x in range(2))
                for c in range(banks):
                    w = min((i + 1) * P - c * HALF, HALF)
                    o = ps[:, 2 * (s % 2) + c, 0:w]
                    k_h, k_l = kT_h[head][:, c * HALF:c * HALF + w], kT_l[head][:, c * HALF:c * HALF + w]
                    mm = product3(o, l_h, l_l, k_h, k_l, stop=(c < banks - 1))
                    if c == banks - 1:
                        mm = nc.tensor.matmul(o[:, w - P:w], identb[:, :], maskb[:, :], start=False, stop=True)
                mm.then_inc(qk_done, 1)

            def turn_probs(b, dp, s):
                head, i, banks = step_of(s)
                wait(pe, exp_done, b, dp * 2 * STEPS + s + 1)
                for c in range(banks):
                    n = tasks_before(s) + c
                    if not (first(dp) and n < 3):
                        wait(pe, pt_lo, b, dp * 2 * TASKS + n - 2)
                    for j in range(4 * c, min(4 * c + 4, i + 1)):
                        tr = nc.tensor.transpose(ps[:, 3 + n % 3, (j - 4 * c) * P:(j - 4 * c + 1) * P],
                                                 prob[:, s % 4, j * P:(j + 1) * P], ident[:, :])
                    tr.then_inc(pt_ready, 1)

            def values(b, dp, s):
                head, i, banks = step_of(s)
                wait(pe, pt_lo, b, dp * 2 * TASKS + tasks_before(s + 1))
                if s % 4 == 0 and not (first(dp) and s == 0):
                    wait(pe, o_done, b, dp * 2 * (STEPS // 4) + s // 4)
                slot = o_slot(i)
                o = ps[:, 6, slot * KL:(slot + 1) * KL]
                for j in range(i + 1):
                    mm = product3(o, pT_h[:, s % 2, j * P:(j + 1) * P], pT_l[:, s % 2, j * P:(j + 1) * P],
                                  v_h[:, j, :], v_l[:, j, :], start=(j == 0), stop=(j == i))
                mm.then_inc(pv_done, 1)

            def double_pair(b, dp):
                for s in range(2 * STEPS):
                    scores(b, dp, s)
                    if not (first(dp) and s < 3):
                        turn_probs(b, dp, s - 3)
                    j = Q_AT.get(s % STEPS)
                    r = s // STEPS
                    if j is not None and not (last(dp) and r == 1):
                        wait(pe, q_ev, b, dp * 12 + 6 * r + 6 + j)
                        query(b, 2 * dp + r + 1, j, 7)
                    if not (first(dp) and s < 4):
                        values(b, dp, s - 4)

            def turn_out(b, t):
                for c in range(2):
                    if t >= 2:
                        wait(pe, ot_lo, b, 2 * (t - 2) + c + 1)
                    for j in range(4):
                        tr = nc.tensor.transpose(ps[:, 2 * (t % 2) + c, j * P:(j + 1) * P],
                                                 o_sb[:, t, (4 * c + j) * P:(4 * c + j + 1) * P], ident[:, :])
                    tr.then_inc(ot_tr, 1)

            def project(b, t):
                wait(pe, ot_lo, b, 2 * t + 2)
                if t >= 2:
                    wait(pe, op_add, b, t - 1)
                for r in range(NP):
                    rs_ = slice(r * P, (r + 1) * P)
                    mm = product3(bank(6 + t % 2, D), pT_h[:, t % 2, rs_], pT_l[:, t % 2, rs_], wb_h[:, r, :],
                                  wb_l[:, r, :], start=(r == 0), stop=(r == NP - 1))
                mm.then_inc(op_mm, 1)

            def hidden(b, n):
                half, f = n // NF0, n % NF0
                if n >= 2:
                    wait(pe, ff_act, b, n - 1)
                for k in range(DC):
                    for w in (w0_h, w0_l):
                        mm = nc.tensor.matmul(bank(4 + n % 2), w[:, k, f * P:(f + 1) * P],
                                              xT_h[:, k, half * HALF:(half + 1) * HALF],
                                              start=(k == 0 and w is w0_h), stop=(k == DC - 1 and w is w0_l))
                mm.then_inc(ff_mm, 1)

            def feed_out(b, t):
                wait(pe, ff_act, b, NF0 * (t // 4 + 1))
                if t < 2:
                    wait(pe, ot_lo, b, 2 * T)
                else:
                    wait(pe, fe_ev, b, t - 1)
                for f in range(NF0):
                    for w in (w1_h, w1_l):
                        mm = nc.tensor.matmul(bank(t % 2, D), dT[:, f, t * P:(t + 1) * P], w[:, f, :],
                                              start=(f == 0 and w is w1_h), stop=(f == NF0 - 1 and w is w1_l))
                mm.then_inc(fe_mm, 1)

            def spectra(b, t):
                wait(pe, ln[1]["lo"], b, t // 2 + 1)
                if t >= 2:
                    wait(pe, sp_sq, b, t - 1)
                for k in range(DC):
                    tt = slice(t * P, (t + 1) * P)
                    mm = product3(bank(4 + t % 2), xT_h[:, k, tt], xT_l[:, k, tt], wsp_h[:, k, :], wsp_l[:, k, :],
                                  start=(k == 0), stop=(k == DC - 1))
                mm.then_inc(sp_mm, 1)

            def gate_up(b, n):
                half, f = n // NF1, n % NF1
                if n >= 2:
                    wait(pe, g_act, b, n - 1)
                    wait(pe, fz_done, b, n - 1)
                for w, at, done in ((gate_w, 0, g_mm), (up_w, 2, u_mm)):
                    for k in range(DC):
                        for x in (xT_h, xT_l):
                            mm = nc.tensor.matmul(bank(at + n % 2), w[:, k, f * P:(f + 1) * P],
                                                  x[:, k, half * HALF:(half + 1) * HALF],
                                                  start=(k == 0 and x is xT_h), stop=(k == DC - 1 and x is xT_l))
                    mm.then_inc(done, 1)

            def cumulate(b, t):
                wait(pe, sp_n, b, t + 1)
                if t >= 2:
                    wait(pe, sp_run, b, t - 1)
                    wait(pe, cs_m, b, t - 1)
                mm = nc.tensor.matmul(bank(4 + t % 2, D), tri[:, :], spec[:, t, D:2 * D], start=True, stop=(t == 0))
                if t:
                    before = spec[:, 0, D:2 * D] if t == 1 else run[:, t, :]
                    mm = nc.tensor.matmul(bank(4 + t % 2, D), ones[:, :], before, start=False, stop=True)
                mm.then_inc(cs_mm, 1)

            def turn_prod(b, t):
                wait(pe, cs_y, b, 2 * t + 2)
                if t >= 2:
                    wait(pe, yt_lo, b, t - 1)
                for k in range(DC):
                    tr = nc.tensor.transpose(ps[:, 6 + t % 2, k * P:(k + 1) * P], prod[:, t % 2, k * P:(k + 1) * P],
                                             ident[:, :])
                tr.then_inc(yt_tr, 1)

            def outputs(b, t):
                wait(pe, yt_lo, b, t + 1)
                wait(pe, f_lo, b, 2 * NF1)
                if t >= 2:
                    wait(pe, l1_ev, b, t - 1)
                for k in range(DC):
                    product3(bank(t % 2, D), sT_h[:, t % 2, k, :], sT_l[:, t % 2, k, :], wo1_h[:, k, :], wo1_l[:, k, :],
                             start=(k == 0), stop=(k == DC - 1))
                for f in range(NF1):
                    for x in (fT_h, fT_l):
                        mm = nc.tensor.matmul(ps[:, t % 2, D:2 * D], x[:, f, t * P:(t + 1) * P], down_w[:, f, :],
                                              start=(f == 0 and x is fT_h), stop=(f == NF1 - 1 and x is fT_l))
                mm.then_inc(l1_mm, 1)

            def first_query(b, j):
                wait(pe, kq_lo, b, min(j + 5, 6))
                if j >= 2:
                    wait(pe, q_ev, b, j - 1)
                query(b, 0, j, 2 + j % 2)

            def ahead(b, items):
                for kind, n in items:
                    if kind == "turn":
                        turn(b, ln[0], n)
                    elif kind == "latent":
                        latent(b, n)
                    elif kind == "turn_latent":
                        turn_latent(b, n)
                    else:
                        first_query(b, n)

            def row(b, following):
                double_pair(b, 0)
                with pe.Fori(1, LAST) as dp:
                    double_pair(b, dp)
                double_pair(b, LAST)
                for s in range(2 * STEPS, 2 * STEPS + 4):
                    if s < 2 * STEPS + 3:
                        turn_probs(b, LAST, s - 3)
                    values(b, LAST, s - 4)
                wait(pe, o_done, b, NP * STEPS // 4)
                turn_out(b, 0)
                for t in range(T):
                    hidden(b, 2 * t)
                    hidden(b, 2 * t + 1)
                    if t + 1 < T:
                        turn_out(b, t + 1)
                    project(b, t)
                for t in range(T - 2):
                    feed_out(b, t)
                turn(b, ln[1], 0)
                turn(b, ln[1], 1)
                feed_out(b, T - 2)
                feed_out(b, T - 1)
                for t in range(T):
                    spectra(b, t)
                    if t == 2 or t == 3:
                        turn(b, ln[1], t)
                for n in range(2 * NF1):
                    gate_up(b, n)
                for t in range(T + 2):
                    if t < T:
                        cumulate(b, t)
                    if 1 <= t <= T:
                        turn_prod(b, t - 1)
                    if t >= 2:
                        if following:
                            ahead(b + 1, AHEAD[t][0])
                        outputs(b, t - 2)
                        if following:
                            ahead(b + 1, AHEAD[t][1])
                if following:
                    wait(pe, l1_ev, b, T)
                    wait(pe, v_lo, b + 1, 1)
                    wait(pe, q_ev, b + 1, 6)

            for g in range(4):
                turn(0, ln[0], g)
            fold_queries()
            pe.wait_ge(w_lo, 1)
            for t in range(T):
                latent(0, t)
            for n in range(6):
                turn_latent(0, n)
            pe.wait_ge(w_lo, 2)
            for j in range(6):
                first_query(0, j)
            fold_spectra()
            fold_outputs()
            pe.wait_ge(w_lo, 9)
            wait(pe, v_lo, 0, 1)
            wait(pe, q_ev, 0, 6)
            with pe.Fori(0, B - 1) as b:
                row(b, True)
            row(B - 1, False)

        @block.scalar
        def _(act):
            def copy(o, i, **kw):
                return nc.scalar.activation(o, i, ACT.Copy, **kw)

            def fold_queries():
                act.wait_ge(in_query, 16 * 5)
                act.wait_ge(w_mm, 1)
                for e in range(2):
                    src = ps[0:QL, 0:2, :].rearrange("p c (r e n) -> p (c r) e n", e=2, n=64)[:, :, e, :]
                    copy(s_wq[:, :, e, 64 * e:64 * e + 64], src).then_inc(w_cp, 1)
                act.wait_ge(w_cp, 2)
                act.wait_ge(w_const, 3)
                copy(wq_h[:, :, :, :], s_wq, scale=gq[:, 0:1]).then_inc(w_hi, 1)

            def split_weights():
                act.wait_ge(w_mm, 2)
                copy(wsp_h[:, :, :], ps[:, 4:6, :]).then_inc(w_hi, 1)
                act.wait_ge(w_mm, 3)
                copy(wo1_h[:, :, :], ps[:, 6, :].rearrange("p (k n) -> p k n", k=DC), scale=WO1UP).then_inc(w_hi, 1)
                act.wait_ge(in_w0, 16 * 2)
                copy(w0_h[:, :, :], s_w0, scale=WUP).then_inc(w_hi, 1)
                copy(w1_h[:, :, :], s_w1, scale=WUP).then_inc(w_hi, 1)
                act.wait_ge(w_mm, 7)
                copy(wb_h[:, 0:2, :], ps[:, 7, :].rearrange("p (r n) -> p r n", r=2), scale=gkv[:, 0:1]).then_inc(w_hi, 1)
                copy(wb_h[:, 2:8, :], ps[:, 0:3, :].rearrange("p g (r n) -> p (g r) n", r=2), scale=gkv[:, 0:1]).then_inc(w_hi, 1)

            def roots(b, L, half):
                wait(act, L["mv"], b, 4 * half + 4)
                hs = slice(4 * half, 4 * half + 4)
                nc.scalar.activation(sd[:, hs], mv[:, hs, 1], ACT.Sqrt, bias=eps[:, 0:1]).then_inc(L["sd"], 1)

            def turned(b, L, g):
                wait(act, L["tr"], b, g + 1)
                copy(xT_h[:, :, 256 * g:256 * g + 256], ps[:, 2 + g % 2, :].rearrange("p (k n) -> p k n", k=DC)).then_inc(L["hi"], 1)

            def latent(b, t):
                wait(act, lat_mm, b, t + 1)
                src = bank(2 + t % 2)
                nc.scalar.activation(qn[:, t, :], src[:, 0:QL], ACT.Square, accum_out=ss[:, 0, t:t + 1])
                nc.scalar.activation(kcat[:, t, 0:KL], src[:, QL:QL + KL], ACT.Square, accum_out=ss[:, 1, t:t + 1])
                copy(lat[:, t, :], src[:, 0:LAT]).then_inc(lat_ev, 1)
                if t == T - 1:
                    wait(act, lat_ev, b, T)
                    nc.scalar.activation(rs[:, 0, :], ss[:, 0, :], ACT.Sqrt, bias=eps[:, 1:2], scale=1.0 / QL)
                    nc.scalar.activation(rs[:, 1, :], ss[:, 1, :], ACT.Sqrt, bias=eps[:, 1:2], scale=1.0 / KL).then_inc(lat_sd, 1)

            def turn_latent(b, n):
                if n == 0:
                    wait(act, kq_n, b, 1)
                    copy(v_h[:, :, :], kcat[:, :, 0:KL]).then_inc(v_hi, 1)
                wait(act, kq_tr, b, n + 1)
                hs = slice(HALF * (n // 3), HALF * (n // 3) + HALF)
                if n % 3 == 0:
                    copy(qT_h[:, hs], ps[0:QL, 2 + n % 2, :]).then_inc(kq_hi, 1)
                elif n % 3 == 1:
                    copy(kTe_h[:, hs], bank(2 + n % 2), scale=ge[:, 0:1]).then_inc(kq_hi, 1)
                else:
                    copy(kTo_h[:, hs], bank(2 + n % 2), scale=go[:, 0:1]).then_inc(kq_hi, 1)

            def query_hi(b, before, r, i):
                half, e = i // 2, i % 2
                wait(act, q_add, b, before + i + 1)
                copy(QT[:, r, e, 0, half * HALF:(half + 1) * HALF], qt[1 + e][:, half, :]).then_inc(q_hi, 1)

            def exponent(b, dp, s):
                head, i, banks = step_of(s)
                wait(act, max_done, b, dp * 2 * STEPS + s + 1)
                if not (first(dp) and s < 4):
                    wait(act, pt_ready, b, dp * 2 * TASKS + tasks_before(s - 3))
                if s % 4 == 0 and not (first(dp) and s < STEPS):
                    wait(act, o_done, b, dp * 2 * (STEPS // 4) + s // 4 - STEPS // 4 + 1)
                w = (i + 1) * P
                sum_slot = s % STEPS // 4 * 4 + o_slot(i)
                nc.scalar.activation(prob[:, s % 4, 0:w], ps[:, 2 * (s % 2):2 * (s % 2) + banks, :].rearrange("p c n -> p (c n)")[:, 0:w],
                                     ACT.Exp, bias=negmax[:, s % STEPS:s % STEPS + 1],
                                     accum_out=rowsum[:, sum_slot:sum_slot + 1]).then_inc(exp_done, 1)

            def probs_hi(b, dp, s):
                head, i, banks = step_of(s)
                if not (first(dp) and s < 2):
                    wait(act, pv_done, b, dp * 2 * STEPS + s - 1)
                for c in range(banks):
                    n = tasks_before(s) + c
                    w = min((i + 1) * P - c * HALF, HALF)
                    wait(act, pt_ready, b, dp * 2 * TASKS + n + 1)
                    copy(pT_h[:, s % 2, c * HALF:c * HALF + w], bank(3 + n % 3, w)).then_inc(pt_hi, 1)

            def double_pair(b, dp):
                for s in range(2 * STEPS):
                    if not (first(dp) and s < 1):
                        exponent(b, dp, s - 1)
                    if not (first(dp) and s < 3):
                        probs_hi(b, dp, s - 3)
                    i, r = QH_AT.get(s % STEPS), s // STEPS
                    if i is not None and not (last(dp) and r == 1):
                        query_hi(b, dp * 8 + 4 * r + 4, 1 - r, i)
            def out_hi(b, t):
                for c in range(2):
                    if t >= 2 and c == 0:
                        wait(act, op_mm, b, t - 1)
                    wait(act, ot_tr, b, 2 * t + c + 1)
                    copy(pT_h[:, t % 2, c * HALF:(c + 1) * HALF], bank(2 * (t % 2) + c)).then_inc(ot_hi, 1)

            def gelu(b, n):
                half, f = n // NF0, n % NF0
                wait(act, ff_mm, b, n + 1)
                nc.scalar.activation(dT[:, f, half * HALF:(half + 1) * HALF], bank(4 + n % 2), ACT.Gelu,
                                     bias=bias0[:, f:f + 1], scale=1 / WUP).then_inc(ff_act, 1)

            def ahead(b, items):
                for kind, n in items:
                    if kind == "turn":
                        turned(b, ln[0], n)
                    elif kind == "latent":
                        latent(b, n)
                    elif kind == "turn_latent":
                        turn_latent(b, n)

            def row(b, following):
                double_pair(b, 0)
                with act.Fori(1, LAST) as dp:
                    double_pair(b, dp)
                double_pair(b, LAST)
                exponent(b, LAST, 2 * STEPS - 1)
                probs_hi(b, LAST, 2 * STEPS - 3)
                probs_hi(b, LAST, 2 * STEPS - 2)
                probs_hi(b, LAST, 2 * STEPS - 1)
                wait(act, pv_done, b, NP * STEPS)
                out_hi(b, 0)
                for t in range(T):
                    gelu(b, 2 * t)
                    gelu(b, 2 * t + 1)
                    if t + 1 < T:
                        out_hi(b, t + 1)
                roots(b, ln[1], 0)
                turned(b, ln[1], 0)
                turned(b, ln[1], 1)
                for t in range(T):
                    if t == 1:
                        roots(b, ln[1], 1)
                    if t == 3 or t == 4:
                        turned(b, ln[1], t - 1)
                    wait(act, sp_mm, b, t + 1)
                    copy(spec[:, t, :], bank(4 + t % 2)).then_inc(sp_cp, 1)
                    if t >= 2:
                        wait(act, sp_ss, b, t - 1)
                    nc.scalar.activation(sq[:, t % 2, :], bank(4 + t % 2), ACT.Square).then_inc(sp_sq, 1)
                wait(act, sp_ss, b, T)
                nc.scalar.activation(rs2[:, :, :], ss2[:, :, :], ACT.Sqrt).then_inc(sp_sd, 1)
                for n in range(2 * NF1 + 1):
                    if n < 2 * NF1:
                        f = n % NF1
                        wait(act, g_mm, b, n + 1)
                        if n >= 2:
                            wait(act, fz_done, b, n - 1)
                        nc.scalar.activation(sil[:, n % 2, :], bank(n % 2), ACT.Silu, scale=gate_s[:, f:f + 1]).then_inc(g_act, 1)
                    if n:
                        half, f = (n - 1) // NF1, (n - 1) % NF1
                        wait(act, fz_done, b, n)
                        copy(fT_h[:, f, half * HALF:(half + 1) * HALF], fz[:, (n - 1) % 2, :]).then_inc(f_hi, 1)
                if following:
                    for half in range(2):
                        roots(b + 1, ln[0], half)
                for t in range(1, T + 2):
                    if t <= T:
                        wait(act, yt_tr, b, t)
                        if t >= 3:
                            wait(act, l1_mm, b, t - 2)
                        copy(sT_h[:, (t - 1) % 2, :, :],
                             ps[:, 6 + (t - 1) % 2, 0:D].rearrange("p (k n) -> p k n", k=DC)).then_inc(yt_hi, 1)
                    if following and t in AHEAD:
                        ahead(b + 1, AHEAD[t][0] + AHEAD[t][1])
                if following:
                    for i in range(4):
                        query_hi(b + 1, 0, 0, i)

            act.wait_ge(in_small, 16 * 8)
            copy(wlat_h[:, :, :], s_lat, scale=WUP).then_inc(w_hi, 1)
            for half in range(2):
                roots(0, ln[0], half)
            for g in range(4):
                turned(0, ln[0], g)
            fold_queries()
            for t in range(T):
                latent(0, t)
            for n in range(6):
                turn_latent(0, n)
            for i in range(4):
                query_hi(0, 0, 0, i)
            split_weights()
            with act.Fori(0, B - 1) as b:
                row(b, True)
            row(B - 1, False)

        @block.vector
        def _(dve):
            tt, ts, stt = nc.vector.tensor_tensor, nc.vector.tensor_scalar, nc.vector.scalar_tensor_tensor

            nc.vector.memset(ge[:, :], 1.0)
            nc.vector.memset(go[:, :], 1.0).then_inc(w_const, 1)
            nc.vector.memset(eps[:, 0:1], LN_EPS)
            nc.vector.memset(eps[:, 1:2], RMS_EPS * WUP * WUP)
            dve.wait_ge(in_small, 16 * 8)
            ts(gq[:, :], gq[:, :], WUP, None, ALU.mult).then_inc(w_const, 1)
            ts(gkv[:, :], gkv[:, :], WUP, None, ALU.mult).then_inc(w_const, 1)
            nc.vector.tensor_copy(identb[:, :], ident[:, :]).then_inc(w_cast, 1)
            nc.vector.tensor_copy(maskb[:, :], s_mask).then_inc(w_cast, 1)

            def round_float8(w, o, m, before):
                n = before * ROUND

                def done(ins):
                    nonlocal n
                    n += 1
                    ins.then_inc(w_qz, 1)
                    dve.wait_ge(w_qz, n)

                o = o[:, :, :].rearrange("p k n -> p (k n)")
                for c in range(2):
                    cs = slice(c * CHUNK, (c + 1) * CHUNK)
                    w_ = w[:, cs]
                    done(ts(m.bitcast(U32), w_.bitcast(U32), 0x7F800000, None, ALU.bitwise_and))
                    done(ts(m, m, 2.0 ** -6, 1.5 * 2.0 ** 20, ALU.max, ALU.mult))
                    done(tt(w_, w_, m, ALU.add))
                    done(tt(w_, w_, m, ALU.subtract))
                    done(tt(m, w_, w_, ALU.mult))
                    done(ts(m, m, 448.0 ** 2, 3e38, ALU.is_gt, ALU.mult))
                    done(ts(m, m, 3e38, 0.0, ALU.mult, ALU.mult))
                    done(tt(o[:, cs], w_, m, ALU.add))

            def split_weights(before, *parts):
                for n, (o, src, scale, h) in enumerate(parts):
                    dve.wait_ge(w_hi, before + n + 1)
                    stt(out=o, in0=src, scalar=scale, in1=h, op0=ALU.mult, op1=ALU.subtract).then_inc(w_lo, 1)

            def stats(b, L, t):
                src = xn if L is ln[0] else xb
                nc.vector.bn_stats(bnst[:, t, :], src[:, t, :]).then_inc(L["stat"], 1)

            def means(b, L, t):
                wait(dve, L["stat"], b, t + 1)
                nc.vector.memset(tick[:, t:t + 1], 0.0)
                nc.vector.bn_aggr(mv[:, t, :], bnst[:, t, :]).then_inc(L["mv"], 1)

            def normalise(b, L, half):
                src = xn if L is ln[0] else xb
                wait(dve, L["sd"], b, half + 1)
                hs = slice(4 * half, 4 * half + 4)
                nc.vector.reciprocal(rstd[:, hs], sd[:, hs]).then_inc(L["rstd"], 1)
                wait(dve, L["rstd"], b, half + 1)
                for t in range(4 * half, 4 * half + 4):
                    ts(xn[:, t, :], src[:, t, :], mv[:, t, 0:1], rstd[:, t:t + 1], ALU.subtract, ALU.mult).then_inc(L["xn"], 1)

            def turned_lo(b, L, g):
                wait(dve, L["hi"], b, g + 1)
                gs_ = slice(256 * g, 256 * g + 256)
                tt(xT_l[:, :, gs_], ps[:, 2 + g % 2, :].rearrange("p (k n) -> p k n", k=DC), xT_h[:, :, gs_],
                   ALU.subtract).then_inc(L["lo"], 1)

            def normal_latents(b):
                wait(dve, lat_sd, b, 1)
                nc.vector.reciprocal(rr[:, :, :], rs[:, :, :]).then_inc(lat_rr, 1)
                x1, x2 = lat[:, :, QL + KL:QL + KL + 32], lat[:, :, QL + KL + 32:LAT]
                tt(ropet[:, 0, :, :], x1, cos_t[:, :, :], ALU.mult)
                tt(ropet[:, 1, :, :], x2, sin_t[:, :, :], ALU.mult)
                tt(ropet[:, 2, :, :], x1, sin_t[:, :, :], ALU.mult)
                tt(ropet[:, 3, :, :], x2, cos_t[:, :, :], ALU.mult).then_inc(rope_m, 1)
                wait(dve, lat_rr, b, 1)
                tt(qn, lat[:, :, 0:QL], rr[:, 0, :].unsqueeze(2).broadcast_to([P, T, QL]), ALU.mult)
                kv_r = rr[:, 1, :].unsqueeze(2).broadcast_to([P, T, KL])
                tt(kcat[:, :, 0:KL], lat[:, :, QL:QL + KL], kv_r, ALU.mult)
                tt(kcat[:, :, P:P + KL], lat[:, :, QL:QL + KL], kv_r, ALU.mult)
                wait(dve, rope_m, b, 1)
                tt(kcat[:, :, KL:KL + 32], ropet[:, 0, :, :], ropet[:, 1, :, :], ALU.subtract)
                tt(kcat[:, :, KL + 32:P], ropet[:, 2, :, :], ropet[:, 3, :, :], ALU.add).then_inc(kq_n, 1)

            def turn_latent(b, j):
                if j == 0:
                    wait(dve, v_hi, b, 1)
                    tt(v_l[:, :, :], kcat[:, :, 0:KL], v_h[:, :, :], ALU.subtract).then_inc(v_lo, 1)
                wait(dve, kq_hi, b, j + 1)
                hs = slice(HALF * (j // 3), HALF * (j // 3) + HALF)
                if j % 3 == 0:
                    tt(qT_l[:, hs], ps[0:QL, 2 + j % 2, :], qT_h[:, hs], ALU.subtract).then_inc(kq_lo, 1)
                else:
                    g, h_, l_ = ((ge, kTe_h, kTe_l), (go, kTo_h, kTo_l))[j % 3 - 1]
                    stt(out=l_[:, hs], in0=bank(2 + j % 2), scalar=g[:, 0:1], in1=h_[:, hs], op0=ALU.mult,
                        op1=ALU.subtract).then_inc(kq_lo, 1)

            def query_ev(b, before, j, where, lo_before=None):
                half = j // 3
                wait(dve, q_mm, b, before + j + 1)
                if j % 3 == 0 and lo_before is not None:
                    wait(dve, q_lo, b, lo_before + 2 * half + 2)
                table = (st, ct_e, ct_o)[j % 3]
                tt(qt[j % 3][:, half, :], bank(where), table[:, half * HALF:(half + 1) * HALF], ALU.mult).then_inc(q_ev, 1)

            def maxima(b, dp, s):
                head, i, banks = step_of(s)
                wait(dve, qk_done, b, dp * 2 * STEPS + s + 1)
                w = (i + 1) * P
                nc.vector.tensor_reduce(negmax[:, s % STEPS:s % STEPS + 1],
                                        ps[:, 2 * (s % 2):2 * (s % 2) + banks, :].rearrange("p c n -> p (c n)")[:, 0:w],
                                        AX_X, ALU.max, negate=True).then_inc(max_done, 1)

            def probs_lo(b, dp, s):
                head, i, banks = step_of(s)
                for c in range(banks):
                    n = tasks_before(s) + c
                    w = min((i + 1) * P - c * HALF, HALF)
                    wait(dve, pt_hi, b, dp * 2 * TASKS + n + 1)
                    cs = slice(c * HALF, c * HALF + w)
                    tt(pT_l[:, s % 2, cs], bank(3 + n % 3, w), pT_h[:, s % 2, cs], ALU.subtract).then_inc(pt_lo, 1)

            def sums(b, dp, s):
                wait(dve, exp_done, b, dp * 2 * STEPS + s + 1)
                nc.vector.reciprocal(rinv[:, s // 4 % 2, :], rowsum[:, s % STEPS - 3:s % STEPS + 1]).then_inc(rinv_done, 1)

            def out_ev(b, dp, s):
                head, i, banks = step_of(s)
                r = s // STEPS
                wait(dve, rinv_done, b, dp * 2 * (STEPS // 4) + s // 4 + 1)
                wait(dve, pv_done, b, dp * 2 * STEPS + s + 1)
                col = (2 * dp + r) * P + KL * head
                near = slice(1, 3) if 2 <= i < T - 2 else slice(0, 4, 3)
                tt(o_sb.rearrange("p (g v) n -> p g v n", v=2)[:, near, :, bass.ds(col, KL)],
                   bank(6, 4 * KL).rearrange("p (g v n) -> p g v n", g=2, v=2),
                   rinv[:, s // 4 % 2, :].rearrange("p (g v) -> p g v", v=2).unsqueeze(3).broadcast_to([P, 2, 2, KL]),
                   ALU.mult).then_inc(o_done, 1)

            def double_pair(b, dp):
                for s in range(2 * STEPS):
                    maxima(b, dp, s)
                    if s % 4 == 3 and not (first(dp) and s < 4):
                        out_ev(b, dp, s - 4)
                    if first(dp) and s == 3:
                        dve.wait_ge(row_free, b * T + 1)
                    if not (first(dp) and s < 3):
                        probs_lo(b, dp, s - 3)
                    if s % 4 == 2 and not (first(dp) and s < 6):
                        sums(b, dp, s - 3)
                    j, r = Q_AT.get(s % STEPS), s // STEPS
                    if j is not None and not (last(dp) and r == 1):
                        query_ev(b, dp * 12 + 6 * r + 6, j, 7, dp * 8 + 4 * r)
            def out_lo(b, t):
                for c in range(2):
                    wait(dve, ot_hi, b, 2 * t + c + 1)
                    cs = slice(c * HALF, (c + 1) * HALF)
                    tt(pT_l[:, t % 2, cs], bank(2 * (t % 2) + c), pT_h[:, t % 2, cs], ALU.subtract).then_inc(ot_lo, 1)

            def ahead(b, items):
                for kind, n in items:
                    if kind == "turn":
                        turned_lo(b, ln[0], n)
                    elif kind == "turn_latent":
                        if n == 0:
                            normal_latents(b)
                        turn_latent(b, n)
                    elif kind == "query":
                        query_ev(b, 0, n, 2 + n % 2)

            def row(b, following):
                double_pair(b, 0)
                with dve.Fori(1, LAST) as dp:
                    double_pair(b, dp)
                double_pair(b, LAST)
                probs_lo(b, LAST, 2 * STEPS - 3)
                probs_lo(b, LAST, 2 * STEPS - 2)
                probs_lo(b, LAST, 2 * STEPS - 1)
                sums(b, LAST, 2 * STEPS - 1)
                out_ev(b, LAST, 2 * STEPS - 1)
                out_lo(b, 0)
                dve.wait_ge(xb_in, b * 16 + 16)
                for t in range(T):
                    if t + 1 < T:
                        out_lo(b, t + 1)
                    wait(dve, op_mm, b, t + 1)
                    stt(out=xb[:, t, :], in0=bank(6 + t % 2, D), scalar=1 / WUP, in1=xb[:, t, :], op0=ALU.mult,
                        op1=ALU.add).then_inc(op_add, 1)
                for t in range(T):
                    wait(dve, fe_mm, b, t + 1)
                    if t >= 2:
                        wait(dve, fe_add, b, t - 1)
                    stt(out=e16[:, t % 2, :], in0=bank(t % 2, D), scalar=1 / WUP, in1=bias1[:, :], op0=ALU.mult,
                        op1=ALU.add).then_inc(fe_ev, 1)
                    wait(dve, fe_ev, b, t + 1)
                    tt(xb[:, t, :], xb[:, t, :], e16[:, t % 2, :], ALU.add).then_inc(fe_add, 1)
                    if t == 4:
                        normalise(b, ln[1], 0)
                    wait(dve, fe_add, b, t + 1)
                    stats(b, ln[1], t)
                    means(b, ln[1], t)
                    if t == 5:
                        turned_lo(b, ln[1], 0)
                        turned_lo(b, ln[1], 1)
                normalise(b, ln[1], 1)
                for t in range(T):
                    if t == 2 or t == 3:
                        turned_lo(b, ln[1], t)
                    wait(dve, sp_sq, b, t + 1)
                    nc.vector.tensor_reduce(ss2[:, t, :].rearrange("p (j h) -> p j h", j=2),
                                            sq[:, t % 2, :].rearrange("p (j c h) -> p j h c", j=2, h=16),
                                            AX_X, ALU.add).then_inc(sp_ss, 1)
                wait(dve, sp_sd, b, 1)
                nc.vector.reciprocal(rr2[:, :, :], rs2[:, :, :]).then_inc(sp_rr, 1)
                for n in range(2 * NF1 + 1):
                    if n < 2 * NF1:
                        f = n % NF1
                        wait(dve, g_act, b, n + 1)
                        wait(dve, u_mm, b, n + 1)
                        if n >= 2:
                            wait(dve, f_lo, b, n - 1)
                        stt(out=fz[:, n % 2, :], in0=bank(2 + n % 2), scalar=up_s[:, f:f + 1], in1=sil[:, n % 2, :],
                            op0=ALU.mult, op1=ALU.mult).then_inc(fz_done, 1)
                    if n:
                        half, f = (n - 1) // NF1, (n - 1) % NF1
                        wait(dve, f_hi, b, n)
                        hs = slice(half * HALF, (half + 1) * HALF)
                        tt(fT_l[:, f, hs], fz[:, (n - 1) % 2, :], fT_h[:, f, hs], ALU.subtract).then_inc(f_lo, 1)
                    if following and n >= 2 * NF1 - T:
                        t = n - (2 * NF1 - T)
                        if t == 0:
                            dve.wait_ge(x_in, (b + 1) * 16 + 16)
                        if t < T:
                            stats(b + 1, ln[0], t)
                        if t >= 1:
                            means(b + 1, ln[0], t - 1)
                for t in range(T + 2):
                    if t < T:
                        wait(dve, cs_mm, b, t + 1)
                        if t >= 2:
                            wait(dve, yt_tr, b, t - 1)
                            wait(dve, cs_y, b, 2 * t - 2)
                        c_ps = bank(4 + t % 2, D)
                        tt(prod[:, t % 2, :], spec[:, t, 0:D], c_ps, ALU.mult)
                        tt(cross[:, t % 2, 0, :], spec[:, t, 32:144], c_ps[:, 144:256], ALU.mult)
                        tt(cross[:, t % 2, 1, :], spec[:, t, 144:256], c_ps[:, 32:144], ALU.mult).then_inc(cs_m, 1)
                    if 1 <= t <= T:
                        wait(dve, yt_hi, b, t)
                        tt(sT_l[:, (t - 1) % 2, :, :], ps[:, 6 + (t - 1) % 2, 0:D].rearrange("p (k n) -> p k n", k=DC),
                           sT_h[:, (t - 1) % 2, :, :], ALU.subtract).then_inc(yt_lo, 1)
                    if following and t < 2:
                        normalise(b + 1, ln[0], t)
                    if following and t in AHEAD:
                        ahead(b + 1, AHEAD[t][0])
                    if t >= 2:
                        u = t - 2
                        wait(dve, l1_mm, b, u + 1)
                        if u >= 2:
                            dve.wait_ge(row_free, b * T + u)
                        tt(fin[:, u % 2, 0, :], ps[:, u % 2, D:2 * D], down_s[:, :], ALU.mult)
                        stt(out=fin[:, u % 2, 1, :], in0=bank(u % 2, D), scalar=1 / WO1UP, in1=xb[:, u, :], op0=ALU.mult,
                            op1=ALU.add).then_inc(l1_ev, 1)
                    if following and t in AHEAD:
                        ahead(b + 1, AHEAD[t][1])

            dve.wait_ge(in_gate, 16)
            round_float8(s_gate, gate_w, reg_a[:, 1536:1536 + CHUNK], 0)
            dve.wait_ge(x_in, 16)
            for t in range(T):
                stats(0, ln[0], t)
            for t in range(T):
                means(0, ln[0], t)
            for half in range(2):
                normalise(0, ln[0], half)
            split_weights(0, (wlat_l[:, :, :], s_lat, WUP, wlat_h[:, :, :]))
            for g in range(4):
                turned_lo(0, ln[0], g)
            split_weights(1, (wq_l[:, :, :, :].rearrange("p r j n -> p (r j n)"), s_wq.rearrange("p r j n -> p (r j n)"),
                              gq[:, 0:1], wq_h[:, :, :, :].rearrange("p r j n -> p (r j n)")))
            dve.wait_ge(in_up, 16)
            round_float8(s_up, up_w, reg_p[:, 1536:1536 + CHUNK], 2)
            dve.wait_ge(in_rot, 16 * 5)
            normal_latents(0)
            for n in range(6):
                turn_latent(0, n)
            for j in range(6):
                query_ev(0, 0, j, 2 + j % 2)
            dve.wait_ge(in_down, 16)
            round_float8(s_down, down_w, reg_p[:, 1536:1536 + CHUNK], 4)
            dve.wait_ge(in_sum, 16 * 7)
            ts(up_s[:, :], up_s[:, :], FDOWN, None, ALU.mult).then_inc(w_cast, 1)
            ts(down_s[:, :], down_s[:, :], 1 / FDOWN, None, ALU.mult).then_inc(w_cast, 1)
            split_weights(2, (wsp_l[:, :, :], ps[:, 4:6, :], 1.0, wsp_h[:, :, :]),
                          (wo1_l[:, :, :], ps[:, 6, :].rearrange("p (k n) -> p k n", k=DC), WO1UP, wo1_h[:, :, :]),
                          (w0_l[:, :, :], s_w0, WUP, w0_h[:, :, :]), (w1_l[:, :, :], s_w1, WUP, w1_h[:, :, :]),
                          (wb_l[:, 0:2, :], ps[:, 7, :].rearrange("p (r n) -> p r n", r=2), gkv[:, 0:1], wb_h[:, 0:2, :]),
                          (wb_l[:, 2:8, :], ps[:, 0:3, :].rearrange("p g (r n) -> p (g r) n", r=2), gkv[:, 0:1],
                           wb_h[:, 2:8, :]))
            dve.wait_ge(w_lo, 8)
            nc.vector.memset(eps[:, 2:3], 0.0).then_inc(w_lo, 1)
            dve.wait_ge(w_lo, 9)
            nc.vector.memset(tick[:, 0:1], 0.0).then_inc(row_free, 1)
            with dve.Fori(0, B - 1) as b:
                row(b, True)
            row(B - 1, False)

        @block.gpsimd
        def _(pool):
            tt = nc.gpsimd.tensor_tensor

            def pair_queries(b, pair, r, half, fresh=False):
                if not fresh:
                    wait(pool, q_lo, b, pair * 4 + 2 * half)
                for e in range(2):
                    wait(pool, q_ev, b, pair * 6 + 3 * half + 2 + e)
                    if e:
                        wait(pool, q_add, b, pair * 4 + 2 * half + 1)
                    rows = slice(64, 128) if e == 0 else slice(0, 64)
                    tt(qt[1 + e][rows, half, :], qt[1 + e][rows, half, :], qt[0][rows, half, :],
                       ALU.add).then_inc(q_add, 1)
                wait(pool, q_add, b, pair * 4 + 2 * half + 2)
                for e in range(2):
                    wait(pool, q_hi, b, pair * 4 + 2 * half + e + 1)
                    hs = slice(half * HALF, (half + 1) * HALF)
                    tt(QT[:, r, e, 1, hs], qt[1 + e][:, half, :], QT[:, r, e, 0, hs], ALU.subtract).then_inc(q_lo, 1)

            def row(b, following):
                with pool.Fori(0, LAST) as dp:
                    for k in range(2):
                        for half in range(2):
                            pair_queries(b, 2 * dp + 1 + k, 1 - k, half)
                for half in range(2):
                    pair_queries(b, NP - 1, 1, half)
                wait(pool, sp_rr, b, 1)
                for t in range(T):
                    v = spec[:, t, :].rearrange("p (j c h) -> p j c h", j=2, h=16)
                    for j in range(2):
                        ins = tt(v[:, j], v[:, j], rr2[:, t, 16 * j:16 * j + 16].unsqueeze(1).broadcast_to([P, 16, 16]), ALU.mult)
                    ins.then_inc(sp_n, 1)
                    wait(pool, sp_n, b, t + 1)
                    if 1 <= t < T - 1:
                        before = spec[:, 0, D:2 * D] if t == 1 else run[:, t, :]
                        if t >= 2:
                            wait(pool, sp_run, b, t - 1)
                        tt(run[:, t + 1, :], before, spec[:, t, D:2 * D], ALU.add).then_inc(sp_run, 1)
                for t in range(T + 2):
                    if t < T:
                        wait(pool, cs_m, b, t + 1)
                        p_ = prod[:, t % 2, :]
                        tt(p_[:, 32:144], p_[:, 32:144], p_[:, 144:256], ALU.subtract).then_inc(cs_y, 1)
                        wait(pool, cs_y, b, 2 * t + 1)
                        tt(p_[:, 144:256], cross[:, t % 2, 0, :], cross[:, t % 2, 1, :], ALU.add).then_inc(cs_y, 1)
                    if t >= 2:
                        u = t - 2
                        wait(pool, l1_ev, b, u + 1)
                        if u >= 2:
                            pool.wait_ge(stored[u % 2], b * (16 * T // 2) + 16 * (u // 2))
                        tt(outb[:, u % 2, :], fin[:, u % 2, 0, :], fin[:, u % 2, 1, :], ALU.add).then_inc(row_free, 1)
                    if following and t == T:
                        pool.wait_ge(row_free, b * T + T)
                        pair_queries(b + 1, 0, 0, 0)
                if following:
                    pool.wait_ge(row_free, b * T + T + 1)
                    pair_queries(b + 1, 0, 0, 1)

            for half in range(2):
                pair_queries(0, 0, 0, half, fresh=(half == 0))
            with pool.Fori(0, B - 1) as b:
                row(b, True)
            row(B - 1, False)


_OUT = ((4, 1024, 256), "float32")


def _layout(i):
    import numpy as np

    H, NOPE, ROPE, VD, S, HD = 16, 128, 64, 128, 1024, 16
    c = np.ascontiguousarray
    w_uq = np.asarray(i["L0_attn_w_uq"]).reshape(96, H, NOPE + ROPE)
    pe = w_uq[:, :, NOPE:]
    swapped = np.concatenate([pe[:, :, 32:], pe[:, :, :32]], axis=2)
    w_pe = np.stack([pe[:, 0::2], pe[:, 1::2], swapped[:, 1::2], swapped[:, 0::2]], axis=2)
    lat = np.concatenate([i["L0_attn_w_dq"], i["L0_attn_w_dkv"], i["L0_attn_w_kr"]], axis=1)
    d = {
        "x": i["L0_attn_x"],
        "w_uqT": w_uq[:, :, :NOPE].transpose(2, 1, 0),
        "w_ukT": np.asarray(i["L0_attn_w_uk"]).reshape(64, H, NOPE).transpose(2, 1, 0),
        "w_uvT": np.asarray(i["L0_attn_w_uv"]).reshape(64, H, VD).transpose(2, 1, 0),
        "w_pe": w_pe,
        "w_o": np.asarray(i["L0_attn_w_o"]).reshape(H, VD, 256).transpose(1, 0, 2),
        "w_lat": lat.reshape(2, 128, 224).transpose(1, 0, 2),
        "g_q": np.asarray(i["L0_attn_g_q"]).reshape(96, 1), "g_kv": np.asarray(i["L0_attn_g_kv"]).reshape(64, 1),
        "W0T": np.asarray(i["L0_ffn_W0"]).T, "W1T": np.asarray(i["L0_ffn_W1"]).T,
        "bias0": np.asarray(i["L0_ffn_bias0"]).reshape(8, 128).T,
        "bias1": np.tile(np.asarray(i["L0_ffn_bias1"]).reshape(1, 256), (128, 1)),
        "W_q": i["L1_attn_W_q"], "W_kv": i["L1_attn_W_kv"], "W_o1T": np.asarray(i["L1_attn_W_o"]).T,
        "gate_w": i["L1_ffn_gate_w"], "up_w": i["L1_ffn_up_w"], "down_w": i["L1_ffn_down_w"],
        "gate_s": np.asarray(i["L1_ffn_gate_scale"]).reshape(6, 128).T,
        "up_s": np.asarray(i["L1_ffn_up_scale"]).reshape(6, 128).T,
        "down_s": np.tile(np.asarray(i["L1_ffn_down_scale"]).reshape(1, 256), (128, 1)),
    }
    inv_freq = (np.float32(1.0) / np.float32(10000.0) ** (np.arange(0, ROPE, 2, dtype=np.float32) / np.float32(ROPE))).astype(np.float32)
    freqs = np.outer(np.arange(S, dtype=np.float32), inv_freq).astype(np.float32).astype(np.float64)
    cos, sin = np.cos(freqs), np.sin(freqs)
    sc = (NOPE + ROPE) ** -0.5 / WUP
    pe_c = np.concatenate([cos, cos], axis=1).T * sc
    pe_s = np.concatenate([-sin, sin], axis=1).T * sc
    flat = np.full_like(pe_c, sc)
    d["rot"] = np.stack([np.concatenate([flat, pe_c]), np.concatenate([pe_c, flat]), np.concatenate([pe_s, pe_s])]).astype(np.float32)
    d["cs"] = np.stack([x.reshape(8, 128, 32).transpose(1, 0, 2) / WUP for x in (cos, sin)]).astype(np.float32)
    j = np.arange(HD)
    rows, back = [], []
    for k in (0, 8):
        rows.append(np.cos(2 * np.pi * j * k / HD) / 4)
        back.append(np.cos(2 * np.pi * j * k / HD) / HD)
    for k in range(1, 8):
        rows.append(np.cos(2 * np.pi * j * k / HD) * 2 ** 0.5 / 4)
        back.append(np.cos(2 * np.pi * j * k / HD) / HD)
    for k in range(1, 8):
        rows.append(-np.sin(2 * np.pi * j * k / HD) * 2 ** 0.5 / 4)
        back.append(-np.sin(2 * np.pi * j * k / HD) / HD)
    dftT = np.zeros((256, 256))
    idftT = np.zeros((256, 256))
    for h in range(H):
        for n in range(16):
            dftT[h * 16:(h + 1) * 16, n * 16 + h] = rows[n]
            idftT[h * 16:(h + 1) * 16, n * 16 + h] = back[n]
    for name, m in (("dftT", dftT), ("idftT", idftT)):
        d[name] = m.reshape(2, 128, 256).transpose(1, 0, 2).astype(np.float32)
    one = np.ones((128, 128), np.float32)
    d["consts"] = np.stack([np.eye(128, dtype=np.float32), np.triu(one), one, np.triu(one, 1) * np.float32(-1e30)])
    return {k: c(v) for k, v in d.items()}


def kernel(**inputs):
    import concourse.bacc as _bacc
    from concourse import mybir as _mybir
    from concourse.bass_utils import run_bass_kernel_spmd as _run

    nc = _bacc.Bacc("TRN2", target_bir_lowering=False, num_devices=1)
    arrays = _layout(inputs)
    aps = {n: nc.dram_tensor(f"in_{n}", v.shape, _mybir.dt.from_np(v.dtype), kind="ExternalInput").ap()
           for n, v in arrays.items()}
    out = nc.dram_tensor("out_x", _OUT[0], _mybir.dt.float32, kind="ExternalOutput").ap()
    two_layer_kernel(nc, aps, out)
    r = _run(nc, [{f"in_{n}": v for n, v in arrays.items()}], core_ids=[0])
    return r.results[0]["out_x"]
```

```python
from contextlib import ExitStack

import concourse.bass as bass
from concourse import mybir

F32 = mybir.dt.float32
F16 = mybir.dt.float16
BF16 = mybir.dt.bfloat16
U32 = mybir.dt.uint32
ALU = mybir.AluOpType
ACT = mybir.ActivationFunctionType
AX_X = mybir.AxisListType.X

P = 128
HALF = 512
WUP = 64.0
WO1UP = 16.0
FDOWN = 1.0 / 64
LN_EPS = 1e-5
RMS_EPS = 1e-6


def two_layer_kernel(nc, a, out):
    B, S, D = a["x"].shape
    T = S // P
    QL, KL, ROPE = 96, 64, 64
    LAT = QL + KL + ROPE
    NP = a["w_pe"].shape[1]
    H = 2 * NP
    F0 = a["W0T"].shape[1]
    NF0 = F0 // P
    F1 = a["gate_w"].shape[1]
    NF1 = F1 // P
    DC = D // P
    STEPS = 2 * T
    TASKS = 3 * T
    LAST = NP // 2 - 1

    with ExitStack() as ctx:
        def sb(name, shape, dt):
            return ctx.enter_context(nc.sbuf_tensor(name, shape, dt))

        def sem(name):
            return ctx.enter_context(nc.semaphore(name))

        ps = ctx.enter_context(nc.psum_tensor("ps", [P, 8, HALF], F32))

        ident = sb("ident", [P, P], F32)
        identb = sb("identb", [P, P], BF16)
        maskb = sb("maskb", [P, P], BF16)
        tri = sb("tri", [P, P], F32)
        ones = sb("ones", [P, P], F32)
        ct_e = sb("ct_e", [P, S], F32)
        ct_o = sb("ct_o", [P, S], F32)
        st = sb("st", [P, S], F32)
        cos_t = sb("cos_t", [P, T, 32], F32)
        sin_t = sb("sin_t", [P, T, 32], F32)
        gq = sb("gq", [QL, 1], F32)
        ge = sb("ge", [P, 1], F32)
        go = sb("go", [P, 1], F32)
        gkv = sb("gkv", [P, 1], F32)
        bias0 = sb("bias0", [P, NF0], F32)
        bias1 = sb("bias1", [P, D], F32)
        gate_s = sb("gate_s", [P, NF1], F32)
        up_s = sb("up_s", [P, NF1], F32)
        down_s = sb("down_s", [P, D], F32)
        eps = sb("eps", [P, 3], F32)
        wlat_h, wlat_l = (sb(f"wlat_{x}", [P, DC, LAT], F16) for x in "hl")
        wq_h, wq_l = (sb(f"wq_{x}", [QL, NP, 3, P], F16) for x in "hl")
        wb_h, wb_l = (sb(f"wb_{x}", [P, NP, D], F16) for x in "hl")
        w0_h, w0_l = (sb(f"w0_{x}", [P, DC, F0], F16) for x in "hl")
        w1_h, w1_l = (sb(f"w1_{x}", [P, NF0, D], F16) for x in "hl")
        wsp_h, wsp_l = (sb(f"wsp_{x}", [P, DC, 2 * D], F16) for x in "hl")
        wo1_h, wo1_l = (sb(f"wo1_{x}", [P, DC, D], F16) for x in "hl")
        gate_w = sb("gate_w", [P, DC, F1], F16)
        up_w = sb("up_w", [P, DC, F1], F16)
        down_w = sb("down_w", [P, NF1, D], F16)

        xb = sb("xb", [P, T, D], F32)
        xT_h, xT_l = (sb(f"xT_{x}", [P, DC, S], F16) for x in "hl")
        qT_h, qT_l = (sb(f"qT_{x}", [QL, S], F16) for x in "hl")
        kTe_h, kTe_l, kTo_h, kTo_l = (sb(f"kT{x}", [P, S], F16) for x in ("eh", "el", "oh", "ol"))
        kT_h, kT_l = [kTe_h, kTo_h], [kTe_l, kTo_l]
        v_h, v_l = (sb(f"v_{x}", [P, T, KL], F16) for x in "hl")
        negmax = sb("negmax", [P, STEPS], F32)
        rowsum = sb("rowsum", [P, STEPS], F32)
        rinv = sb("rinv", [P, 2, 4], F32)
        bnst = [sb(f"bnst{i}", [P, T, 6], F32) for i in range(2)]
        mv = [sb(f"mv{i}", [P, T, 2], F32) for i in range(2)]
        sd = [sb(f"sd{i}", [P, T], F32) for i in range(2)]
        rstd = [sb(f"rstd{i}", [P, T], F32) for i in range(2)]
        shift = sb("shift", [P, T], F32)
        tick = sb("tick", [P, T], F32)
        ss = sb("ss", [P, 2, T], F32)
        rs = sb("rs", [P, 2, T], F32)
        rr = sb("rr", [P, 2, T], F32)
        ss2 = sb("ss2", [P, T, 32], F32)
        rs2 = sb("rs2", [P, T, 32], F32)
        rr2 = sb("rr2", [P, T, 32], F32)
        e16 = sb("e16", [P, 2, D], F16)
        outb = sb("outb", [P, 2, D], F32)

        reg_o = sb("reg_o", [P, 8192], F32)
        reg_p = sb("reg_p", [P, 4096], F32)
        reg_q = sb("reg_q", [P, 4096], F32)
        reg_a = sb("reg_a", [P, 4096], F32)
        reg_x = sb("reg_x", [P, 2048], F32)
        reg_t = sb("reg_t", [P, 2048], F32)
        s_wo = reg_o[:, 0:4096].rearrange("p (h n) -> p h n", h=H)
        s_w0 = reg_o[:, 4096:6144].rearrange("p (k n) -> p k n", k=DC)
        s_w1 = reg_o[:, 6144:8192].rearrange("p (k n) -> p k n", k=NF0)
        s_uqT = reg_p[:, 0:1536].rearrange("p (h n) -> p h n", h=H)
        s_ukT = reg_p[:, 1536:2560].rearrange("p (h n) -> p h n", h=H)
        s_uvT = reg_p[:, 2560:3584].rearrange("p (h n) -> p h n", h=H)
        s_lat = reg_p[:, 3584:3584 + 448].rearrange("p (k n) -> p k n", k=DC)
        s_wq = reg_q[0:QL, 0:3072].rearrange("p (r j n) -> p r j n", r=NP, j=3)
        s_q1 = reg_q[:, 3072:3584].rearrange("p (k n) -> p k n", k=DC)
        s_kv1 = reg_q[:, 3584:4096].rearrange("p (k n) -> p k n", k=DC)
        s_gate = reg_a[:, 0:1536]
        s_down = reg_p[:, 0:1536]
        xb_flat = xb[:, :, :].rearrange("p t n -> p (t n)")
        s_up = xb_flat[:, 0:1536]
        s_o1 = xb_flat[:, 1536:2048].rearrange("p (k n) -> p k n", k=DC)
        s_ft = reg_t[:, 1024:1536].rearrange("p (k n) -> p k n", k=DC)
        s_gt = reg_t[:, 1536:2048].rearrange("p (k n) -> p k n", k=DC)
        s_mask = outb[:, 0, 0:P]
        xn = reg_x[:, :].rearrange("p (t n) -> p t n", t=T)
        run = reg_q[:, 2048:4096].rearrange("p (t n) -> p t n", t=T)
        lat = reg_a[:, 0:T * LAT].rearrange("p (t n) -> p t n", t=T)
        kcat = reg_a[:, 1792:1792 + T * 192].rearrange("p (t n) -> p t n", t=T)
        qn = reg_a[:, 3328:3328 + T * QL].rearrange("p (t n) -> p t n", t=T)
        ropet = reg_t[:, 0:4 * T * 32].rearrange("p (j t n) -> p j t n", j=4, t=T)
        qt = [reg_a[:, 1024 * j:1024 * j + 1024].rearrange("p (h n) -> p h n", h=2) for j in range(3)]
        QT = reg_q[:, :].bitcast(F16).rearrange("p (r e j n) -> p r e j n", r=2, e=2, j=2)
        dT = reg_q[:, :].bitcast(F16).rearrange("p (f n) -> p f n", f=NF0)
        prob = reg_p[:, :].rearrange("p (j n) -> p j n", j=4)
        pT_h = reg_t[:, 0:1024].bitcast(F16).rearrange("p (j n) -> p j n", j=2)
        pT_l = reg_t[:, 1024:2048].bitcast(F16).rearrange("p (j n) -> p j n", j=2)
        o_sb = reg_o[:, :].rearrange("p (t n) -> p t n", t=T)
        spec = reg_p[:, :].rearrange("p (t n) -> p t n", t=T)
        sq = reg_a[:, 0:1024].rearrange("p (j n) -> p j n", j=2)
        sil = reg_a[:, 1024:2048].rearrange("p (j n) -> p j n", j=2)
        fz = reg_a[:, 2048:3072].rearrange("p (j n) -> p j n", j=2)
        prod = reg_o[:, 6144:6656].rearrange("p (j n) -> p j n", j=2)
        cross = reg_o[:, 7168:7616].rearrange("p (j i n) -> p j i n", j=2, i=2)
        fin = reg_t[:, 1024:2048].rearrange("p (j i n) -> p j i n", j=2, i=2)
        sT_h = reg_o[:, 6656:6912].bitcast(F16).rearrange("p (j k n) -> p j k n", j=2, k=2)
        sT_l = reg_o[:, 6912:7168].bitcast(F16).rearrange("p (j k n) -> p j k n", j=2, k=2)
        fT_h = reg_o[:, 0:3072].bitcast(F16).rearrange("p (f n) -> p f n", f=NF1)
        fT_l = reg_o[:, 3072:6144].bitcast(F16).rearrange("p (f n) -> p f n", f=NF1)

        N = {}

        def per_row(name, n):
            s = sem(name)
            N[id(s)] = n
            return s

        in_small = sem("in_small")
        in_gate = sem("in_gate")
        in_query = sem("in_query")
        in_rot = sem("in_rot")
        in_sum = sem("in_sum")
        in_up = sem("in_up")
        in_down = sem("in_down")
        in_spec = sem("in_spec")
        in_w0 = sem("in_w0")
        in_out = sem("in_out")
        w_const = sem("w_const")
        w_mm = sem("w_mm")
        w_cast = sem("w_cast")
        w_cp = sem("w_cp")
        w_hi = sem("w_hi")
        w_lo = sem("w_lo")
        w_qz = sem("w_qz")
        w_xz = sem("w_xz")
        w_qp = sem("w_qp")
        w_ex = sem("w_ex")
        x_in = sem("x_in")
        xs_in = sem("xs_in")
        xb_in = sem("xb_in")
        row_free = sem("row_free")
        stored = [sem("stored0"), sem("stored1")]
        ln = [{k: per_row(f"ln{i}_{k}", n) for k, n in
               (("stat", T), ("mv", T), ("sd", 2), ("rstd", 2), ("xn", T), ("tr", 4), ("hi", 4), ("lo", 4))}
              for i in range(2)]
        ln0_shift = per_row("ln0_shift", 2)
        lat_mm = per_row("lat_mm", T)
        lat_ev = per_row("lat_ev", T)
        lat_sd = per_row("lat_sd", 1)
        lat_rr = per_row("lat_rr", 1)
        rope_m = per_row("rope_m", 1)
        k_rot = per_row("k_rot", 1)
        kq_n = per_row("kq_n", 1)
        v_hi = per_row("v_hi", 1)
        v_lo = per_row("v_lo", 1)
        kq_tr = per_row("kq_tr", 6)
        kq_hi = per_row("kq_hi", 6)
        kq_lo = per_row("kq_lo", 6)
        q_mm = per_row("q_mm", 6 * NP)
        q_ev = per_row("q_ev", 6 * NP)
        q_add = per_row("q_add", 4 * NP)
        q_hi = per_row("q_hi", 4 * NP)
        q_lo = per_row("q_lo", 4 * NP)
        qk_done = per_row("qk_done", STEPS * NP)
        max_done = per_row("max_done", STEPS * NP)
        exp_done = per_row("exp_done", STEPS * NP)
        pt_ready = per_row("pt_ready", TASKS * NP)
        pt_hi = per_row("pt_hi", TASKS * NP)
        pt_lo = per_row("pt_lo", TASKS * NP)
        pv_done = per_row("pv_done", STEPS * NP)
        rinv_done = per_row("rinv_done", STEPS // 4 * NP)
        o_done = per_row("o_done", STEPS // 4 * NP)
        ot_tr = per_row("ot_tr", 2 * T)
        ot_hi = per_row("ot_hi", 2 * T)
        ot_lo = per_row("ot_lo", 2 * T)
        op_mm = per_row("op_mm", T)
        op_add = per_row("op_add", T)
        ff_mm = per_row("ff_mm", 2 * NF0)
        ff_act = per_row("ff_act", 2 * NF0)
        fe_mm = per_row("fe_mm", T)
        fe_ev = per_row("fe_ev", T)
        fe_add = per_row("fe_add", T)
        sp_mm = per_row("sp_mm", T)
        sp_cp = per_row("sp_cp", T)
        sp_sq = per_row("sp_sq", T)
        sp_ss = per_row("sp_ss", T)
        sp_sd = per_row("sp_sd", 1)
        sp_rr = per_row("sp_rr", 1)
        sp_n = per_row("sp_n", T)
        sp_run = per_row("sp_run", T - 2)
        g_mm = per_row("g_mm", 2 * NF1)
        u_mm = per_row("u_mm", 2 * NF1)
        g_act = per_row("g_act", 2 * NF1)
        fz_done = per_row("fz_done", 2 * NF1)
        f_hi = per_row("f_hi", 2 * NF1)
        f_lo = per_row("f_lo", 2 * NF1)
        cs_mm = per_row("cs_mm", T)
        cs_m = per_row("cs_m", T)
        cs_y = per_row("cs_y", 2 * T)
        yt_tr = per_row("yt_tr", T)
        yt_hi = per_row("yt_hi", T)
        yt_lo = per_row("yt_lo", T)
        l1_mm = per_row("l1_mm", T)
        l1_ev = per_row("l1_ev", T)

        def wait(eng, s, b, n):
            eng.wait_ge(s, b * N[id(s)] + n)

        def bank(i, n=HALF):
            return ps[:, i, 0:n]

        ORDER = [T - 1 - k // 2 if k % 2 == 0 else k // 2 for k in range(T)]

        def step_of(s):
            i = ORDER[s % T]
            return s % STEPS // T, i, 1 + (i >= T // 2)

        def o_slot(i):
            return {0: 0, 1: 1, T - 2: 2, T - 1: 3}.get(i, i - 2)

        def tasks_before(s):
            return 3 * (s // 2) + 2 * (s % 2)

        def first(dp):
            return isinstance(dp, int) and dp == 0

        def last(dp):
            return isinstance(dp, int) and dp == LAST

        Q_AT = {1: 0, 2: 1, 5: 2, 6: 3, 9: 4, 10: 5}
        Q_BANK = (6, 6, 7, 7, 6, 6)
        QH_AT = {4: 0, 8: 1, 12: 2, 14: 3}
        AHEAD = {2: ([("turn", 0), ("turn", 1)], [("turn", 2), ("turn", 3)]),
                 3: ([("latent", 0), ("latent", 1)], [("latent", 2), ("latent", 3)]),
                 4: ([("latent", 4), ("latent", 5)], [("latent", 6), ("latent", 7), ("normal", 0)]),
                 5: ([], [("turn_latent", 0), ("turn_latent", 1)]),
                 6: ([("turn_latent", 2), ("turn_latent", 3)], [("turn_latent", 4), ("turn_latent", 5)]),
                 7: ([("query", 0), ("query", 1)], [("query", 2), ("query", 3), ("low", 0)]),
                 8: ([("low", 1), ("query", 4), ("query", 5)], [("low", 2)]),
                 9: ([], [("low", 3)])}
        TURNS = [(0, 0), (1, 0), (0, 1), (0, 2), (1, 1), (1, 2)]
        WIDE = 8
        GATE_BANK = [(0, 1, 6, 7)[n % 4] if n < WIDE else n % 2 for n in range(2 * NF1)]
        UP_BANK = [2 + n % 4 if n < WIDE else 2 + n % 2 for n in range(2 * NF1)]
        CHUNK = 768
        ROUND = 7

        def round_float8(eng, ops, done, before, w, o, m, c):
            cs = slice(c * CHUNK, (c + 1) * CHUNK)
            w, o = w[:, cs], o[:, :, :].rearrange("p k n -> p (k n)")[:, cs]
            n = before * ROUND
            ops.tensor_scalar(m, m, 2.0 ** -6, 1.5 * 2.0 ** 20, ALU.max, ALU.mult).then_inc(done, 1)
            eng.wait_ge(done, n + 1)
            ops.tensor_tensor(w, w, m, ALU.add).then_inc(done, 1)
            eng.wait_ge(done, n + 2)
            ops.tensor_tensor(w, w, m, ALU.subtract).then_inc(done, 1)
            eng.wait_ge(done, n + 3)
            ops.tensor_tensor(m, w, w, ALU.mult).then_inc(done, 1)
            eng.wait_ge(done, n + 4)
            ops.tensor_scalar(m, m, 448.0 ** 2, 3e38, ALU.is_gt, ALU.mult).then_inc(done, 1)
            eng.wait_ge(done, n + 5)
            ops.tensor_scalar(m, m, 3e38, 0.0, ALU.mult, ALU.mult).then_inc(done, 1)
            eng.wait_ge(done, n + 6)
            ops.tensor_tensor(o, w, m, ALU.add).then_inc(done, 1)
            eng.wait_ge(done, n + 7)

        block = ctx.enter_context(nc.Block())

        @block.sync
        def _(sp):
            def load(done, *pairs):
                for dst, src in pairs:
                    sp.dma_start(dst, src).then_inc(done, 16)

            def flat_k(w, k):
                return w.rearrange("p (k n) -> p k n", k=k)

            def by_rows(w):
                return w.rearrange("(k p) n -> p k n", p=P)

            load(in_gate, (flat_k(s_gate, DC), by_rows(a["gate_w"])))
            load(in_small, (ident[:, :], a["consts"][0]), (s_mask, a["consts"][3]), (s_lat, a["w_lat"]),
                 (gq[:, :], a["g_q"]), (gkv[0:KL, :], a["g_kv"]), (gkv[KL:P, :], a["g_kv"]))
            sp.wait_ge(w_const, 1)
            load(in_small, (ge[0:KL, :], a["g_kv"]), (go[KL:P, :], a["g_kv"]))
            load(x_in, (xn, a["x"][0].rearrange("(t p) n -> p t n", p=P)))
            load(in_query, (s_uqT, a["w_uqT"]), (s_ukT, a["w_ukT"]),
                 (s_wq[:, :, 0, 64:128], a["w_pe"][:, :, 0, :]), (s_wq[:, :, 1, 0:64], a["w_pe"][:, :, 1, :]),
                 (s_wq[:, :, 2, 0:128], a["w_pe"][:, :, 2:4, :].rearrange("p r j n -> p r (j n)")))
            load(in_up, (flat_k(s_up, DC), by_rows(a["up_w"])))
            load(in_rot, (cos_t[:, :, :], a["cs"][0]), (sin_t[:, :, :], a["cs"][1]),
                 (st[:, :], a["rot"][2]), (ct_e[:, :], a["rot"][0]), (ct_o[:, :], a["rot"][1]))
            sp.wait_ge(w_mm, 1)
            load(in_down, (flat_k(s_down, NF1), by_rows(a["down_w"])))
            load(in_sum, (up_s[:, :], a["up_s"]), (down_s[:, :], a["down_s"]), (gate_s[:, :], a["gate_s"]),
                 (bias0[:, :], a["bias0"]), (bias1[:, :], a["bias1"]), (tri[:, :], a["consts"][1]), (ones[:, :], a["consts"][2]))
            load(in_spec, (s_q1, by_rows(a["W_q"])), (s_kv1, by_rows(a["W_kv"])), (s_ft, a["dftT"]),
                 (s_gt, a["idftT"]), (s_o1, by_rows(a["W_o1T"])))
            load(in_w0, (s_w0, by_rows(a["W0T"])), (s_w1, by_rows(a["W1T"])))
            load(in_out, (s_uvT, a["w_uvT"]), (s_wo, a["w_o"]))
            sp.wait_ge(w_mm, 3)
            sp.wait_ge(w_qp, 3 * ROUND)
            load(xb_in, (xb[:, :, :], a["x"][0].rearrange("(t p) n -> p t n", p=P)))

            def store(b):
                for t in range(T):
                    sp.wait_ge(row_free, b * T + t + 2)
                    sp.dma_start(out[b, t * P:(t + 1) * P, :], outb[:, t % 2, :]).then_inc(stored[t % 2], 16)
                for s in stored:
                    sp.wait_ge(s, b * (16 * T // 2) + 16 * T // 2)

            with sp.Fori(0, B - 1) as b:
                wait(sp, ln[0]["tr"], b, 4)
                load(xs_in, (xn, a["x"][b + 1].rearrange("(t p) n -> p t n", p=P)))
                wait(sp, ln[1]["tr"], b, 4)
                load(x_in, (xn, a["x"][b + 1].rearrange("(t p) n -> p t n", p=P)))
                store(b)
                load(xb_in, (xb[:, :, :], a["x"][b + 1].rearrange("(t p) n -> p t n", p=P)))
            store(B - 1)

        @block.tensor
        def _(pe):
            def product3(o, l_h, l_l, r_h, r_l, start=True, stop=True):
                nc.tensor.matmul(o, l_h, r_h, start=start, stop=False)
                nc.tensor.matmul(o, l_h, r_l, start=False, stop=False)
                return nc.tensor.matmul(o, l_l, r_h, start=False, stop=stop)

            def fold_queries():
                pe.wait_ge(in_query, 16 * 5)
                for h in range(H):
                    mm = nc.tensor.matmul(ps[0:QL, h // 8, h % 8 * 64:h % 8 * 64 + 64], s_uqT[:, h, :], s_ukT[:, h, :],
                                          start=True, stop=True)
                mm.then_inc(w_mm, 1)

            def fold_spectra():
                pe.wait_ge(in_spec, 16 * 5)
                for k in range(DC):
                    for j, w in enumerate((s_q1, s_kv1)):
                        for c in range(DC):
                            mm = nc.tensor.matmul(ps[:, 4 + k, j * D:(j + 1) * D], w[:, c, k * P:(k + 1) * P], s_ft[:, c, :],
                                                  start=(c == 0), stop=(c == DC - 1))
                mm.then_inc(w_mm, 1)
                for k in range(DC):
                    for c in range(DC):
                        mm = nc.tensor.matmul(ps[:, 6, k * D:(k + 1) * D], s_gt[:, c, k * P:(k + 1) * P], s_o1[:, c, :],
                                              start=(c == 0), stop=(c == DC - 1))
                mm.then_inc(w_mm, 1)

            def fold_outputs(g, where):
                for r in range(2):
                    for e in range(2):
                        h = 4 * g + 2 * r + e
                        mm = nc.tensor.matmul(ps[64 * e:64 * e + 64, where, r * D:(r + 1) * D], s_uvT[:, h, :],
                                              s_wo[:, h, :], start=True, stop=True)
                mm.then_inc(w_mm, 1)

            def turn(b, L, g):
                wait(pe, L["xn"], b, 2 * g + 2)
                if g >= 2:
                    wait(pe, L["lo"], b, g - 1)
                for k in range(DC):
                    for j in range(2):
                        tr = nc.tensor.transpose(ps[:, 2 + g % 2, 256 * k + P * j:256 * k + P * j + P],
                                                 xn[:, 2 * g + j, k * P:(k + 1) * P], ident[:, :])
                tr.then_inc(L["tr"], 1)

            def latent(b, t):
                wait(pe, ln[0]["lo"], b, 4 if t < 2 else t // 2 + 1)
                if t >= 2:
                    wait(pe, lat_ev, b, t - 1)
                for k in range(DC):
                    tt = slice(t * P, (t + 1) * P)
                    mm = product3(bank(2 + t % 2, LAT), xT_h[:, k, tt], xT_l[:, k, tt], wlat_h[:, k, :],
                                  wlat_l[:, k, :], start=(k == 0), stop=(k == DC - 1))
                mm.then_inc(lat_mm, 1)

            def turn_latent(b, n):
                half, what = TURNS[n]
                if n == 0:
                    wait(pe, kq_n, b, 1)
                if n == 2:
                    wait(pe, k_rot, b, 1)
                if n >= 2:
                    wait(pe, kq_lo, b, n - 1)
                src, lo, w = ((qn, 0, QL), (kcat, 0, P), (kcat, 64, P))[what]
                for i in range(4):
                    tr = nc.tensor.transpose(ps[0:w, 2 + n % 2, P * i:P * i + P],
                                             src[:, 4 * half + i, lo:lo + w], ident[:, :])
                tr.then_inc(kq_tr, 1)

            def query(b, pair, j, where):
                half, r = 1 - j // 3, (2, 0, 1)[j % 3]
                hs = slice(HALF * half, HALF * half + HALF)
                product3(bank(where), wq_h[:, pair, r, :], wq_l[:, pair, r, :], qT_h[:, hs], qT_l[:, hs]).then_inc(q_mm, 1)

            def scores(b, dp, s):
                head, i, banks = step_of(s)
                r = s // STEPS
                if s % STEPS in (0, 1, T):
                    wait(pe, q_lo, b, 8 * dp + 4 * r + {0: 1, 1: 3, T: 4}[s % STEPS])
                if not (first(dp) and s < 2):
                    wait(pe, exp_done, b, dp * 2 * STEPS + s - 1)
                l_h, l_l = (QT[:, r, head, x, i * P:(i + 1) * P] for x in range(2))
                for c in range(banks):
                    w = min((i + 1) * P - c * HALF, HALF)
                    o = ps[:, 2 * (s % 2) + c, 0:w]
                    k_h, k_l = kT_h[head][:, c * HALF:c * HALF + w], kT_l[head][:, c * HALF:c * HALF + w]
                    mm = product3(o, l_h, l_l, k_h, k_l, stop=(c < banks - 1))
                    if c == banks - 1:
                        mm = nc.tensor.matmul(o[:, w - P:w], identb[:, :], maskb[:, :], start=False, stop=True)
                mm.then_inc(qk_done, 1)

            def turn_probs(b, dp, s):
                head, i, banks = step_of(s)
                wait(pe, exp_done, b, dp * 2 * STEPS + s + 1)
                for c in range(banks):
                    n = tasks_before(s) + c
                    if not (first(dp) and n < 3):
                        wait(pe, pt_lo, b, dp * 2 * TASKS + n - 2)
                    for j in range(4 * c, min(4 * c + 4, i + 1)):
                        tr = nc.tensor.transpose(ps[:, 3 + n % 3, (j - 4 * c) * P:(j - 4 * c + 1) * P],
                                                 prob[:, s % 4, j * P:(j + 1) * P], ident[:, :])
                    tr.then_inc(pt_ready, 1)

            def values(b, dp, s):
                head, i, banks = step_of(s)
                wait(pe, pt_lo, b, dp * 2 * TASKS + tasks_before(s + 1))
                g, r = s // 4, s // STEPS
                if s % 4 == 0:
                    if not (first(dp) and g < 2):
                        wait(pe, o_done, b, dp * 2 * (STEPS // 4) + g - 1)
                    if g % 4 < 3 and not (last(dp) and r == 1):
                        wait(pe, q_ev, b, dp * 12 + 6 * r + 6 + 2 * (g % 4 + 1))
                slot = o_slot(i)
                o = ps[:, 6 + g % 2, slot * KL:(slot + 1) * KL]
                for j in range(i + 1):
                    mm = product3(o, pT_h[:, s % 2, j * P:(j + 1) * P], pT_l[:, s % 2, j * P:(j + 1) * P],
                                  v_h[:, j, :], v_l[:, j, :], start=(j == 0), stop=(j == i))
                mm.then_inc(pv_done, 1)

            def double_pair(b, dp):
                for s in range(2 * STEPS):
                    scores(b, dp, s)
                    if not (first(dp) and s < 3):
                        turn_probs(b, dp, s - 3)
                    j = Q_AT.get(s % STEPS)
                    r = s // STEPS
                    if j is not None and not (last(dp) and r == 1):
                        if j % 2:
                            wait(pe, q_ev, b, dp * 12 + 6 * r + 6 + j)
                        elif j == 4 or not (first(dp) and r == 0):
                            wait(pe, o_done, b, dp * 2 * (STEPS // 4) + 4 * r + j // 2 - 1)
                        query(b, 2 * dp + r + 1, j, Q_BANK[j])
                    if not (first(dp) and s < 4):
                        values(b, dp, s - 4)

            def turn_out(b, t):
                for c in range(2):
                    if t >= 2:
                        wait(pe, ot_lo, b, 2 * (t - 2) + c + 1)
                    for j in range(4):
                        tr = nc.tensor.transpose(ps[:, 2 * (t % 2) + c, j * P:(j + 1) * P],
                                                 o_sb[:, t, (4 * c + j) * P:(4 * c + j + 1) * P], ident[:, :])
                    tr.then_inc(ot_tr, 1)

            def project(b, t):
                wait(pe, ot_lo, b, 2 * t + 2)
                if t >= 2:
                    wait(pe, op_add, b, t - 1)
                for r in range(NP):
                    rs_ = slice(r * P, (r + 1) * P)
                    mm = product3(bank(6 + t % 2, D), pT_h[:, t % 2, rs_], pT_l[:, t % 2, rs_], wb_h[:, r, :],
                                  wb_l[:, r, :], start=(r == 0), stop=(r == NP - 1))
                mm.then_inc(op_mm, 1)

            def hidden(b, n):
                half, f = n // NF0, n % NF0
                if n >= 2:
                    wait(pe, ff_act, b, n - 1)
                for k in range(DC):
                    for w in (w0_h, w0_l):
                        mm = nc.tensor.matmul(bank(4 + n % 2), w[:, k, f * P:(f + 1) * P],
                                              xT_h[:, k, half * HALF:(half + 1) * HALF],
                                              start=(k == 0 and w is w0_h), stop=(k == DC - 1 and w is w0_l))
                mm.then_inc(ff_mm, 1)

            def feed_out(b, t):
                wait(pe, ff_act, b, NF0 * (t // 4 + 1))
                if t < 2:
                    wait(pe, ot_lo, b, 2 * T)
                else:
                    wait(pe, fe_ev, b, t - 1)
                for f in range(NF0):
                    for w in (w1_h, w1_l):
                        mm = nc.tensor.matmul(bank(t % 2, D), dT[:, f, t * P:(t + 1) * P], w[:, f, :],
                                              start=(f == 0 and w is w1_h), stop=(f == NF0 - 1 and w is w1_l))
                mm.then_inc(fe_mm, 1)

            def spectra(b, t):
                wait(pe, ln[1]["lo"], b, t // 2 + 1)
                if t >= 2:
                    wait(pe, sp_sq, b, t - 1)
                for k in range(DC):
                    tt = slice(t * P, (t + 1) * P)
                    mm = product3(bank(4 + t % 2), xT_h[:, k, tt], xT_l[:, k, tt], wsp_h[:, k, :], wsp_l[:, k, :],
                                  start=(k == 0), stop=(k == DC - 1))
                mm.then_inc(sp_mm, 1)

            def gate_up(b, n):
                half, f = n // NF1, n % NF1
                before = max((m for m in range(n) if UP_BANK[m] == UP_BANK[n]), default=None)
                if before is not None:
                    wait(pe, g_act, b, before + 1)
                    wait(pe, fz_done, b, before + 1)
                elif n in (2, 3):
                    wait(pe, sp_sq, b, T - 3 + n)
                for w, at, done in ((gate_w, GATE_BANK[n], g_mm), (up_w, UP_BANK[n], u_mm)):
                    for k in range(DC):
                        for x in (xT_h, xT_l):
                            mm = nc.tensor.matmul(bank(at), w[:, k, f * P:(f + 1) * P],
                                                  x[:, k, half * HALF:(half + 1) * HALF],
                                                  start=(k == 0 and x is xT_h), stop=(k == DC - 1 and x is xT_l))
                    mm.then_inc(done, 1)

            def cumulate(b, t):
                wait(pe, sp_n, b, t + 1)
                if t >= 2:
                    wait(pe, sp_run, b, t - 1)
                    wait(pe, cs_m, b, t - 1)
                mm = nc.tensor.matmul(bank(4 + t % 2, D), tri[:, :], spec[:, t, D:2 * D], start=True, stop=(t == 0))
                if t:
                    before = spec[:, 0, D:2 * D] if t == 1 else run[:, t, :]
                    mm = nc.tensor.matmul(bank(4 + t % 2, D), ones[:, :], before, start=False, stop=True)
                mm.then_inc(cs_mm, 1)

            def turn_prod(b, t):
                wait(pe, cs_y, b, 2 * t + 2)
                if t >= 2:
                    wait(pe, yt_lo, b, t - 1)
                for k in range(DC):
                    tr = nc.tensor.transpose(ps[:, 6 + t % 2, k * P:(k + 1) * P], prod[:, t % 2, k * P:(k + 1) * P],
                                             ident[:, :])
                tr.then_inc(yt_tr, 1)

            def outputs(b, t):
                wait(pe, yt_lo, b, t + 1)
                wait(pe, f_lo, b, 2 * NF1)
                if t >= 2:
                    wait(pe, l1_ev, b, t - 1)
                for k in range(DC):
                    product3(bank(t % 2, D), sT_h[:, t % 2, k, :], sT_l[:, t % 2, k, :], wo1_h[:, k, :], wo1_l[:, k, :],
                             start=(k == 0), stop=(k == DC - 1))
                for f in range(NF1):
                    for x in (fT_h, fT_l):
                        mm = nc.tensor.matmul(ps[:, t % 2, D:2 * D], x[:, f, t * P:(t + 1) * P], down_w[:, f, :],
                                              start=(f == 0 and x is fT_h), stop=(f == NF1 - 1 and x is fT_l))
                mm.then_inc(l1_mm, 1)

            def first_query(b, j):
                wait(pe, kq_lo, b, min(j + 5, 6))
                if j >= 2:
                    wait(pe, q_ev, b, j - 1)
                query(b, 0, j, 2 + j % 2)

            def ahead(b, items):
                for kind, n in items:
                    if kind == "turn":
                        turn(b, ln[0], n)
                    elif kind == "latent":
                        latent(b, n)
                    elif kind == "turn_latent":
                        turn_latent(b, n)
                    elif kind == "query":
                        first_query(b, n)

            def row(b, following):
                double_pair(b, 0)
                with pe.Fori(1, LAST) as dp:
                    double_pair(b, dp)
                double_pair(b, LAST)
                for s in range(2 * STEPS, 2 * STEPS + 4):
                    if s < 2 * STEPS + 3:
                        turn_probs(b, LAST, s - 3)
                    values(b, LAST, s - 4)
                wait(pe, o_done, b, NP * STEPS // 4)
                turn_out(b, 0)
                for t in range(T):
                    hidden(b, 2 * t)
                    hidden(b, 2 * t + 1)
                    if t + 1 < T:
                        turn_out(b, t + 1)
                    project(b, t)
                for t in range(T - 2):
                    feed_out(b, t)
                turn(b, ln[1], 0)
                turn(b, ln[1], 1)
                feed_out(b, T - 2)
                feed_out(b, T - 1)
                for t in range(T):
                    spectra(b, t)
                    if t == 2 or t == 3:
                        turn(b, ln[1], t)
                pe.wait_ge(w_qp, 3 * ROUND)
                for n in range(2 * NF1):
                    if n >= 2 * NF1 - 3:
                        if n < 2 * NF1 - 1:
                            wait(pe, fz_done, b, WIDE - 2 * NF1 + 2 + n)
                            cumulate(b, n - (2 * NF1 - 3))
                        else:
                            turn_prod(b, 0)
                    gate_up(b, n)
                for t in range(2, T + 2):
                    if t < T:
                        cumulate(b, t)
                    if t <= T:
                        turn_prod(b, t - 1)
                    if t >= 2:
                        if following:
                            if t == 2:
                                wait(pe, fz_done, b, 2 * NF1)
                            ahead(b + 1, AHEAD[t][0])
                        outputs(b, t - 2)
                        if following:
                            ahead(b + 1, AHEAD[t][1])
                if following:
                    wait(pe, l1_ev, b, T)
                    wait(pe, v_lo, b + 1, 1)
                    wait(pe, q_ev, b + 1, 6)

            pe.wait_ge(in_small, 16 * 8)
            fold_queries()
            for g in range(4):
                turn(0, ln[0], g)
            pe.wait_ge(w_lo, 1)
            for t in range(T):
                latent(0, t)
            fold_spectra()
            pe.wait_ge(in_out, 16 * 2)
            pe.wait_ge(w_cp, 2)
            for g, where in enumerate((7, 0, 1)):
                fold_outputs(g, where)
            for n in range(6):
                turn_latent(0, n)
            pe.wait_ge(w_lo, 3)
            for j in range(6):
                first_query(0, j)
            fold_outputs(3, 4)
            pe.wait_ge(w_lo, 10)
            wait(pe, v_lo, 0, 1)
            wait(pe, q_ev, 0, 6)
            with pe.Fori(0, B - 1) as b:
                row(b, True)
            row(B - 1, False)

        @block.scalar
        def _(act):
            def copy(o, i, **kw):
                return nc.scalar.activation(o, i, ACT.Copy, **kw)

            def fold_queries():
                act.wait_ge(in_query, 16 * 5)
                act.wait_ge(w_mm, 1)
                for e in range(2):
                    src = ps[0:QL, 0:2, :].rearrange("p c (r e n) -> p (c r) e n", e=2, n=64)[:, :, e, :]
                    copy(s_wq[:, :, e, 64 * e:64 * e + 64], src).then_inc(w_cp, 1)
                act.wait_ge(w_cp, 2)
                act.wait_ge(w_const, 3)
                copy(wq_h[:, :, :, :], s_wq, scale=gq[:, 0:1]).then_inc(w_hi, 1)

            def roots(b, L, half):
                wait(act, L["mv"], b, 4 * half + 4)
                hs = slice(4 * half, 4 * half + 4)
                i = int(L is ln[1])
                nc.scalar.activation(sd[i][:, hs], mv[i][:, hs, 1], ACT.Sqrt, bias=eps[:, 0:1]).then_inc(L["sd"], 1)

            def normalise(b, t):
                if t == 0:
                    act.wait_ge(x_in, b * 16 + 16)
                if t % 4 == 0:
                    wait(act, ln0_shift, b, t // 4 + 1)
                nc.scalar.activation(xn[:, t, :], xn[:, t, :], ACT.Identity, bias=shift[:, t:t + 1],
                                     scale=rstd[0][:, t:t + 1]).then_inc(ln[0]["xn"], 1)

            def turned(b, L, g):
                wait(act, L["tr"], b, g + 1)
                copy(xT_h[:, :, 256 * g:256 * g + 256], ps[:, 2 + g % 2, :].rearrange("p (k n) -> p k n", k=DC)).then_inc(L["hi"], 1)

            def latent(b, t):
                wait(act, lat_mm, b, t + 1)
                src = bank(2 + t % 2)
                nc.scalar.activation(qn[:, t, :], src[:, 0:QL], ACT.Square, accum_out=ss[:, 0, t:t + 1])
                nc.scalar.activation(kcat[:, t, 0:KL], src[:, QL:QL + KL], ACT.Square, accum_out=ss[:, 1, t:t + 1])
                copy(lat[:, t, :], src[:, 0:LAT]).then_inc(lat_ev, 1)
                if t == T - 1:
                    wait(act, lat_ev, b, T)
                    nc.scalar.activation(rs[:, 0, :], ss[:, 0, :], ACT.Sqrt, bias=eps[:, 1:2], scale=1.0 / QL)
                    nc.scalar.activation(rs[:, 1, :], ss[:, 1, :], ACT.Sqrt, bias=eps[:, 1:2], scale=1.0 / KL).then_inc(lat_sd, 1)

            def turn_latent(b, n):
                if n == 0:
                    wait(act, kq_n, b, 1)
                    copy(v_h[:, :, :], kcat[:, :, 0:KL]).then_inc(v_hi, 1)
                wait(act, kq_tr, b, n + 1)
                half, what = TURNS[n]
                hs = slice(HALF * half, HALF * half + HALF)
                if what == 0:
                    copy(qT_h[:, hs], ps[0:QL, 2 + n % 2, :]).then_inc(kq_hi, 1)
                elif what == 1:
                    copy(kTe_h[:, hs], bank(2 + n % 2), scale=ge[:, 0:1]).then_inc(kq_hi, 1)
                else:
                    copy(kTo_h[:, hs], bank(2 + n % 2), scale=go[:, 0:1]).then_inc(kq_hi, 1)

            def query_hi(b, before, r, i):
                half, e = 1 - i // 2, i % 2
                wait(act, q_add, b, before + i + 1)
                copy(QT[:, r, e, 0, half * HALF:(half + 1) * HALF], qt[1 + e][:, half, :]).then_inc(q_hi, 1)

            def exponent(b, dp, s):
                head, i, banks = step_of(s)
                wait(act, max_done, b, dp * 2 * STEPS + s + 1)
                if not (first(dp) and s < 4):
                    wait(act, pt_ready, b, dp * 2 * TASKS + tasks_before(s - 3))
                if s % 4 == 0 and not (first(dp) and s < STEPS):
                    wait(act, o_done, b, dp * 2 * (STEPS // 4) + s // 4 - STEPS // 4 + 1)
                w = (i + 1) * P
                sum_slot = s % STEPS // 4 * 4 + o_slot(i)
                nc.scalar.activation(prob[:, s % 4, 0:w], ps[:, 2 * (s % 2):2 * (s % 2) + banks, :].rearrange("p c n -> p (c n)")[:, 0:w],
                                     ACT.Exp, bias=negmax[:, s % STEPS:s % STEPS + 1],
                                     accum_out=rowsum[:, sum_slot:sum_slot + 1]).then_inc(exp_done, 1)

            def probs_hi(b, dp, s):
                head, i, banks = step_of(s)
                if not (first(dp) and s < 2):
                    wait(act, pv_done, b, dp * 2 * STEPS + s - 1)
                for c in range(banks):
                    n = tasks_before(s) + c
                    w = min((i + 1) * P - c * HALF, HALF)
                    wait(act, pt_ready, b, dp * 2 * TASKS + n + 1)
                    copy(pT_h[:, s % 2, c * HALF:c * HALF + w], bank(3 + n % 3, w)).then_inc(pt_hi, 1)

            def double_pair(b, dp):
                for s in range(2 * STEPS):
                    if not (first(dp) and s < 1):
                        exponent(b, dp, s - 1)
                    if not (first(dp) and s < 3):
                        probs_hi(b, dp, s - 3)
                    i, r = QH_AT.get(s % STEPS), s // STEPS
                    if i is not None and not (last(dp) and r == 1):
                        query_hi(b, dp * 8 + 4 * r + 4, 1 - r, i)
            def out_hi(b, t):
                for c in range(2):
                    if t >= 2 and c == 0:
                        wait(act, op_mm, b, t - 1)
                    wait(act, ot_tr, b, 2 * t + c + 1)
                    copy(pT_h[:, t % 2, c * HALF:(c + 1) * HALF], bank(2 * (t % 2) + c)).then_inc(ot_hi, 1)

            def gelu(b, n):
                half, f = n // NF0, n % NF0
                wait(act, ff_mm, b, n + 1)
                nc.scalar.activation(dT[:, f, half * HALF:(half + 1) * HALF], bank(4 + n % 2), ACT.Gelu,
                                     bias=bias0[:, f:f + 1], scale=1 / WUP).then_inc(ff_act, 1)

            def ahead(b, items):
                for kind, n in items:
                    if kind == "turn":
                        turned(b, ln[0], n)
                    elif kind == "latent":
                        latent(b, n)
                    elif kind == "turn_latent":
                        turn_latent(b, n)
                    elif kind == "low":
                        query_hi(b, 0, 0, n)

            def turned_prod(b, t):
                wait(act, yt_tr, b, t)
                if t >= 3:
                    wait(act, l1_mm, b, t - 2)
                copy(sT_h[:, (t - 1) % 2, :, :],
                     ps[:, 6 + (t - 1) % 2, 0:D].rearrange("p (k n) -> p k n", k=DC)).then_inc(yt_hi, 1)

            def row(b, following):
                double_pair(b, 0)
                with act.Fori(1, LAST) as dp:
                    double_pair(b, dp)
                double_pair(b, LAST)
                exponent(b, LAST, 2 * STEPS - 1)
                probs_hi(b, LAST, 2 * STEPS - 3)
                probs_hi(b, LAST, 2 * STEPS - 2)
                probs_hi(b, LAST, 2 * STEPS - 1)
                wait(act, pv_done, b, NP * STEPS)
                out_hi(b, 0)
                for t in range(T):
                    gelu(b, 2 * t)
                    gelu(b, 2 * t + 1)
                    if t + 1 < T:
                        out_hi(b, t + 1)
                roots(b, ln[1], 0)
                if following:
                    for half in range(2):
                        roots(b + 1, ln[0], half)
                turned(b, ln[1], 0)
                turned(b, ln[1], 1)
                for t in range(T):
                    if t == 1:
                        roots(b, ln[1], 1)
                    if t == 3 or t == 4:
                        turned(b, ln[1], t - 1)
                    wait(act, sp_mm, b, t + 1)
                    copy(spec[:, t, :], bank(4 + t % 2)).then_inc(sp_cp, 1)
                    if t >= 2:
                        wait(act, sp_ss, b, t - 1)
                    nc.scalar.activation(sq[:, t % 2, :], bank(4 + t % 2), ACT.Square).then_inc(sp_sq, 1)
                wait(act, sp_ss, b, T)
                nc.scalar.activation(rs2[:, :, :], ss2[:, :, :], ACT.Sqrt).then_inc(sp_sd, 1)
                for n in range(2 * NF1 + 1):
                    if n < 2 * NF1:
                        f = n % NF1
                        wait(act, g_mm, b, n + 1)
                        if n >= 2:
                            wait(act, fz_done, b, n - 1)
                        nc.scalar.activation(sil[:, n % 2, :], bank(GATE_BANK[n]), ACT.Silu, scale=gate_s[:, f:f + 1]).then_inc(g_act, 1)
                    if n:
                        half, f = (n - 1) // NF1, (n - 1) % NF1
                        wait(act, fz_done, b, n)
                        copy(fT_h[:, f, half * HALF:(half + 1) * HALF], fz[:, (n - 1) % 2, :]).then_inc(f_hi, 1)
                    if following and n >= 2 * NF1 + 1 - T:
                        normalise(b + 1, n - (2 * NF1 + 1 - T))
                turned_prod(b, 1)
                for t in range(2, T + 2):
                    if t <= T:
                        turned_prod(b, t)
                    if following:
                        ahead(b + 1, AHEAD[t][0] + AHEAD[t][1])

            act.wait_ge(in_small, 16 * 8)
            copy(wlat_h[:, :, :], s_lat, scale=WUP).then_inc(w_hi, 1)
            for half in range(2):
                roots(0, ln[0], half)
            for t in range(T):
                normalise(0, t)
            for g in range(4):
                turned(0, ln[0], g)
            fold_queries()
            act.wait_ge(w_qz, 2 * ROUND)
            for t in range(T):
                latent(0, t)
            act.wait_ge(w_mm, 2)
            copy(wsp_h[:, :, :], ps[:, 4:6, :]).then_inc(w_hi, 1)
            act.wait_ge(w_mm, 3)
            copy(wo1_h[:, :, :], ps[:, 6, :].rearrange("p (k n) -> p k n", k=DC), scale=WO1UP).then_inc(w_hi, 1)
            act.wait_ge(in_w0, 16 * 2)
            copy(w0_h[:, :, :], s_w0, scale=WUP).then_inc(w_hi, 1)
            copy(w1_h[:, :, :], s_w1, scale=WUP).then_inc(w_hi, 1)
            for n in range(3):
                turn_latent(0, n)
            act.wait_ge(w_mm, 6)
            copy(wb_h[:, 0:2, :], ps[:, 7, :].rearrange("p (r n) -> p r n", r=2), scale=gkv[:, 0:1]).then_inc(w_hi, 1)
            copy(wb_h[:, 2:6, :], ps[:, 0:2, :].rearrange("p g (r n) -> p (g r) n", r=2), scale=gkv[:, 0:1]).then_inc(w_hi, 1)
            for n in range(3, 6):
                turn_latent(0, n)
            for i in range(4):
                query_hi(0, 0, 0, i)
            act.wait_ge(w_mm, 7)
            copy(wb_h[:, 6:8, :], ps[:, 4, :].rearrange("p (r n) -> p r n", r=2), scale=gkv[:, 0:1]).then_inc(w_hi, 1)
            with act.Fori(0, B - 1) as b:
                row(b, True)
            row(B - 1, False)

        @block.vector
        def _(dve):
            tt, ts, stt = nc.vector.tensor_tensor, nc.vector.tensor_scalar, nc.vector.scalar_tensor_tensor

            nc.vector.memset(ge[:, :], 1.0)
            nc.vector.memset(go[:, :], 1.0).then_inc(w_const, 1)
            nc.vector.memset(eps[:, 0:1], LN_EPS)
            nc.vector.memset(eps[:, 1:2], RMS_EPS * WUP * WUP)
            dve.wait_ge(in_small, 16 * 8)
            ts(gq[:, :], gq[:, :], WUP, None, ALU.mult).then_inc(w_const, 1)
            ts(gkv[:, :], gkv[:, :], WUP, None, ALU.mult).then_inc(w_const, 1)
            nc.vector.tensor_copy(identb[:, :], ident[:, :]).then_inc(w_cast, 1)
            nc.vector.tensor_copy(maskb[:, :], s_mask).then_inc(w_cast, 1)

            def split_weights(before, *parts):
                for n, (o, src, scale, h) in enumerate(parts):
                    dve.wait_ge(w_hi, before + n + 1)
                    stt(out=o, in0=src, scalar=scale, in1=h, op0=ALU.mult, op1=ALU.subtract).then_inc(w_lo, 1)

            def stats(b, L, t):
                i, src = (0, xn) if L is ln[0] else (1, xb)
                nc.vector.bn_stats(bnst[i][:, t, :], src[:, t, :]).then_inc(L["stat"], 1)

            def means(b, L, t):
                wait(dve, L["stat"], b, t + 1)
                nc.vector.memset(tick[:, t:t + 1], 0.0)
                i = int(L is ln[1])
                nc.vector.bn_aggr(mv[i][:, t, :], bnst[i][:, t, :]).then_inc(L["mv"], 1)

            def normalise(b, L, half):
                wait(dve, L["sd"], b, half + 1)
                hs = slice(4 * half, 4 * half + 4)
                i = int(L is ln[1])
                nc.vector.reciprocal(rstd[i][:, hs], sd[i][:, hs]).then_inc(L["rstd"], 1)
                wait(dve, L["rstd"], b, half + 1)
                if L is ln[0]:
                    stt(out=shift[:, hs], in0=mv[0][:, hs, 0], scalar=-1.0, in1=rstd[0][:, hs], op0=ALU.mult,
                        op1=ALU.mult).then_inc(ln0_shift, 1)
                    return
                for t in range(4 * half, 4 * half + 4):
                    ts(xn[:, t, :], xb[:, t, :], mv[1][:, t, 0:1], rstd[1][:, t:t + 1], ALU.subtract, ALU.mult).then_inc(L["xn"], 1)

            def turned_lo(b, L, g):
                wait(dve, L["hi"], b, g + 1)
                gs_ = slice(256 * g, 256 * g + 256)
                tt(xT_l[:, :, gs_], ps[:, 2 + g % 2, :].rearrange("p (k n) -> p k n", k=DC), xT_h[:, :, gs_],
                   ALU.subtract).then_inc(L["lo"], 1)

            def normal_latents(b):
                wait(dve, lat_sd, b, 1)
                nc.vector.reciprocal(rr[:, :, :], rs[:, :, :]).then_inc(lat_rr, 1)
                wait(dve, lat_rr, b, 1)
                tt(qn, lat[:, :, 0:QL], rr[:, 0, :].unsqueeze(2).broadcast_to([P, T, QL]), ALU.mult)
                kv_r = rr[:, 1, :].unsqueeze(2).broadcast_to([P, T, KL])
                tt(kcat[:, :, 0:KL], lat[:, :, QL:QL + KL], kv_r, ALU.mult).then_inc(kq_n, 1)

            def turn_latent(b, j):
                if j == 0:
                    wait(dve, v_hi, b, 1)
                    tt(v_l[:, :, :], kcat[:, :, 0:KL], v_h[:, :, :], ALU.subtract).then_inc(v_lo, 1)
                wait(dve, kq_hi, b, j + 1)
                half, what = TURNS[j]
                hs = slice(HALF * half, HALF * half + HALF)
                if what == 0:
                    tt(qT_l[:, hs], ps[0:QL, 2 + j % 2, :], qT_h[:, hs], ALU.subtract).then_inc(kq_lo, 1)
                else:
                    g, h_, l_ = ((ge, kTe_h, kTe_l), (go, kTo_h, kTo_l))[what - 1]
                    stt(out=l_[:, hs], in0=bank(2 + j % 2), scalar=g[:, 0:1], in1=h_[:, hs], op0=ALU.mult,
                        op1=ALU.subtract).then_inc(kq_lo, 1)

            def query_ev(b, before, j, where, lo_before=None):
                half = 1 - j // 3
                wait(dve, q_mm, b, before + j + 1)
                if j % 3 == 0 and lo_before is not None:
                    wait(dve, q_lo, b, lo_before + 2 * (j // 3) + 2)
                table = (st, ct_e, ct_o)[j % 3]
                tt(qt[j % 3][:, half, :], bank(where), table[:, half * HALF:(half + 1) * HALF], ALU.mult).then_inc(q_ev, 1)

            def first_query(b, j):
                query_ev(b, 0, j, 2 + j % 2)
                half, e = 1 - j // 3, j % 3 - 1
                if e >= 0:
                    wait(dve, q_ev, b, j + 1)
                    rows = slice(64, 128) if e == 0 else slice(0, 64)
                    tt(qt[1 + e][rows, half, :], qt[1 + e][rows, half, :], qt[0][rows, half, :], ALU.add).then_inc(q_add, 1)

            def first_low(b, i):
                half, e = 1 - i // 2, i % 2
                wait(dve, q_hi, b, i + 1)
                hs = slice(half * HALF, (half + 1) * HALF)
                tt(QT[:, 0, e, 1, hs], qt[1 + e][:, half, :], QT[:, 0, e, 0, hs], ALU.subtract).then_inc(q_lo, 1)

            def maxima(b, dp, s):
                head, i, banks = step_of(s)
                wait(dve, qk_done, b, dp * 2 * STEPS + s + 1)
                w = (i + 1) * P
                nc.vector.tensor_reduce(negmax[:, s % STEPS:s % STEPS + 1],
                                        ps[:, 2 * (s % 2):2 * (s % 2) + banks, :].rearrange("p c n -> p (c n)")[:, 0:w],
                                        AX_X, ALU.max, negate=True).then_inc(max_done, 1)

            def probs_lo(b, dp, s):
                head, i, banks = step_of(s)
                for c in range(banks):
                    n = tasks_before(s) + c
                    w = min((i + 1) * P - c * HALF, HALF)
                    wait(dve, pt_hi, b, dp * 2 * TASKS + n + 1)
                    cs = slice(c * HALF, c * HALF + w)
                    tt(pT_l[:, s % 2, cs], bank(3 + n % 3, w), pT_h[:, s % 2, cs], ALU.subtract).then_inc(pt_lo, 1)

            def sums(b, dp, s):
                wait(dve, exp_done, b, dp * 2 * STEPS + s + 1)
                nc.vector.reciprocal(rinv[:, s // 4 % 2, :], rowsum[:, s % STEPS - 3:s % STEPS + 1]).then_inc(rinv_done, 1)

            def out_ev(b, dp, s):
                head, i, banks = step_of(s)
                r = s // STEPS
                wait(dve, rinv_done, b, dp * 2 * (STEPS // 4) + s // 4 + 1)
                wait(dve, pv_done, b, dp * 2 * STEPS + s + 1)
                col = (2 * dp + r) * P + KL * head
                near = slice(1, 3) if 2 <= i < T - 2 else slice(0, 4, 3)
                tt(o_sb.rearrange("p (g v) n -> p g v n", v=2)[:, near, :, bass.ds(col, KL)],
                   bank(6 + s // 4 % 2, 4 * KL).rearrange("p (g v n) -> p g v n", g=2, v=2),
                   rinv[:, s // 4 % 2, :].rearrange("p (g v) -> p g v", v=2).unsqueeze(3).broadcast_to([P, 2, 2, KL]),
                   ALU.mult).then_inc(o_done, 1)

            def double_pair(b, dp):
                for s in range(2 * STEPS):
                    maxima(b, dp, s)
                    if s % 4 == 0 and not (first(dp) and s < 8):
                        out_ev(b, dp, s - 5)
                    if first(dp) and s == 3:
                        dve.wait_ge(row_free, b * T + 1)
                    j, r = Q_AT.get(s % STEPS), s // STEPS
                    if j is not None and not (last(dp) and r == 1):
                        query_ev(b, dp * 12 + 6 * r + 6, j, Q_BANK[j], dp * 8 + 4 * r)
                    if not (first(dp) and s < 3):
                        probs_lo(b, dp, s - 3)
                    if s % 4 == 2 and not (first(dp) and s < 6):
                        sums(b, dp, s - 3)
            def out_lo(b, t):
                for c in range(2):
                    wait(dve, ot_hi, b, 2 * t + c + 1)
                    cs = slice(c * HALF, (c + 1) * HALF)
                    tt(pT_l[:, t % 2, cs], bank(2 * (t % 2) + c), pT_h[:, t % 2, cs], ALU.subtract).then_inc(ot_lo, 1)

            def multiply(b, t):
                wait(dve, cs_mm, b, t + 1)
                if t >= 2:
                    wait(dve, yt_tr, b, t - 1)
                    wait(dve, cs_y, b, 2 * t - 2)
                c_ps = bank(4 + t % 2, D)
                tt(prod[:, t % 2, :], spec[:, t, 0:D], c_ps, ALU.mult)
                tt(cross[:, t % 2, 0, :], spec[:, t, 32:144], c_ps[:, 144:256], ALU.mult)
                tt(cross[:, t % 2, 1, :], spec[:, t, 144:256], c_ps[:, 32:144], ALU.mult).then_inc(cs_m, 1)

            def ahead(b, items):
                for kind, n in items:
                    if kind == "turn":
                        turned_lo(b, ln[0], n)
                    elif kind == "normal":
                        normal_latents(b)
                    elif kind == "turn_latent":
                        turn_latent(b, n)
                    elif kind == "query":
                        first_query(b, n)
                    elif kind == "low":
                        first_low(b, n)

            def row(b, following):
                double_pair(b, 0)
                with dve.Fori(1, LAST) as dp:
                    double_pair(b, dp)
                double_pair(b, LAST)
                out_ev(b, LAST, 2 * STEPS - 5)
                probs_lo(b, LAST, 2 * STEPS - 3)
                probs_lo(b, LAST, 2 * STEPS - 2)
                probs_lo(b, LAST, 2 * STEPS - 1)
                sums(b, LAST, 2 * STEPS - 1)
                out_ev(b, LAST, 2 * STEPS - 1)
                out_lo(b, 0)
                dve.wait_ge(xb_in, b * 16 + 16)
                for t in range(T):
                    if t + 1 < T:
                        out_lo(b, t + 1)
                    wait(dve, op_mm, b, t + 1)
                    stt(out=xb[:, t, :], in0=bank(6 + t % 2, D), scalar=1 / WUP, in1=xb[:, t, :], op0=ALU.mult,
                        op1=ALU.add).then_inc(op_add, 1)
                    if following:
                        if t == 0:
                            dve.wait_ge(xs_in, b * 16 + 16)
                        stats(b + 1, ln[0], t)
                        if t >= 1:
                            means(b + 1, ln[0], t - 1)
                if following:
                    means(b + 1, ln[0], T - 1)
                for t in range(T):
                    wait(dve, fe_mm, b, t + 1)
                    if t >= 2:
                        wait(dve, fe_add, b, t - 1)
                    stt(out=e16[:, t % 2, :], in0=bank(t % 2, D), scalar=1 / WUP, in1=bias1[:, :], op0=ALU.mult,
                        op1=ALU.add).then_inc(fe_ev, 1)
                    wait(dve, fe_ev, b, t + 1)
                    tt(xb[:, t, :], xb[:, t, :], e16[:, t % 2, :], ALU.add).then_inc(fe_add, 1)
                    if t == 4:
                        normalise(b, ln[1], 0)
                    if following and t == 6:
                        for half in range(2):
                            normalise(b + 1, ln[0], half)
                    wait(dve, fe_add, b, t + 1)
                    stats(b, ln[1], t)
                    means(b, ln[1], t)
                    if t == 5:
                        turned_lo(b, ln[1], 0)
                        turned_lo(b, ln[1], 1)
                normalise(b, ln[1], 1)
                for t in range(T):
                    if t == 2 or t == 3:
                        turned_lo(b, ln[1], t)
                    wait(dve, sp_sq, b, t + 1)
                    nc.vector.tensor_reduce(ss2[:, t, :].rearrange("p (j h) -> p j h", j=2),
                                            sq[:, t % 2, :].rearrange("p (j c h) -> p j h c", j=2, h=16),
                                            AX_X, ALU.add).then_inc(sp_ss, 1)
                wait(dve, sp_sd, b, 1)
                nc.vector.reciprocal(rr2[:, :, :], rs2[:, :, :]).then_inc(sp_rr, 1)
                for n in range(2 * NF1 + 1):
                    if 2 * NF1 - 2 <= n < 2 * NF1:
                        multiply(b, n - (2 * NF1 - 2))
                    if n < 2 * NF1:
                        f = n % NF1
                        wait(dve, g_act, b, n + 1)
                        wait(dve, u_mm, b, n + 1)
                        if n >= 2:
                            wait(dve, f_lo, b, n - 1)
                        stt(out=fz[:, n % 2, :], in0=bank(UP_BANK[n]), scalar=up_s[:, f:f + 1], in1=sil[:, n % 2, :],
                            op0=ALU.mult, op1=ALU.mult).then_inc(fz_done, 1)
                    if n:
                        half, f = (n - 1) // NF1, (n - 1) % NF1
                        wait(dve, f_hi, b, n)
                        hs = slice(half * HALF, (half + 1) * HALF)
                        tt(fT_l[:, f, hs], fz[:, (n - 1) % 2, :], fT_h[:, f, hs], ALU.subtract).then_inc(f_lo, 1)
                for t in range(T + 2):
                    if 2 <= t < T:
                        multiply(b, t)
                    if 1 <= t <= T:
                        wait(dve, yt_hi, b, t)
                        tt(sT_l[:, (t - 1) % 2, :, :], ps[:, 6 + (t - 1) % 2, 0:D].rearrange("p (k n) -> p k n", k=DC),
                           sT_h[:, (t - 1) % 2, :, :], ALU.subtract).then_inc(yt_lo, 1)
                    if following and t in AHEAD:
                        ahead(b + 1, AHEAD[t][0])
                    if t >= 2:
                        u = t - 2
                        wait(dve, l1_mm, b, u + 1)
                        if u >= 2:
                            dve.wait_ge(row_free, b * T + u)
                        tt(fin[:, u % 2, 0, :], ps[:, u % 2, D:2 * D], down_s[:, :], ALU.mult)
                        stt(out=fin[:, u % 2, 1, :], in0=bank(u % 2, D), scalar=1 / WO1UP, in1=xb[:, u, :], op0=ALU.mult,
                            op1=ALU.add).then_inc(l1_ev, 1)
                    if following and t in AHEAD:
                        ahead(b + 1, AHEAD[t][1])

            def exponents(done, w, m, c):
                nc.vector.tensor_scalar(m.bitcast(U32), w[:, c * CHUNK:(c + 1) * CHUNK].bitcast(U32), 0x7F800000, None,
                                        ALU.bitwise_and).then_inc(done, 1)

            def round_chunk(before, w, o, m, c):
                exponents(w_xz, w, m, c)
                dve.wait_ge(w_xz, before + 1)
                round_float8(dve, nc.vector, w_qz, before, w, o, m, c)

            dve.wait_ge(in_gate, 16)
            round_chunk(0, s_gate, gate_w, reg_a[:, 1536:1536 + CHUNK], 0)
            dve.wait_ge(x_in, 16)
            for t in range(T):
                stats(0, ln[0], t)
            for t in range(T):
                means(0, ln[0], t)
            for half in range(2):
                normalise(0, ln[0], half)
            round_chunk(1, s_gate, gate_w, reg_a[:, 1536:1536 + CHUNK], 1)
            split_weights(0, (wlat_l[:, :, :], s_lat, WUP, wlat_h[:, :, :]))
            dve.wait_ge(in_down, 16)
            exponents(w_ex, s_down, reg_p[:, 1536:1536 + CHUNK], 0)
            for g in range(4):
                turned_lo(0, ln[0], g)
            split_weights(1, (wq_l[:, :, :, :].rearrange("p r j n -> p (r j n)"), s_wq.rearrange("p r j n -> p (r j n)"),
                              gq[:, 0:1], wq_h[:, :, :, :].rearrange("p r j n -> p (r j n)")))
            round_chunk(2, s_down, down_w, reg_t[:, 0:CHUNK], 1)
            dve.wait_ge(in_up, 16)
            for c in range(2):
                exponents(w_ex, s_up, reg_x[:, c * CHUNK:(c + 1) * CHUNK], c)
            dve.wait_ge(in_rot, 16 * 5)
            normal_latents(0)
            split_weights(2, (wsp_l[:, :, :], ps[:, 4:6, :], 1.0, wsp_h[:, :, :]),
                          (wo1_l[:, :, :], ps[:, 6, :].rearrange("p (k n) -> p k n", k=DC), WO1UP, wo1_h[:, :, :]))
            for n in range(6):
                turn_latent(0, n)
                if n == 3:
                    split_weights(6, (wb_l[:, 0:2, :], ps[:, 7, :].rearrange("p (r n) -> p r n", r=2), gkv[:, 0:1],
                                      wb_h[:, 0:2, :]),
                                  (wb_l[:, 2:6, :], ps[:, 0:2, :].rearrange("p g (r n) -> p (g r) n", r=2), gkv[:, 0:1],
                                   wb_h[:, 2:6, :]))
                if 1 <= n <= 2:
                    split_weights(3 + n, ((w0_l[:, :, :], s_w0, WUP, w0_h[:, :, :]), (w1_l[:, :, :], s_w1, WUP, w1_h[:, :, :]))[n - 1])
            for j in range(6):
                first_query(0, j)
            for i in range(4):
                first_low(0, i)
            dve.wait_ge(in_sum, 16 * 7)
            ts(up_s[:, :], up_s[:, :], FDOWN, None, ALU.mult).then_inc(w_cast, 1)
            ts(down_s[:, :], down_s[:, :], 1 / FDOWN, None, ALU.mult).then_inc(w_cast, 1)
            split_weights(8, (wb_l[:, 6:8, :], ps[:, 4, :].rearrange("p (r n) -> p r n", r=2), gkv[:, 0:1], wb_h[:, 6:8, :]))
            dve.wait_ge(w_lo, 9)
            dve.wait_ge(w_qp, ROUND)
            nc.vector.memset(eps[:, 2:3], 0.0).then_inc(w_lo, 1)
            dve.wait_ge(w_lo, 10)
            nc.vector.memset(tick[:, 0:1], 0.0).then_inc(row_free, 1)
            with dve.Fori(0, B - 1) as b:
                row(b, True)
            row(B - 1, False)

        @block.gpsimd
        def _(pool):
            tt = nc.gpsimd.tensor_tensor

            def pair_queries(b, pair, r, part):
                half = 1 - part
                wait(pool, q_lo, b, pair * 4 + 2 * part)
                for e in range(2):
                    wait(pool, q_ev, b, pair * 6 + 3 * part + 2 + e)
                    if e:
                        wait(pool, q_add, b, pair * 4 + 2 * part + 1)
                    rows = slice(64, 128) if e == 0 else slice(0, 64)
                    tt(qt[1 + e][rows, half, :], qt[1 + e][rows, half, :], qt[0][rows, half, :],
                       ALU.add).then_inc(q_add, 1)
                wait(pool, q_add, b, pair * 4 + 2 * part + 2)
                for e in range(2):
                    wait(pool, q_hi, b, pair * 4 + 2 * part + e + 1)
                    hs = slice(half * HALF, (half + 1) * HALF)
                    tt(QT[:, r, e, 1, hs], qt[1 + e][:, half, :], QT[:, r, e, 0, hs], ALU.subtract).then_inc(q_lo, 1)

            def rotate_keys(b):
                wait(pool, lat_ev, b, T)
                x1, x2 = lat[:, :, QL + KL:QL + KL + 32], lat[:, :, QL + KL + 32:LAT]
                tt(ropet[:, 0, :, :], x1, cos_t[:, :, :], ALU.mult)
                tt(ropet[:, 1, :, :], x2, sin_t[:, :, :], ALU.mult)
                tt(ropet[:, 2, :, :], x1, sin_t[:, :, :], ALU.mult)
                tt(ropet[:, 3, :, :], x2, cos_t[:, :, :], ALU.mult).then_inc(rope_m, 1)
                wait(pool, lat_rr, b, 1)
                tt(kcat[:, :, P:P + KL], lat[:, :, QL:QL + KL], rr[:, 1, :].unsqueeze(2).broadcast_to([P, T, KL]), ALU.mult)
                wait(pool, rope_m, b, 1)
                tt(kcat[:, :, KL:KL + 32], ropet[:, 0, :, :], ropet[:, 1, :, :], ALU.subtract)
                tt(kcat[:, :, KL + 32:P], ropet[:, 2, :, :], ropet[:, 3, :, :], ALU.add).then_inc(k_rot, 1)

            def combine(b, t):
                wait(pool, cs_m, b, t + 1)
                p_ = prod[:, t % 2, :]
                tt(p_[:, 32:144], p_[:, 32:144], p_[:, 144:256], ALU.subtract).then_inc(cs_y, 1)
                wait(pool, cs_y, b, 2 * t + 1)
                tt(p_[:, 144:256], cross[:, t % 2, 0, :], cross[:, t % 2, 1, :], ALU.add).then_inc(cs_y, 1)

            def row(b, following):
                with pool.Fori(0, LAST) as dp:
                    for k in range(2):
                        for half in range(2):
                            pair_queries(b, 2 * dp + 1 + k, 1 - k, half)
                for half in range(2):
                    pair_queries(b, NP - 1, 1, half)
                wait(pool, sp_rr, b, 1)
                for t in range(T):
                    v = spec[:, t, :].rearrange("p (j c h) -> p j c h", j=2, h=16)
                    for j in range(2):
                        ins = tt(v[:, j], v[:, j], rr2[:, t, 16 * j:16 * j + 16].unsqueeze(1).broadcast_to([P, 16, 16]), ALU.mult)
                    ins.then_inc(sp_n, 1)
                    wait(pool, sp_n, b, t + 1)
                    if 1 <= t < T - 1:
                        before = spec[:, 0, D:2 * D] if t == 1 else run[:, t, :]
                        if t >= 2:
                            wait(pool, sp_run, b, t - 1)
                        tt(run[:, t + 1, :], before, spec[:, t, D:2 * D], ALU.add).then_inc(sp_run, 1)
                    if t >= T - 2:
                        combine(b, t - (T - 2))
                for t in range(2, T + 2):
                    if t < T:
                        combine(b, t)
                    if t >= 2:
                        u = t - 2
                        wait(pool, l1_ev, b, u + 1)
                        if u >= 2:
                            pool.wait_ge(stored[u % 2], b * (16 * T // 2) + 16 * (u // 2))
                        tt(outb[:, u % 2, :], fin[:, u % 2, 0, :], fin[:, u % 2, 1, :], ALU.add).then_inc(row_free, 1)
                    if following and t == 4:
                        rotate_keys(b + 1)
                if following:
                    pool.wait_ge(row_free, b * T + T + 1)

            pool.wait_ge(w_ex, 1)
            round_float8(pool, nc.gpsimd, w_qp, 0, s_down, down_w, reg_p[:, 1536:1536 + CHUNK], 0)
            pool.wait_ge(in_rot, 16 * 5)
            pool.wait_ge(w_qz, 3 * ROUND)
            rotate_keys(0)
            for c in range(2):
                pool.wait_ge(w_ex, 2 + c)
                round_float8(pool, nc.gpsimd, w_qp, 1 + c, s_up, up_w, reg_x[:, c * CHUNK:(c + 1) * CHUNK], c)
            pool.wait_ge(w_qp, 3 * ROUND)
            wait(pool, k_rot, 0, 1)
            with pool.Fori(0, B - 1) as b:
                row(b, True)
            row(B - 1, False)


_OUT = ((4, 1024, 256), "float32")


def _layout(i):
    import numpy as np

    H, NOPE, ROPE, VD, S, HD = 16, 128, 64, 128, 1024, 16
    c = np.ascontiguousarray
    w_uq = np.asarray(i["L0_attn_w_uq"]).reshape(96, H, NOPE + ROPE)
    pe = w_uq[:, :, NOPE:]
    swapped = np.concatenate([pe[:, :, 32:], pe[:, :, :32]], axis=2)
    w_pe = np.stack([pe[:, 0::2], pe[:, 1::2], swapped[:, 1::2], swapped[:, 0::2]], axis=2)
    lat = np.concatenate([i["L0_attn_w_dq"], i["L0_attn_w_dkv"], i["L0_attn_w_kr"]], axis=1)
    d = {
        "x": i["L0_attn_x"],
        "w_uqT": w_uq[:, :, :NOPE].transpose(2, 1, 0),
        "w_ukT": np.asarray(i["L0_attn_w_uk"]).reshape(64, H, NOPE).transpose(2, 1, 0),
        "w_uvT": np.asarray(i["L0_attn_w_uv"]).reshape(64, H, VD).transpose(2, 1, 0),
        "w_pe": w_pe,
        "w_o": np.asarray(i["L0_attn_w_o"]).reshape(H, VD, 256).transpose(1, 0, 2),
        "w_lat": lat.reshape(2, 128, 224).transpose(1, 0, 2),
        "g_q": np.asarray(i["L0_attn_g_q"]).reshape(96, 1), "g_kv": np.asarray(i["L0_attn_g_kv"]).reshape(64, 1),
        "W0T": np.asarray(i["L0_ffn_W0"]).T, "W1T": np.asarray(i["L0_ffn_W1"]).T,
        "bias0": np.asarray(i["L0_ffn_bias0"]).reshape(8, 128).T,
        "bias1": np.tile(np.asarray(i["L0_ffn_bias1"]).reshape(1, 256), (128, 1)),
        "W_q": i["L1_attn_W_q"], "W_kv": i["L1_attn_W_kv"], "W_o1T": np.asarray(i["L1_attn_W_o"]).T,
        "gate_w": i["L1_ffn_gate_w"], "up_w": i["L1_ffn_up_w"], "down_w": i["L1_ffn_down_w"],
        "gate_s": np.asarray(i["L1_ffn_gate_scale"]).reshape(6, 128).T,
        "up_s": np.asarray(i["L1_ffn_up_scale"]).reshape(6, 128).T,
        "down_s": np.tile(np.asarray(i["L1_ffn_down_scale"]).reshape(1, 256), (128, 1)),
    }
    inv_freq = (np.float32(1.0) / np.float32(10000.0) ** (np.arange(0, ROPE, 2, dtype=np.float32) / np.float32(ROPE))).astype(np.float32)
    freqs = np.outer(np.arange(S, dtype=np.float32), inv_freq).astype(np.float32).astype(np.float64)
    cos, sin = np.cos(freqs), np.sin(freqs)
    sc = (NOPE + ROPE) ** -0.5 / WUP
    pe_c = np.concatenate([cos, cos], axis=1).T * sc
    pe_s = np.concatenate([-sin, sin], axis=1).T * sc
    flat = np.full_like(pe_c, sc)
    d["rot"] = np.stack([np.concatenate([flat, pe_c]), np.concatenate([pe_c, flat]), np.concatenate([pe_s, pe_s])]).astype(np.float32)
    d["cs"] = np.stack([x.reshape(8, 128, 32).transpose(1, 0, 2) / WUP for x in (cos, sin)]).astype(np.float32)
    j = np.arange(HD)
    rows, back = [], []
    for k in (0, 8):
        rows.append(np.cos(2 * np.pi * j * k / HD) / 4)
        back.append(np.cos(2 * np.pi * j * k / HD) / HD)
    for k in range(1, 8):
        rows.append(np.cos(2 * np.pi * j * k / HD) * 2 ** 0.5 / 4)
        back.append(np.cos(2 * np.pi * j * k / HD) / HD)
    for k in range(1, 8):
        rows.append(-np.sin(2 * np.pi * j * k / HD) * 2 ** 0.5 / 4)
        back.append(-np.sin(2 * np.pi * j * k / HD) / HD)
    dftT = np.zeros((256, 256))
    idftT = np.zeros((256, 256))
    for h in range(H):
        for n in range(16):
            dftT[h * 16:(h + 1) * 16, n * 16 + h] = rows[n]
            idftT[h * 16:(h + 1) * 16, n * 16 + h] = back[n]
    for name, m in (("dftT", dftT), ("idftT", idftT)):
        d[name] = m.reshape(2, 128, 256).transpose(1, 0, 2).astype(np.float32)
    one = np.ones((128, 128), np.float32)
    d["consts"] = np.stack([np.eye(128, dtype=np.float32), np.triu(one), one, np.triu(one, 1) * np.float32(-1e30)])
    return {k: c(v) for k, v in d.items()}


def kernel(**inputs):
    import concourse.bacc as _bacc
    from concourse import mybir as _mybir
    from concourse.bass_utils import run_bass_kernel_spmd as _run

    nc = _bacc.Bacc("TRN2", target_bir_lowering=False, num_devices=1)
    arrays = _layout(inputs)
    aps = {n: nc.dram_tensor(f"in_{n}", v.shape, _mybir.dt.from_np(v.dtype), kind="ExternalInput").ap()
           for n, v in arrays.items()}
    out = nc.dram_tensor("out_x", _OUT[0], _mybir.dt.float32, kind="ExternalOutput").ap()
    two_layer_kernel(nc, aps, out)
    r = _run(nc, [{f"in_{n}": v for n, v in arrays.items()}], core_ids=[0])
    return r.results[0]["out_x"]
```
